# Optimizing a Trainium2 kernel written in Bass

```python
import numpy as np
import jax
import jax.numpy as jnp

def _softmax(x, axis=-1):
    return jax.nn.softmax(x, axis=axis)

def _gelu(x):
    return jax.nn.gelu(x, approximate=True)

def _silu(x):
    return jax.nn.silu(x)

def _sigmoid(x):
    return jax.nn.sigmoid(x)

def _layernorm(x, axis=-1, eps=1e-05):
    m = jnp.mean(x, axis=axis, keepdims=True)
    v = jnp.var(x, axis=axis, keepdims=True)
    return (x - m) / jnp.sqrt(v + eps)

def _scatter_add(tgt, idx, src, axis=0):
    return tgt.at[idx].add(src)

def _segment_sum(src, seg, n):
    return jax.ops.segment_sum(src, seg, n)
kernel_name = 'mk_audio_tower_d2_tok_audfeat768_r4_d9a280'

def setup_inputs(seed: int=0):
    np.random.seed(seed)
    _w = jnp.asarray

    def _rec_inputs():
        import jax
        import jax.numpy as jnp
        _rk = jax.random.key(seed)
        x = -0.000222058 + 0.999998 * jax.random.normal(jax.random.fold_in(_rk, 1), (16, 256, 192), jnp.float32)
        return x
    x = _rec_inputs()

    def _L0_tok_setup():
        import jax, jax.numpy as jnp
        import numpy as np
        B, S, D, K = (8, 1024, 192, 7)
        EPS = 1e-05
        key = jax.random.key(seed)
        k0, k1, k2, k3, k4 = jax.random.split(key, 5)
        return {'x': jax.random.normal(k0, (B, S, D), jnp.float32), 'w_dw': jax.random.normal(k1, (D, 1, K), jnp.float32) * 0.2, 'b_dw': jax.random.normal(k2, (D,), jnp.float32) * 0.02, 'w_pw': jax.random.normal(k3, (D, D, 1), jnp.float32) * 0.03, 'b_pw': jax.random.normal(k4, (D,), jnp.float32) * 0.02, 'gamma': jnp.ones((D,), jnp.float32), 'beta': jnp.zeros((D,), jnp.float32)}
    _L0_tok_all = _L0_tok_setup()
    _L0_tok_in = {k: v for k, v in _L0_tok_all.items() if k in ('w_dw', 'b_dw', 'w_pw', 'b_pw', 'gamma', 'beta')}
    del _L0_tok_all

    def _L0_attn_setup():
        import jax, jax.numpy as jnp
        import numpy as np
        key = jax.random.key(seed)
        ks = jax.random.split(key, 4)
        B, S, D = (8, 512, 192)
        lim = (6.0 / (D + D)) ** 0.5
        Z = jax.random.normal(ks[0], (B, S, D), dtype=jnp.float32)
        Wq = jax.random.uniform(ks[1], (D, D), dtype=jnp.float32, minval=-lim, maxval=lim)
        Wk = jax.random.uniform(ks[2], (D, D), dtype=jnp.float32, minval=-lim, maxval=lim)
        Wv = jax.random.uniform(ks[3], (D, D), dtype=jnp.float32, minval=-lim, maxval=lim)
        bq = jnp.zeros((D,), dtype=jnp.float32)
        bk = jnp.zeros((D,), dtype=jnp.float32)
        bv = jnp.zeros((D,), dtype=jnp.float32)
        return {'Z': Z, 'Wq': Wq, 'bq': bq, 'Wk': Wk, 'bk': bk, 'Wv': Wv, 'bv': bv}
    _L0_attn_all = _L0_attn_setup()
    _L0_attn_in = {k: v for k, v in _L0_attn_all.items() if k in ('Wq', 'bq', 'Wk', 'bk', 'Wv', 'bv')}
    del _L0_attn_all

    def _L0_ffn_setup():
        import jax, jax.numpy as jnp
        import numpy as np
        E = 192
        H = 12
        D = E // H
        HID = 768
        NEXP = 4
        TOPK = 2
        EPS = 1e-05

        def _ln(x, g, b):
            m = jnp.mean(x, axis=-1, keepdims=True)
            v = jnp.mean(jnp.square(x - m), axis=-1, keepdims=True)
            return (x - m) * jax.lax.rsqrt(v + EPS) * g + b
        key = jax.random.key(seed)
        ks = jax.random.split(key, 10)
        s = 0.02
        return {'x': jax.random.normal(ks[0], (8, 256, E), jnp.float32), 'ln1_g': jnp.ones((E,), jnp.float32), 'ln1_b': jnp.zeros((E,), jnp.float32), 'in_w': jax.random.normal(ks[1], (3 * E, E), jnp.float32) * s, 'in_b': jnp.zeros((3 * E,), jnp.float32), 'out_w': jax.random.normal(ks[2], (E, E), jnp.float32) * s, 'out_b': jnp.zeros((E,), jnp.float32), 'mlp_w1': jax.random.normal(ks[3], (E, HID), jnp.float32) * s, 'mlp_b1': jnp.zeros((HID,), jnp.float32), 'mlp_w2': jax.random.normal(ks[4], (HID, E), jnp.float32) * s, 'mlp_b2': jnp.zeros((E,), jnp.float32), 'ln2_g': jnp.ones((E,), jnp.float32), 'ln2_b': jnp.zeros((E,), jnp.float32), 'gate_w': jax.random.normal(ks[5], (NEXP, E), jnp.float32) * s, 'gate_b': jnp.zeros((NEXP,), jnp.float32), 'exp_w1': jax.random.normal(ks[6], (NEXP, E, HID), jnp.float32) * s, 'exp_b1': jnp.zeros((NEXP, HID), jnp.float32), 'exp_w2': jax.random.normal(ks[7], (NEXP, HID, E), jnp.float32) * s, 'exp_b2': jnp.zeros((NEXP, E), jnp.float32)}
    _L0_ffn_all = _L0_ffn_setup()
    _L0_ffn_in = {k: v for k, v in _L0_ffn_all.items() if k in ('ln1_g', 'ln1_b', 'in_w', 'in_b', 'out_w', 'out_b', 'mlp_w1', 'mlp_b1', 'mlp_w2', 'mlp_b2', 'ln2_g', 'ln2_b', 'gate_w', 'gate_b', 'exp_w1', 'exp_b1', 'exp_w2', 'exp_b2')}
    del _L0_ffn_all

    def _L1_attn_setup():
        import jax, jax.numpy as jnp
        import numpy as np
        B, T, C = (16, 512, 192)

        def _wkv(k, v, w, u):
            Bb, Tt, Cc = k.shape

            def step(carry, kv):
                num, den, mx = carry
                kt, vt = kv
                m_out = jnp.maximum(mx, kt + u)
                e1 = jnp.exp(mx - m_out)
                e2 = jnp.exp(kt + u - m_out)
                out = (e1 * num + e2 * vt) / (e1 * den + e2)
                m_new = jnp.maximum(mx + w, kt)
                e1s = jnp.exp(mx + w - m_new)
                e2s = jnp.exp(kt - m_new)
                return ((e1s * num + e2s * vt, e1s * den + e2s, m_new), out)
            init = (jnp.zeros((Bb, Cc), k.dtype), jnp.zeros((Bb, Cc), k.dtype), jnp.full((Bb, Cc), -1e+38, k.dtype))
            _, outs = jax.lax.scan(step, init, (jnp.swapaxes(k, 0, 1), jnp.swapaxes(v, 0, 1)))
            return jnp.swapaxes(outs, 0, 1)
        key = jax.random.key(seed)
        ks = jax.random.split(key, 10)
        s = 0.02
        return {'x': jax.random.normal(ks[0], (B, T, C), dtype=jnp.float32), 'time_decay': jax.random.normal(ks[1], (C,), dtype=jnp.float32) * 0.5, 'time_first': jax.random.normal(ks[2], (C,), dtype=jnp.float32) * 0.5, 'mix_k': jax.random.uniform(ks[3], (C,), dtype=jnp.float32), 'mix_v': jax.random.uniform(ks[4], (C,), dtype=jnp.float32), 'mix_r': jax.random.uniform(ks[5], (C,), dtype=jnp.float32), 'Wk': jax.random.normal(ks[6], (C, C), dtype=jnp.float32) * s, 'Wv': jax.random.normal(ks[7], (C, C), dtype=jnp.float32) * s, 'Wr': jax.random.normal(ks[8], (C, C), dtype=jnp.float32) * s, 'Wo': jax.random.normal(ks[9], (C, C), dtype=jnp.float32) * s}
    _L1_attn_all = _L1_attn_setup()
    _L1_attn_in = {k: v for k, v in _L1_attn_all.items() if k in ('time_decay', 'time_first', 'mix_k', 'mix_v', 'mix_r', 'Wk', 'Wv', 'Wr', 'Wo')}
    del _L1_attn_all

    def _L1_ffn_setup():
        import jax, jax.numpy as jnp
        import numpy as np
        EPS_NORM = 1e-06
        EPS_Q = 1e-05

        def rmsnorm(x, g):
            return x * jax.lax.rsqrt(jnp.mean(x * x, axis=-1, keepdims=True) + EPS_NORM) * g

        def activation_quant(x):
            scale = 127.0 / jnp.maximum(jnp.max(jnp.abs(x), axis=-1, keepdims=True), EPS_Q)
            return jnp.clip(jnp.round(x * scale), -128, 127) / scale

        def weight_quant(w):
            scale = 1.0 / jnp.maximum(jnp.mean(jnp.abs(w)), EPS_Q)
            return jnp.clip(jnp.round(w * scale), -1, 1) / scale

        def bitlinear(x, w, g):
            x_norm = rmsnorm(x, g)
            x_q = x_norm + jax.lax.stop_gradient(activation_quant(x_norm) - x_norm)
            w_q = w + jax.lax.stop_gradient(weight_quant(w) - w)
            return jnp.einsum('bsd,od->bso', x_q, w_q)
        key = jax.random.key(seed)
        k1, k2, k3 = jax.random.split(key, 3)
        B, S, D, H = (8, 1024, 192, 512)
        x = jax.random.normal(k1, (B, S, D), dtype=jnp.float32)
        w_in = jax.random.normal(k2, (2 * H, D), dtype=jnp.float32) * 0.002
        w_out = jax.random.normal(k3, (D, H), dtype=jnp.float32) * 0.002
        g_in = jnp.ones((D,), dtype=jnp.float32)
        g_out = jnp.ones((H,), dtype=jnp.float32)
        return {'x': x, 'w_in': w_in, 'g_in': g_in, 'w_out': w_out, 'g_out': g_out}
    _L1_ffn_all = _L1_ffn_setup()
    _L1_ffn_in = {k: v for k, v in _L1_ffn_all.items() if k in ('w_in', 'g_in', 'w_out', 'g_out')}
    del _L1_ffn_all
    return {'x': x, 'L0_tok_w_dw': _L0_tok_in['w_dw'], 'L0_tok_b_dw': _L0_tok_in['b_dw'], 'L0_tok_w_pw': _L0_tok_in['w_pw'], 'L0_tok_b_pw': _L0_tok_in['b_pw'], 'L0_tok_gamma': _L0_tok_in['gamma'], 'L0_tok_beta': _L0_tok_in['beta'], 'L0_attn_Wq': _L0_attn_in['Wq'], 'L0_attn_bq': _L0_attn_in['bq'], 'L0_attn_Wk': _L0_attn_in['Wk'], 'L0_attn_bk': _L0_attn_in['bk'], 'L0_attn_Wv': _L0_attn_in['Wv'], 'L0_attn_bv': _L0_attn_in['bv'], 'L0_ffn_ln1_g': _L0_ffn_in['ln1_g'], 'L0_ffn_ln1_b': _L0_ffn_in['ln1_b'], 'L0_ffn_in_w': _L0_ffn_in['in_w'], 'L0_ffn_in_b': _L0_ffn_in['in_b'], 'L0_ffn_out_w': _L0_ffn_in['out_w'], 'L0_ffn_out_b': _L0_ffn_in['out_b'], 'L0_ffn_mlp_w1': _L0_ffn_in['mlp_w1'], 'L0_ffn_mlp_b1': _L0_ffn_in['mlp_b1'], 'L0_ffn_mlp_w2': _L0_ffn_in['mlp_w2'], 'L0_ffn_mlp_b2': _L0_ffn_in['mlp_b2'], 'L0_ffn_ln2_g': _L0_ffn_in['ln2_g'], 'L0_ffn_ln2_b': _L0_ffn_in['ln2_b'], 'L0_ffn_gate_w': _L0_ffn_in['gate_w'], 'L0_ffn_gate_b': _L0_ffn_in['gate_b'], 'L0_ffn_exp_w1': _L0_ffn_in['exp_w1'], 'L0_ffn_exp_b1': _L0_ffn_in['exp_b1'], 'L0_ffn_exp_w2': _L0_ffn_in['exp_w2'], 'L0_ffn_exp_b2': _L0_ffn_in['exp_b2'], 'L1_attn_time_decay': _L1_attn_in['time_decay'], 'L1_attn_time_first': _L1_attn_in['time_first'], 'L1_attn_mix_k': _L1_attn_in['mix_k'], 'L1_attn_mix_v': _L1_attn_in['mix_v'], 'L1_attn_mix_r': _L1_attn_in['mix_r'], 'L1_attn_Wk': _L1_attn_in['Wk'], 'L1_attn_Wv': _L1_attn_in['Wv'], 'L1_attn_Wr': _L1_attn_in['Wr'], 'L1_attn_Wo': _L1_attn_in['Wo'], 'L1_ffn_w_in': _L1_ffn_in['w_in'], 'L1_ffn_g_in': _L1_ffn_in['g_in'], 'L1_ffn_w_out': _L1_ffn_in['w_out'], 'L1_ffn_g_out': _L1_ffn_in['g_out']}

def reference(x, L0_tok_w_dw, L0_tok_b_dw, L0_tok_w_pw, L0_tok_b_pw, L0_tok_gamma, L0_tok_beta, L0_attn_Wq, L0_attn_bq, L0_attn_Wk, L0_attn_bk, L0_attn_Wv, L0_attn_bv, L0_ffn_ln1_g, L0_ffn_ln1_b, L0_ffn_in_w, L0_ffn_in_b, L0_ffn_out_w, L0_ffn_out_b, L0_ffn_mlp_w1, L0_ffn_mlp_b1, L0_ffn_mlp_w2, L0_ffn_mlp_b2, L0_ffn_ln2_g, L0_ffn_ln2_b, L0_ffn_gate_w, L0_ffn_gate_b, L0_ffn_exp_w1, L0_ffn_exp_b1, L0_ffn_exp_w2, L0_ffn_exp_b2, L1_attn_time_decay, L1_attn_time_first, L1_attn_mix_k, L1_attn_mix_v, L1_attn_mix_r, L1_attn_Wk, L1_attn_Wv, L1_attn_Wr, L1_attn_Wo, L1_ffn_w_in, L1_ffn_g_in, L1_ffn_w_out, L1_ffn_g_out):
    import jax
    import jax.numpy as jnp

    def _L0_tok_ref(x, w_dw, b_dw, w_pw, b_pw, gamma, beta):
        import jax, jax.numpy as jnp
        import numpy as np
        B, S, D, K = (8, 1024, 192, 7)
        EPS = 1e-05
        d = w_dw.shape[0]
        h = jnp.transpose(x, (0, 2, 1))
        h = jax.lax.conv_general_dilated(h, w_dw, window_strides=(1,), padding='SAME', dimension_numbers=('NCH', 'OIH', 'NCH'), feature_group_count=d) + b_dw[None, :, None]
        h = jnp.einsum('od,bds->bos', w_pw[:, :, 0], h) + b_pw[None, :, None]
        h = jax.nn.relu(h)
        h = jax.lax.reduce_window(h, -jnp.inf, jax.lax.max, (1, 1, 2), (1, 1, 2), 'VALID')
        h = jnp.transpose(h, (0, 2, 1))
        y = jnp.real(jnp.fft.fft2(h))
        mu = jnp.mean(y, axis=-1, keepdims=True)
        var = jnp.var(y, axis=-1, keepdims=True)
        return (y - mu) * jax.lax.rsqrt(var + EPS) * gamma + beta

    def _L0_attn_ref(Z, Wq, bq, Wk, bk, Wv, bv):
        import jax, jax.numpy as jnp
        import numpy as np
        D = Z.shape[-1]
        scale = 1.0 / D ** 0.5
        Q = jnp.einsum('bsd,ed->bse', Z, Wq) + bq
        K = jnp.einsum('bsd,ed->bse', Z, Wk) + bk
        V = jnp.einsum('bsd,ed->bse', Z, Wv) + bv
        scores = jnp.einsum('bqd,bkd->bqk', Q, K) * scale
        attn = jax.nn.softmax(scores, axis=-1)
        Z_hat = jnp.einsum('bqk,bkd->bqd', attn, V)
        return Z_hat

    def _L0_ffn_ref(x, ln1_g, ln1_b, in_w, in_b, out_w, out_b, mlp_w1, mlp_b1, mlp_w2, mlp_b2, ln2_g, ln2_b, gate_w, gate_b, exp_w1, exp_b1, exp_w2, exp_b2):
        import jax, jax.numpy as jnp
        import numpy as np
        E = 192
        H = 12
        D = E // H
        HID = 768
        NEXP = 4
        TOPK = 2
        EPS = 1e-05

        def _ln(x, g, b):
            m = jnp.mean(x, axis=-1, keepdims=True)
            v = jnp.mean(jnp.square(x - m), axis=-1, keepdims=True)
            return (x - m) * jax.lax.rsqrt(v + EPS) * g + b
        B, N, _ = x.shape
        h = _ln(x, ln1_g, ln1_b)
        qkv = h @ in_w.T + in_b
        q, k, v = jnp.split(qkv, 3, axis=-1)
        q = q.reshape(B, N, H, D)
        k = k.reshape(B, N, H, D)
        v = v.reshape(B, N, H, D)
        scores = jnp.einsum('bqhd,bkhd->bhqk', q, k) / jnp.sqrt(jnp.float32(D))
        attn = jax.nn.softmax(scores, axis=-1)
        ctx = jnp.einsum('bhqk,bkhd->bqhd', attn, v).reshape(B, N, E)
        x = x + ctx @ out_w.T + out_b
        x = x + jax.nn.gelu(x @ mlp_w1 + mlp_b1, approximate=False) @ mlp_w2 + mlp_b2
        xm = _ln(x, ln2_g, ln2_b)
        logits = xm @ gate_w.T + gate_b
        topv, topi = jax.lax.top_k(logits, TOPK)
        gates = jax.nn.softmax(topv, axis=-1)
        onehot = jax.nn.one_hot(topi, NEXP, dtype=x.dtype)
        comb = jnp.einsum('bnk,bnke->bne', gates, onehot)
        moe_out = jnp.zeros_like(x)
        for e in range(NEXP):
            he = jax.nn.gelu(xm @ exp_w1[e] + exp_b1[e], approximate=False)
            oe = he @ exp_w2[e] + exp_b2[e]
            moe_out = moe_out + comb[..., e:e + 1] * oe
        return x + moe_out

    def _L1_attn_ref(x, time_decay, time_first, mix_k, mix_v, mix_r, Wk, Wv, Wr, Wo):
        import jax, jax.numpy as jnp
        import numpy as np
        B, T, C = (16, 512, 192)

        def _wkv(k, v, w, u):
            Bb, Tt, Cc = k.shape

            def step(carry, kv):
                num, den, mx = carry
                kt, vt = kv
                m_out = jnp.maximum(mx, kt + u)
                e1 = jnp.exp(mx - m_out)
                e2 = jnp.exp(kt + u - m_out)
                out = (e1 * num + e2 * vt) / (e1 * den + e2)
                m_new = jnp.maximum(mx + w, kt)
                e1s = jnp.exp(mx + w - m_new)
                e2s = jnp.exp(kt - m_new)
                return ((e1s * num + e2s * vt, e1s * den + e2s, m_new), out)
            init = (jnp.zeros((Bb, Cc), k.dtype), jnp.zeros((Bb, Cc), k.dtype), jnp.full((Bb, Cc), -1e+38, k.dtype))
            _, outs = jax.lax.scan(step, init, (jnp.swapaxes(k, 0, 1), jnp.swapaxes(v, 0, 1)))
            return jnp.swapaxes(outs, 0, 1)
        x_prev = jnp.pad(x, ((0, 0), (1, 0), (0, 0)))[:, :-1]
        k = jnp.einsum('btc,dc->btd', x * mix_k + x_prev * (1.0 - mix_k), Wk)
        v = jnp.einsum('btc,dc->btd', x * mix_v + x_prev * (1.0 - mix_v), Wv)
        r = jax.nn.sigmoid(jnp.einsum('btc,dc->btd', x * mix_r + x_prev * (1.0 - mix_r), Wr))
        w = -jnp.exp(time_decay)
        wkv = _wkv(k, v, w, time_first)
        return jnp.einsum('btc,dc->btd', r * wkv, Wo)

    def _L1_ffn_ref(x, w_in, g_in, w_out, g_out):
        import jax, jax.numpy as jnp
        import numpy as np
        EPS_NORM = 1e-06
        EPS_Q = 1e-05

        def rmsnorm(x, g):
            return x * jax.lax.rsqrt(jnp.mean(x * x, axis=-1, keepdims=True) + EPS_NORM) * g

        def activation_quant(x):
            scale = 127.0 / jnp.maximum(jnp.max(jnp.abs(x), axis=-1, keepdims=True), EPS_Q)
            return jnp.clip(jnp.round(x * scale), -128, 127) / scale

        def weight_quant(w):
            scale = 1.0 / jnp.maximum(jnp.mean(jnp.abs(w)), EPS_Q)
            return jnp.clip(jnp.round(w * scale), -1, 1) / scale

        def bitlinear(x, w, g):
            x_norm = rmsnorm(x, g)
            x_q = x_norm + jax.lax.stop_gradient(activation_quant(x_norm) - x_norm)
            w_q = w + jax.lax.stop_gradient(weight_quant(w) - w)
            return jnp.einsum('bsd,od->bso', x_q, w_q)
        h = bitlinear(x, w_in, g_in)
        up, gate = jnp.split(h, 2, axis=-1)
        y = jax.nn.silu(gate) * up
        return bitlinear(y, w_out, g_out)
    h = _L0_tok_ref(x, L0_tok_w_dw, L0_tok_b_dw, L0_tok_w_pw, L0_tok_b_pw, L0_tok_gamma, L0_tok_beta)
    h = h + _L0_attn_ref(_layernorm(h, axis=-1), L0_attn_Wq, L0_attn_bq, L0_attn_Wk, L0_attn_bk, L0_attn_Wv, L0_attn_bv)
    h = h + _L0_ffn_ref(_layernorm(h, axis=-1), L0_ffn_ln1_g, L0_ffn_ln1_b, L0_ffn_in_w, L0_ffn_in_b, L0_ffn_out_w, L0_ffn_out_b, L0_ffn_mlp_w1, L0_ffn_mlp_b1, L0_ffn_mlp_w2, L0_ffn_mlp_b2, L0_ffn_ln2_g, L0_ffn_ln2_b, L0_ffn_gate_w, L0_ffn_gate_b, L0_ffn_exp_w1, L0_ffn_exp_b1, L0_ffn_exp_w2, L0_ffn_exp_b2)
    h = h + _L1_attn_ref(_layernorm(h, axis=-1), L1_attn_time_decay, L1_attn_time_first, L1_attn_mix_k, L1_attn_mix_v, L1_attn_mix_r, L1_attn_Wk, L1_attn_Wv, L1_attn_Wr, L1_attn_Wo)
    h = h + _L1_ffn_ref(_layernorm(h, axis=-1), L1_ffn_w_in, L1_ffn_g_in, L1_ffn_w_out, L1_ffn_g_out)
    return h

_drawn_inputs = setup_inputs


def setup_inputs(seed=0):
    import zlib

    import numpy as np

    out = dict(_drawn_inputs(seed))
    spreads = {'L0_tok_gamma': (1.0, 0.2),
     'L0_tok_beta': (0.0, 0.1),
     'L0_attn_bq': (0.0, 0.554),
     'L0_attn_bk': (0.0, 2.0),
     'L0_attn_bv': (0.0, 0.1),
     'L0_ffn_ln1_g': (1.0, 0.6),
     'L0_ffn_ln1_b': (0.0, 0.8),
     'L0_ffn_in_b': (0.0, 0.567),
     'L0_ffn_out_b': (0.0, 0.466),
     'L0_ffn_mlp_b1': (0.0, 0.456),
     'L0_ffn_mlp_b2': (0.0, 0.319),
     'L0_ffn_ln2_g': (1.0, 0.6),
     'L0_ffn_ln2_b': (0.0, 0.742),
     'L0_ffn_gate_b': (0.0, 0.361),
     'L0_ffn_exp_b1': (0.0, 0.74),
     'L0_ffn_exp_b2': (0.0, 0.1),
     'L1_ffn_g_in': (1.0, 0.6),
     'L1_ffn_g_out': (1.0, 0.6)}
    factors = {'L0_ffn_in_w': 6.632,
     'L0_ffn_out_w': 3.811,
     'L1_attn_time_decay': 8.0,
     'L1_attn_time_first': 8.0,
     'L1_attn_mix_k': 8.0,
     'L1_attn_mix_v': 8.0,
     'L1_attn_mix_r': 8.0,
     'L1_attn_Wk': 8.0,
     'L1_attn_Wv': 5.518,
     'L1_attn_Wr': 8.0,
     'L1_attn_Wo': 5.523,
     'L1_ffn_w_in': 8.0,
     'L1_ffn_w_out': 8.0}
    for name, (base, spread) in spreads.items():
        noise = np.random.default_rng([zlib.crc32(name.encode()), seed]).standard_normal(out[name].shape)
        drawn = base * np.exp(spread * noise) if base else spread * noise
        out[name] = jnp.asarray(drawn.astype(out[name].dtype))
    for name, factor in factors.items():
        out[name] = (out[name] * factor).astype(out[name].dtype)
    return out
```

```python
from contextlib import ExitStack

import numpy as np
import concourse.bass as bass
from concourse import mybir

ALU = mybir.AluOpType
ACT = mybir.ActivationFunctionType
AX = mybir.AxisListType
F32 = mybir.dt.float32
F32R = mybir.dt.float32r
BF16 = mybir.dt.bfloat16

B, S, C = 16, 256, 192
T = S // 2
C1 = C - 128
TAPS = 7
HEADS, HD = 12, 16
HID, HCH = 768, 6
NEXP = 4
BH = 512
GB = 4
NG = B // GB
EPS = 1e-5
EPS_RMS = 1e-6
EPS_Q = 1e-5
MAGIC = 12582912.0
FAR = -1e38
WEACH = 2 * HID + HCH * C
PIECE = (NEXP + 1) * WEACH // (2 * B)

COLS = ["b_dw", "b_pw", "bq", "bk", "ln1_g", "ln1_b", "ln2_g", "ln2_b", "decay", "first", "mix_k", "mix_v", "mix_r"]
COL = {n: 2 * i for i, n in enumerate(COLS)}
QB = 2 * len(COLS)
KB = QB + 3
TAP = KB + 3
HB = TAP + 2 * TAPS
NCOL = HB + HCH * (NEXP + 1)
ROWS = [("gamma", C), ("beta", C), ("bv", C), ("in_bv", C), ("out_b", C), ("mlp_b2", C), ("exp_b2", NEXP * C),
        ("g_in", C), ("gate_b", NEXP), ("g_out", BH)]
ROW = {}
NROW = 0
for _n, _w in ROWS:
    ROW[_n] = (NROW, NROW + _w)
    NROW += _w


RETIRED = ["b_" + n for n in ("st mv rs_a rstd normed turned zT qk_made qk v_made v scored rowmax max exp p_turned pT "
                              "recip attended added").split()] + \
          ["c_" + n for n in ("st mv rs_a rstd1 rr var2 rs2_a rstd x normed xb turned zT q_made q k_made k v_made v "
                              "scored max sub exp attended recip ctx ctx_turned cT projected added").split()]


PLAIN = ("e_consts", "e_decay", "e_wd", "f_prep", "f_prep2", "f_wsum", "f_wmean")


class Unit:

    def __init__(self, v, lo, slot):
        self.v, self.lo, self.slot = v, lo, slot


def pipelined(eng, n, unroll, ahead, stages):
    lag_max = max(k for _, k in stages)
    first = -(-(lag_max + ahead) // unroll) * unroll
    rounds = max(0, (n - first) // unroll)

    def step(t, lo, j, hi):
        for fn, lag in stages:
            if lo - lag >= 0 and hi - lag < n:
                fn(Unit(t - lag if lag else t, lo - lag, (j - lag) % unroll))

    if rounds < 2:
        for t in range(n + lag_max):
            step(t, t, t, t)
        return
    for t in range(first):
        step(t, t, t, t)
    with eng.Fori(0, rounds) as i:
        for j in range(unroll):
            step(i * unroll + (first + j), first + j, j, n - 1)
    for t in range(first + rounds * unroll, n + lag_max):
        step(t, t, t, t)


def audio_tower(nc, d, out):
    with ExitStack() as ctx:
        scope = [ctx]

        def sb(name, shape, dt=F32):
            return scope[-1].enter_context(nc.sbuf_tensor(name, shape, dt))

        start = {}
        retired = list(RETIRED)

        class Sems(dict):
            def __missing__(self, name):
                if name[:2] in ("e_", "f_") and name not in PLAIN and retired:
                    self[name] = self[retired.pop(0)]
                    start[name] = B
                else:
                    self[name] = ctx.enter_context(nc.semaphore(name))
                return self[name]

        s = Sems()

        def after(eng, name, u, back=0, per=1, k=None, nop=False):
            k = per if k is None else k
            if u.lo - back < 0:
                assert isinstance(u.v, int)
                return
            sem = s[name]
            eng.wait_ge(sem, u.v * per + (k - back * per + start.get(name, 0)))
            if nop:
                eng.nop(nofuse=True)

        PS = ctx.enter_context(nc.psum_tensor("PS", [128, 8, 512], F32))

        H = sb("H", [128, B, C])
        cols = sb("cols", [128, NCOL])
        rows = sb("rows", [128, NROW])
        ident = sb("ident", [128, 128])
        identb = sb("identb", [128, 128], BF16)
        expo = sb("expo", [128, 2])

        def col(name, c, n=128):
            return cols[0:n, COL[name] + c:COL[name] + c + 1]

        def row(name):
            return rows[:, ROW[name][0]:ROW[name][1]]

        mem_w = ExitStack()
        scope.append(mem_w)
        NF = NEXP + 1
        WH = sb("WH", [128, NF * WEACH], F32R)
        WL = sb("WL", [128, NF * WEACH], F32R)

        def w_up(w, f):
            return w[:, f * WEACH:f * WEACH + 2 * HID].rearrange("p (k n) -> p k n", k=2)

        def w_down(w, f):
            return w[:, f * WEACH + 2 * HID:(f + 1) * WEACH].rearrange("p (m n) -> p m n", m=HCH)

        X = sb("X", [128, B, C])

        mem_abc = ExitStack()
        scope.append(mem_abc)
        raw = [sb(f"raw{i}", [128, PIECE]) for i in range(2)]
        mem = ExitStack()
        scope.append(mem)
        x0 = sb("x0", [128, B // 2, 2, S + TAPS - 1])
        x1 = sb("x1", [128, B // 2, S + TAPS - 1])
        wpw = sb("wpw", [128, 2, C])
        fd = sb("fd", [128, 2, 2 * C])
        fs = sb("fs", [128, 2, T])
        cv0 = [sb(f"cv0{i}", [128, 2, S]) for i in range(2)]
        cv1 = [sb(f"cv1{i}", [128, S]) for i in range(2)]
        hp = [sb(f"hp{i}", [128, 2, T]) for i in range(4)]
        hT = [sb(f"hT{i}", [128, 2, T]) for i in range(4)]
        Z = [sb(f"Z{i}", [128, 2 * C]) for i in range(2)]
        yn = [sb(f"yn{i}", [128, C]) for i in range(4)]
        st = [sb(f"stA{i}", [128, 6]) for i in range(4)]
        mv = [sb(f"mvA{i}", [128, 2]) for i in range(4)]
        rs = [sb(f"rsA{i}", [128, 2]) for i in range(4)]
        A = dict(x0=x0, x1=x1, wpw=wpw, fd=fd, fs=fs, cv0=cv0, cv1=cv1, hp=hp, hT=hT, Z=Z, yn=yn, st=st, mv=mv, rs=rs)
        scope.pop().close()

        mem = ExitStack()
        scope.append(mem)
        Bm = dict(wq=sb("wq", [128, 2, C]), wk=sb("wk", [128, 2, C]), wv=sb("wv", [128, 2, C]),
                  **{n: [sb(f"{n}B{i}", sh) for i in range(2)] for n, sh in (
                      ("st", [128, 6]), ("mv", [128, 2]), ("rs", [128, 2]), ("zn", [128, C]), ("zT", [128, 2, T]),
                      ("qT", [128, 2, T]), ("kT", [128, 2, T]), ("v", [128, C]), ("p", [128, T]), ("pT", [128, T]),
                      ("nm", [128, 2]), ("sum", [128, 2]), ("un", [128, C]))})
        scope.pop().close()

        mem = ExitStack()
        scope.append(mem)
        Cm = dict(wq=sb("wqC", [128, 2, 384]), wk=sb("wkC", [128, 2, 384]), wv=sb("wvC", [128, 2, C]),
                  wo=sb("woC", [128, 2, C]), E=sb("E", [128, HEADS, T]), PT=sb("PT", [128, HEADS, T]),
                  **{n: [sb(f"{n}C{i}", sh) for i in range(2)] for n, sh in (
                      ("st", [128, 6]), ("mv", [128, 2]), ("rs", [128, 6]), ("zn", [128, C]), ("zT", [128, 2, T]),
                      ("qT", [128, 3, T]), ("kT", [128, 3, T]), ("v", [128, HEADS, HD + 1]), ("mx", [128, HEADS]),
                      ("rd", [128, HEADS]), ("cx", [128, C]), ("cT", [128, 2, T]))})
        scope.pop().close()
        scope.pop().close()

        mem = ExitStack()
        scope.append(mem)
        wg = sb("wg", [128, 2, NEXP])
        D = dict(
            xs=[sb(f"xs{t}", [128, 256]) for t in range(GB)],
            XF=sb("XF", [128, 2, NG, GB * T]),
            hA=[sb(f"hA{i}", [128, GB * T], F32R) for i in range(2)],
            lA=[sb(f"lA{i}", [128, GB * T], F32R) for i in range(2)],
            sB=[sb(f"sB{i}", [128, GB * T], F32R) for i in range(2)],
            G=[sb(f"G{i}", [128, GB * T]) for i in range(2)],
            Gh=sb("Gh", [128, HCH, GB * T], F32R), Gl=sb("Gl", [128, HCH, GB * T], F32R),
            st=sb("stD", [128, GB, 6]), mv=sb("mvD", [128, GB, 2]), rs=sb("rsD", [128, GB, 2]),
            LG=sb("LG", [128, B, NEXP]), rank=sb("rank", [128, B, NEXP]), cmp=sb("cmp", [128, B, NEXP]),
            top=sb("top", [128, B]), comb=sb("comb", [128, B, NEXP]),
            acc=[sb(f"acc{t}", [128, C]) for t in range(GB)], tmp=[sb(f"tmpD{t}", [128, C]) for t in range(2)])
        scope.pop().close()
        scope.pop().close()

        mem_ef = ExitStack()
        scope.append(mem_ef)
        rawI = sb("rawI", [128, 2, 2 * BH])
        rawO = sb("rawO", [128, BH // 128, C])
        wI = sb("wI", [128, 2, 2 * BH], BF16)
        wO = sb("wO", [128, BH // 128, C], BF16)
        qs = sb("qs", [128, 8])
        ones = sb("ones", [128, 128])
        mem = ExitStack()
        scope.append(mem)
        NB6 = GB + GB // 2
        Em = dict(
            w={n: sb(f"w{n}E", [128, 2, C]) for n in "kvro"},
            om={n: sb(f"om{n}", [128, 2]) for n in "kvr"}, ndec=sb("ndec", [128, 2]),
            WD=sb("WD", [128, NB6, T + 1]),
            zn=[sb(f"znE{t}", [128, 256]) for t in range(GB)],
            st=sb("stE", [128, GB, 6]), mv=sb("mvE", [128, GB, 2]), rs=sb("rsE", [128, GB, 2]),
            zT=sb("zTE", [128, NB6, T + 1]), mt={n: sb(f"mt{n}", [128, NB6, T]) for n in "kvr"},
            mx={n: sb(f"mixed{n}", [128, NB6, T]) for n in "kvr"},
            **{n: [sb(f"{n}E{i}", [128, NB6, T]) for i in range(2)] for n in ("ku", "v", "er")},
            K=[sb(f"KE{i}", [128, NB6, T + 1]) for i in range(2)],
            **{n: sb(f"{n}E", [128, NB6, T + 1]) for n in ("MX", "D1", "E2s", "EV", "NUM", "DEN")},
            **{n: sb(f"{n}E", [128, NB6, T]) for n in ("mo", "a", "b", "c", "dd", "e1", "e2", "t1", "t2", "t3")},
            rw=[sb(f"rw{i}", [128, NB6, T]) for i in range(2)])
        scope.pop().close()
        mem = ExitStack()
        scope.append(mem)
        Fm = dict(**{n: [sb(f"{n}F{i}", sh, dt) for i in range(2)] for n, sh, dt in (
            ("st", [128, 6], F32), ("mv", [128, 2], F32), ("rs", [128, 12], F32), ("xn", [128, C], F32),
            ("xg", [128, C], F32), ("q", [128, C], BF16), ("qT", [128, 2, T], BF16), ("sg", [128, BH], F32),
            ("y", [128, BH], F32), ("yg", [128, BH], F32), ("sq", [128, BH], F32), ("q2", [128, BH], BF16),
            ("q2T", [128, BH // 128, T], BF16))}, o=sb("o", [128, B, C]))
        scope.pop().close()
        scope.pop().close()

        block = ctx.enter_context(nc.Block())
        def shifted(u):
            return Unit(u.v + B, u.lo + B, u.slot)

        def arrived(eng, u):
            eng.wait_ge(s[f"in_w{u.slot}"], u.v // 2 * 16 + 16 if isinstance(u.v, int) else (u.v - u.slot) * 8 + 16)

        def phase_end(eng, name, k):
            eng.drain().then_inc(s["phase_" + name], 1)
            for n in ("pe", "act", "dve", "pool"):
                eng.wait_ge(s["phase_" + n], k)

        @block.sync
        def _(sp):
            def load(dst, name, sem):
                sp.dma_start(dst, d[name]).then_inc(s[sem], 16)
            load(A["x0"][:, 0:2], "x0a", "in_x0")
            load(A["x1"][:, 0:2], "x1a", "in_x0")
            load(cols[:, :], "cols", "in_x0")
            load(A["x0"][:, 2:8], "x0b", "in_x")
            load(A["x1"][:, 2:8], "x1b", "in_x")
            load(A["wpw"][:, :, :], "wpw", "in_A")
            load(A["fd"][:, :, :], "fd", "in_A")
            load(A["fs"][:, :, :], "fs", "in_A")
            load(rows[:, :], "rows", "in_A")
            load(ident[:, :], "ident", "in_A")

            def ended(k):
                for n in ("pe", "act", "dve", "pool"):
                    sp.wait_ge(s["phase_" + n], k)

            ended(1)
            for n in ("wq", "wk", "wv"):
                load(Bm[n][:, :, :], n, "in_B")

            def load_piece(u):
                after(sp, "w_lo", u, back=2)
                sp.dma_start(raw[u.slot][:, :], d["w_ffn"][:, bass.ts(u.v, PIECE)]).then_inc(s[f"in_w{u.slot}"], 16)

            pipelined(sp, B, 2, 2, [(load_piece, 0)])
            ended(2)
            for n in ("wq", "wk", "wv", "wo"):
                load(Cm[n][:, :, :], n + "C", "in_C")
            pipelined(sp, B, 2, 2, [(lambda u: load_piece(shifted(u)), 0)])
            ended(3)
            load(wg[:, :, :], "wg", "in_D")
            ended(4)
            for n in "kvro":
                load(Em["w"][n][:, :, :], f"w{n}E", "in_E")
            load(rawI[:, :, :], "w_in", "in_F")
            load(rawO[:, :, :], "w_out", "in_F")
            for g in range(NG):
                sp.wait_ge(s["o_ready"], GB * (g + 1))
                sp.dma_start(out[GB * g:GB * g + GB].rearrange("b t c -> t b c"),
                             Fm["o"][:, GB * g:GB * g + GB, :]).then_inc(s["stored"], 16)
            sp.wait_ge(s["stored"], 16 * NG)

        def mm(o, l, r, start, stop, **kw):
            return nc.tensor.matmul(o, l, r, start=start, stop=stop, **kw)

        @block.tensor
        def _(pe):
            a = A

            def a_pointwise(u):
                after(pe, "tap_a", u, per=TAPS - 1)
                after(pe, "tap_b", u, per=TAPS - 1)
                for p in range(2):
                    bank = PS[:, 2 * u.slot + p, :]
                    after(pe, "pooled", u, back=2, per=2, k=p + 1)
                    for m, (lo, hi) in enumerate(((0, 128), (128, C))):
                        o = bank[0:hi - lo, m * S:m * S + S]
                        mm(o, a["wpw"][:, 0, lo:hi], a["cv0"][u.slot][:, p, :], True, False)
                        last = mm(o, a["wpw"][64 * p:64 * p + 64, 1, lo:hi],
                                  a["cv1"][u.slot][64 * p:64 * p + 64, :], False, True)
                    last.then_inc(s["pointwise"], 1)

            def a_dft(u):
                for p in range(2):
                    h = a["hT"][2 * u.slot + p]
                    after(pe, "relu", u, per=2, k=p + 1)
                    after(pe, "z_copied", u, back=1, per=2, k=p + 1)
                    mm(PS[:, 4 + p, 0:2 * C], h[:, 0, :], a["fd"][:, 0, :], True, False)
                    mm(PS[:, 4 + p, 0:2 * C], h[0:C1, 1, :], a["fd"][0:C1, 1, :], False, True)\
                        .then_inc(s["dft_c"], 1)
                for p in range(2):
                    after(pe, "z_copied", u, per=2, k=p + 1)
                    after(pe, "y_normed", u, back=1, per=2, k=p + 1)
                    mm(PS[:, 6 + p, 0:C], a["fs"][:, 0, :], a["Z"][p][:, 0:C], True, False)
                    mm(PS[:, 6 + p, 0:C], a["fs"][:, 1, :], a["Z"][p][:, C:2 * C], False, True)\
                        .then_inc(s["dft_t"], 1)

            pe.wait_ge(s["in_A"], 16 * 5)
            pipelined(pe, B // 2, 2, 2, [(a_pointwise, 1), (a_dft, 2)])
            phase_end(pe, "pe", 1)

            m_ = Bm

            def b_turn(u):
                after(pe, "b_normed", u)
                after(pe, "b_zT", u, back=1)
                pe.transpose(PS[:, 0, 0:128], m_["zn"][u.slot][:, 0:128], ident[:, :])
                pe.transpose(PS[0:C1, 0, 128:256], m_["zn"][u.slot][:, 128:C], ident[:, :]).then_inc(s["b_turned"], 1)

            def b_qkv(u):
                z = m_["zT"][u.slot]
                after(pe, "b_zT", u)
                after(pe, "b_qk", u, back=1)
                for j, w in enumerate((m_["wq"], m_["wk"])):
                    for m, (lo, hi) in enumerate(((0, 128), (128, C))):
                        o = PS[0:hi - lo, 1, (2 * j + m) * T:(2 * j + m + 1) * T]
                        mm(o, w[:, 0, lo:hi], z[:, 0, :], True, False)
                        last = mm(o, w[0:C1, 1, lo:hi], z[0:C1, 1, :], False, True)
                last.then_inc(s["b_qk_made"], 1)
                after(pe, "b_v", u, back=1)
                mm(PS[:, 2, 0:C], z[:, 0, :], m_["wv"][:, 0, :], True, False)
                mm(PS[:, 2, 0:C], z[0:C1, 1, :], m_["wv"][0:C1, 1, :], False, True).then_inc(s["b_v_made"], 1)

            def b_scores(u):
                q, k = m_["qT"][u.slot], m_["kT"][u.slot]
                after(pe, "b_qk", u)
                after(pe, "b_exp", u, back=1)
                mm(PS[:, 3, 0:T], q[:, 0, :], k[:, 0, :], True, False)
                mm(PS[:, 3, 0:T], q[0:C1, 1, :], k[0:C1, 1, :], False, True).then_inc(s["b_scored"], 1)

            def b_turn_p(u):
                after(pe, "b_exp", u)
                after(pe, "b_pT", u, back=1)
                pe.transpose(PS[:, 4, 0:T], m_["p"][u.slot][:, :], ident[:, :]).then_inc(s["b_p_turned"], 1)

            def b_values(u):
                after(pe, "b_pT", u)
                after(pe, "b_v", u)
                after(pe, "b_added", u, back=1)
                mm(PS[:, 5, 0:C], m_["pT"][u.slot][:, :], m_["v"][u.slot][:, :], True, True)\
                    .then_inc(s["b_attended"], 1)

            pe.wait_ge(s["in_B"], 48)
            pipelined(pe, B, 2, 2, [(b_scores, 2), (b_qkv, 1), (b_turn_p, 2), (b_turn, 0), (b_values, 2)])
            phase_end(pe, "pe", 2)

            c = Cm

            def c_turn(u):
                after(pe, "c_normed", u)
                after(pe, "c_added", u, back=3)
                pe.transpose(PS[:, 6, 0:128], c["zn"][u.slot][:, 0:128], ident[:, :])
                pe.transpose(PS[0:C1, 6, 128:256], c["zn"][u.slot][:, 128:C], ident[:, :]).then_inc(s["c_turned"], 1)

            def c_scores(u):
                after(pe, "c_q", u)
                after(pe, "c_k", u)
                after(pe, "c_sub", u, back=1)
                for g in range(3):
                    for j in range(4):
                        last = mm(PS[:, j, g * T:(g + 1) * T], c["qT"][u.slot][32 * j:32 * j + HD, g, :],
                                  c["kT"][u.slot][32 * j:32 * j + HD, g, :], True, True)
                last.then_inc(s["c_scored"], 1)

            def c_turn_ctx(u):
                after(pe, "c_ctx", u)
                pe.transpose(PS[:, 7, 0:128], c["cx"][u.slot][:, 0:128], ident[:, :])
                pe.transpose(PS[0:C1, 7, 128:256], c["cx"][u.slot][:, 128:C], ident[:, :])\
                    .then_inc(s["c_ctx_turned"], 1)

            def c_qkv(u):
                z = c["zT"][u.slot]
                after(pe, "c_zT", u)
                for j, (w, bank) in enumerate(((c["wq"], 6), (c["wk"], 7))):
                    if j == 1:
                        after(pe, "c_cT", u, back=2)
                    for g in range(3):
                        o = PS[:, bank, g * T:(g + 1) * T]
                        mm(o, w[:, 0, g * 128:(g + 1) * 128], z[:, 0, :], True, False)
                        last = mm(o, w[0:C1, 1, g * 128:(g + 1) * 128], z[0:C1, 1, :], False, True)
                    last.then_inc(s["c_q_made" if j == 0 else "c_k_made"], 1)
                after(pe, "c_pT", u, back=2, per=3, k=2)
                mm(PS[:, 5, 0:C], z[:, 0, :], c["wv"][:, 0, :], True, False)
                mm(PS[:, 5, 0:C], z[0:C1, 1, :], c["wv"][0:C1, 1, :], False, True).then_inc(s["c_v_made"], 1)

            def c_project(u):
                t = c["cT"][u.slot]
                after(pe, "c_cT", u)
                after(pe, "c_q", Unit(u.v + 2, u.lo + 2, u.slot), back=0) if not isinstance(u.v, int) or u.v + 2 < B else None
                mm(PS[:, 6, 0:C], t[:, 0, :], c["wo"][:, 0, :], True, False)
                mm(PS[:, 6, 0:C], t[0:C1, 1, :], c["wo"][0:C1, 1, :], False, True).then_inc(s["c_projected"], 1)

            def c_values(u):
                nxt = Unit(u.v + 1, u.lo + 1, u.slot)
                more = not isinstance(u.v, int) or u.v + 1 < B
                after(pe, "c_exp", u)
                for r in range(3):
                    if r == 0:
                        after(pe, "c_pT", u, back=1, per=3, k=3)
                    if r == 1:
                        after(pe, "c_v", nxt if more else u)
                    if r == 2:
                        after(pe, "c_pT", u, per=3, k=1)
                    for j in range(4):
                        last = pe.transpose(PS[:, 4 + r % 2, j * T:(j + 1) * T], c["E"][:, 4 * r + j, :], ident[:, :])
                    last.then_inc(s["c_p_turned"], 1)
                after(pe, "c_pT", u, per=3)
                after(pe, "c_v", u)
                if more:
                    after(pe, "c_k", nxt)
                for h in range(HEADS):
                    last = mm(PS[:, 7, h * (HD + 1):(h + 1) * (HD + 1)], c["PT"][:, (h % 4) * 3 + h // 4, :],
                              c["v"][u.slot][:, h, :], True, True)
                last.then_inc(s["c_attended"], 1)

            pe.wait_ge(s["in_C"], 64)
            pipelined(pe, B, 2, 3, [(c_turn, 0), (c_scores, 1), (c_turn_ctx, 2), (c_qkv, 0), (c_project, 2),
                                    (c_values, 1)])
            phase_end(pe, "pe", 3)

            q = D

            def ups(f, weights, sl):
                wh, wl = weights
                for m in range(HCH):
                    after(pe, "gelu", f, back=1, per=HCH, k=HCH + m - 1) if m < 2 else \
                        after(pe, "gelu", f, per=HCH, k=m - 1)
                    o, k = PS[:, 2 + m % 2, :], slice(m * 128, m * 128 + 128)
                    mm(o, wh[:, 0, k], q["hA"][sl][:, :], True, False)
                    mm(o, wl[:, 0, k], q["hA"][sl][:, :], False, False)
                    mm(o, wh[:, 0, k], q["lA"][sl][:, :], False, False)
                    mm(o, wh[:, 1, k], q["sB"][sl][:, :], False, False)
                    mm(o, wl[0:C1, 1, k], q["sB"][sl][0:C1, :], False, True).then_inc(s["up"], 1)

            def downs(f, weights):
                wh, wl = weights
                for m in range(HCH):
                    after(pe, "gelu_split", f, per=HCH, k=m + 1)
                    if m == 0:
                        after(pe, "down_read", f, back=1, per=GB)
                    for t in range(GB):
                        o, k = PS[:, 4 + t, 0:C], slice(t * T, t * T + T)
                        mm(o, q["Gh"][:, m, k], wh[:, m, :], m == 0, False)
                        mm(o, q["Gh"][:, m, k], wl[:, m, :], False, False)
                        last = mm(o, q["Gl"][:, m, k], wh[:, m, :], False, m == HCH - 1)
                        if m == HCH - 1:
                            last.then_inc(s["down"], 1)

            def turn_group(sem_in, u, sem_free, sem_out):
                after(pe, sem_in, u, per=GB)
                if sem_free is not None:
                    sem_free()
                for t in range(GB):
                    pe.transpose(PS[:, 0, t * T:(t + 1) * T], q["xs"][t][:, 0:128], ident[:, :])
                for t in range(GB):
                    last = pe.transpose(PS[:, 1, t * T:(t + 1) * T], q["xs"][t][:, 128:256], ident[:, :])
                last.then_inc(sem_out, 1)

            def d_mlp(u):
                turn_group("x_copied", u, lambda: after(pe, "gate_read", u, back=1), s["x_turned"])
                after(pe, "x_split", u)
                ups(u, (w_up(WH, 0), w_up(WL, 0)), 0)
                downs(u, (w_down(WH, 0), w_down(WL, 0)))
                turn_group("xm_copied", u, None, s["xm_turned"])
                after(pe, "xm_scaled", u, per=2)
                for t in range(GB):
                    o = PS[:, 0, t * NEXP:(t + 1) * NEXP]
                    mm(o, q["G"][0][:, t * T:(t + 1) * T], wg[:, 0, :], True, False)
                    last = mm(o, q["G"][1][0:C1, t * T:(t + 1) * T], wg[0:C1, 1, :], False, True)
                last.then_inc(s["gated"], 1)

            pe.wait_ge(s["in_D"], 16)
            pipelined(pe, NG, 1, 2, [(d_mlp, 0)])

            def d_experts(u):
                after(pe, "xm_split", u)
                for e in range(NEXP):
                    f = Unit(u.v * NEXP + (NG + e), u.lo * NEXP + NG + e, 0)
                    ups(f, (w_up(WH, 1 + e), w_up(WL, 1 + e)), u.slot)
                    downs(f, (w_down(WH, 1 + e), w_down(WL, 1 + e)))

            pipelined(pe, NG, 2, 0, [(d_experts, 0)])
            phase_end(pe, "pe", 4)

            e_ = Em
            pe.wait_ge(s["in_E"], 64)

            def e_turn(u):
                after(pe, "e_normed", u, per=GB)
                after(pe, "e_added", u, back=2, per=GB)
                for t in range(GB):
                    pe.transpose(PS[:, 0, t * T:(t + 1) * T], e_["zn"][t][:, 0:128], ident[:, :])
                for t in range(GB):
                    last = pe.transpose(PS[:, 1, t * T:(t + 1) * T], e_["zn"][t][:, 128:256], ident[:, :])
                last.then_inc(s["e_turned"], 1)

            def e_project(u):
                for j, n in enumerate("kvr"):
                    w, x = e_["w"][n], e_["mx"][n]
                    after(pe, "e_mixed", u, per=3, k=j + 1)
                    after(pe, f"e_read_{n}", u, back=1)
                    b0, b1 = PS[:, 2 + 2 * j, :], PS[:, 3 + 2 * j, :]
                    mm(b0, w[:, 0, 0:128], x[:, 0:GB, :], True, False)

                    def rest(p):
                        return mm(b0[:, 256 * p:256 * p + 256], w[64 * p:64 * p + 64, 1, 0:128],
                                  x[64 * p:64 * p + 64, GB:NB6, :], False, p == 1)

                    rest(0).then_inc(s["e_half"], 1)
                    for p in range(2):
                        mm(b1[64 * p:64 * p + 64, 0:256], w[:, 0, 128:C], x[:, 2 * p:2 * p + 2, :], True, False)
                    for p in range(2):
                        mm(b1[64 * p:64 * p + 64, 0:256], w[64 * p:64 * p + 64, 1, 128:C],
                           x[64 * p:64 * p + 64, GB:NB6, :], False, True)
                    after(pe, "e_half", u, per=3, k=j + 1)
                    last = rest(1)
                    last.then_inc(s["e_projected"], 1)

            def e_out(u):
                after(pe, "e_rw", u)
                nxt_read = (not isinstance(u.v, int)) or u.v + 1 < NG
                if nxt_read:
                    after(pe, "e_zT", Unit(u.v + 1, u.lo + 1, 0), per=3)
                for t in range(GB):
                    o = PS[:, t // 2, (t % 2) * C:(t % 2) * C + C]
                    p = t // 2
                    mm(o, e_["rw"][u.slot][:, t, :], e_["w"]["o"][:, 0, :], True, False)
                    last = mm(o, e_["rw"][u.slot][64 * p:64 * p + 64, GB + t % 2, :],
                              e_["w"]["o"][64 * p:64 * p + 64, 1, :], False, True)
                last.then_inc(s["e_out"], 1)

            pipelined(pe, NG, 2, 2, [(e_turn, 0), (e_project, 0), (e_out, 1)])
            pe.wait_ge(s["f_wsum"], 1)
            mm(PS[:, 7, 256:258], ones[:, :], qs[:, 0:2], True, True).then_inc(s["f_wmean"], 1)
            phase_end(pe, "pe", 5)

            f_ = Fm

            def f_turn(u):
                after(pe, "f_q", u)
                after(pe, "f_qT", u, back=1)
                tb = PS[:, 0, :].bitcast(BF16)
                pe.transpose(tb[:, 0:128], f_["q"][u.slot][:, 0:128], identb[:, :])
                pe.transpose(tb[0:C1, 128:256], f_["q"][u.slot][:, 128:C], identb[:, :]).then_inc(s["f_turned"], 1)

            def f_up(u):
                after(pe, "f_qT", u)
                for j in range(2):
                    o = PS[:, 1 + 2 * u.slot + j, :]
                    if j == 0:
                        after(pe, "f_y", u, back=2)
                    for k in range(2):
                        n = 128 if k == 0 else C1
                        last = mm(o, f_["qT"][u.slot][0:n, k, :], wI[0:n, k, j * BH:(j + 1) * BH], k == 0, k == 1)
                last.then_inc(s["f_up"], 1)

            def f_turn2(u):
                after(pe, "f_q2", u)
                after(pe, "f_q2T", u, back=1)
                tb = PS[:, 5, :].bitcast(BF16)
                for k in range(BH // 128):
                    last = pe.transpose(tb[:, k * T:(k + 1) * T], f_["q2"][u.slot][:, k * 128:(k + 1) * 128],
                                        identb[:, :])
                last.then_inc(s["f_turned2"], 1)

            def f_down(u):
                after(pe, "f_q2T", u)
                after(pe, "o_ready", u, back=1)
                for k in range(BH // 128):
                    last = mm(PS[:, 6, 0:C], f_["q2T"][u.slot][:, k, :], wO[:, k, :], k == 0, k == BH // 128 - 1)
                last.then_inc(s["f_down"], 1)

            pipelined(pe, B, 2, 2, [(f_turn2, 2), (f_down, 2), (f_turn, 0), (f_up, 0)])

        @block.scalar
        def _(act):
            def w_high(u):
                arrived(act, u)
                act.copy(WH[:, bass.ts(u.v, PIECE)], raw[u.slot][:, :]).then_inc(s["w_hi"], 1)

            a = A
            act.wait_ge(s["in_x0"], 48)

            def a_tap(u):
                after(act, "pointwise", u, back=2, per=2)
                act.activation(a["cv0"][u.slot][:, :, :], a["x0"][:, u.v, :, 0:S], ACT.Identity,
                               bias=col("b_dw", 0), scale=cols[:, TAP:TAP + 1])
                act.activation(a["cv1"][u.slot][:, :], a["x1"][:, u.v, 0:S], ACT.Identity,
                               bias=col("b_dw", 1), scale=cols[:, TAP + TAPS:TAP + TAPS + 1]).then_inc(s["tap0"], 1)

            def a_tap_(u):
                if u.lo == 2:
                    act.wait_ge(s["in_x"], 32)
                a_tap(u)

            def a_relu(u):
                for p in range(2):
                    i = 2 * u.slot + p
                    after(act, "pooled", u, per=2, k=p + 1)
                    after(act, "dft_c", u, back=2, per=2, k=p + 1)
                    act.activation(a["hT"][i][:, 0, :], a["hp"][i][:, 0, :], ACT.Relu, bias=col("b_pw", 0))
                    act.activation(a["hT"][i][0:C1, 1, :], a["hp"][i][0:C1, 1, :], ACT.Relu,
                                   bias=col("b_pw", 1, C1)).then_inc(s["relu"], 1)

            def a_copy(u):
                for p in range(2):
                    after(act, "dft_c", u, per=2, k=p + 1)
                    after(act, "dft_t", u, back=1, per=2, k=p + 1)
                    act.copy(a["Z"][p][:, :], PS[:, 4 + p, 0:2 * C]).then_inc(s["z_copied"], 1)

            pipelined(act, B // 2, 2, 2, [(a_tap_, 0), (a_relu, 1), (a_copy, 2)])
            phase_end(act, "act", 1)

            m_ = Bm

            def b_zT(u):
                after(act, "b_turned", u)
                after(act, "b_v_made", u, back=2)
                act.copy(m_["zT"][u.slot][:, 0, :], PS[:, 0, 0:128])
                act.copy(m_["zT"][u.slot][0:C1, 1, :], PS[0:C1, 0, 128:256]).then_inc(s["b_zT"], 1)

            def b_qk(u):
                after(act, "b_qk_made", u)
                after(act, "b_scored", u, back=2)
                for j, (n, bias) in enumerate((("qT", "bq"), ("kT", "bk"))):
                    act.activation(m_[n][u.slot][:, 0, :], PS[:, 1, 2 * j * T:(2 * j + 1) * T], ACT.Identity,
                                   bias=col(bias, 0))
                    last = act.activation(m_[n][u.slot][0:C1, 1, :], PS[0:C1, 1, (2 * j + 1) * T:(2 * j + 2) * T],
                                          ACT.Identity, bias=col(bias, 1, C1))
                last.then_inc(s["b_qk"], 1)

            def b_exp(u):
                after(act, "b_max", u)
                after(act, "b_p_turned", u, back=2)
                act.activation(m_["p"][u.slot][:, :], PS[:, 3, 0:T], ACT.Exp, bias=m_["nm"][u.slot][:, 1:2],
                               scale=C ** -0.5, accum_out=m_["sum"][u.slot][:, 0:1]).then_inc(s["b_exp"], 1)

            pipelined(act, B, 2, 2, [(b_exp, 2), (b_qk, 1), (b_zT, 0), (w_high, 0)])
            phase_end(act, "act", 2)

            c = Cm

            def c_zT(u):
                after(act, "c_turned", u)
                after(act, "c_v_made", u, back=2)
                act.activation(c["zT"][u.slot][:, 0, :], PS[:, 6, 0:128], ACT.Identity, bias=col("ln1_b", 0),
                               scale=col("ln1_g", 0))
                act.activation(c["zT"][u.slot][0:C1, 1, :], PS[0:C1, 6, 128:256], ACT.Identity,
                               bias=col("ln1_b", 1, C1), scale=col("ln1_g", 1, C1)).then_inc(s["c_zT"], 1)

            def c_q(u):
                after(act, "c_q_made", u)
                after(act, "c_scored", u, back=2)
                for g in range(3):
                    last = act.activation(c["qT"][u.slot][:, g, :], PS[:, 6, g * T:(g + 1) * T], ACT.Identity,
                                          bias=cols[:, QB + g:QB + g + 1])
                last.then_inc(s["c_q"], 1)

            def c_exp(u):
                after(act, "c_sub", u)
                act.activation(c["E"][:, :, :], c["E"][:, :, :], ACT.Exp, scale=HD ** -0.5).then_inc(s["c_exp"], 1)

            def c_pT(u):
                for r in range(3):
                    after(act, "c_p_turned", u, per=3, k=r + 1)
                    after(act, "c_attended", u, back=1)
                    act.copy(c["PT"][:, 4 * r:4 * r + 4, :],
                             PS[:, 4 + r % 2, :].rearrange("p (h t) -> p h t", h=4)).then_inc(s["c_pT"], 1)

            def c_cT(u):
                after(act, "c_ctx_turned", u)
                after(act, "c_projected", u, back=2)
                act.copy(c["cT"][u.slot][:, 0, :], PS[:, 7, 0:128])
                act.copy(c["cT"][u.slot][0:C1, 1, :], PS[0:C1, 7, 128:256]).then_inc(s["c_cT"], 1)

            pipelined(act, B, 2, 3, [(c_zT, 0), (c_cT, 2), (c_q, 0), (c_exp, 1),
                                     (lambda u: w_high(shifted(u)), 0), (c_pT, 1)])
            phase_end(act, "act", 3)

            q = D

            def gelus(f, fi):
                for m in range(HCH):
                    after(act, "up", f, per=HCH, k=m + 1)
                    after(act, "gelu_split", f, back=1, per=HCH, k=HCH + m - 1) if m < 2 else \
                        after(act, "gelu_split", f, per=HCH, k=m - 1)
                    act.activation(q["G"][m % 2][:, :], PS[:, 2 + m % 2, :], ACT.Gelu,
                                   bias=cols[:, HB + fi * HCH + m:HB + fi * HCH + m + 1]).then_inc(s["gelu"], 1)

            def d_mlp(u):
                after(act, "x_turned", u)
                act.copy(q["hA"][0][:, :], PS[:, 0, :]).then_inc(s["x_hi"], 1)
                act.copy(q["sB"][0][:, :], PS[:, 1, :]).then_inc(s["x_hi"], 1)
                after(act, "gated", u, back=1)
                gelus(u, 0)
                after(act, "xm_turned", u)
                after(act, "gelu_split", u, per=HCH)
                for k in range(2):
                    last = act.activation(q["G"][k][:, :], PS[:, k, :], ACT.Identity, bias=col("ln2_b", k),
                                          scale=col("ln2_g", k)).then_inc(s["xm_scaled"], 1)
                after(act, "xm_scaled", u, per=2)
                for k in range(2):
                    act.copy(q["XF"][:, k, u.v, :], q["G"][k][:, :]).then_inc(s["xf_made"], 1)

            pipelined(act, NG, 1, 2, [(d_mlp, 0)])
            act.wait_ge(s["logit_sub"], 1)
            act.wait_ge(s["gated"], NG)
            act.activation(q["comb"][:, :, :], q["cmp"][:, :, :], ACT.Exp).then_inc(s["gate_exp"], 1)

            def d_experts(u):
                for e in range(NEXP):
                    gelus(Unit(u.v * NEXP + (NG + e), u.lo * NEXP + NG + e, 0), 1 + e)

            pipelined(act, NG, 2, 0, [(d_experts, 0)])
            phase_end(act, "act", 4)

            e_ = Em
            act.wait_ge(s["e_consts"], 9)
            act.activation(e_["ndec"][:, :], cols[:, COL["decay"]:COL["decay"] + 2], ACT.Exp)\
                .then_inc(s["e_decay"], 1)

            def e_zT(u):
                after(act, "e_turned", u)
                after(act, "e_mixed", u, back=1, per=3)
                act.copy(e_["zT"][:, 0:GB, 1:T + 1], PS[:, 0, :].rearrange("p (b t) -> p b t", b=GB))\
                    .then_inc(s["e_zT"], 1)
                for p in range(2):
                    act.copy(e_["zT"][64 * p:64 * p + 64, GB:NB6, 1:T + 1],
                             PS[64 * p:64 * p + 64, 1, 256 * p:256 * p + 256].rearrange("p (b t) -> p b t", b=2))\
                        .then_inc(s["e_zT"], 1)
                after(act, "e_zT", u, per=3)
                for n in "kvr":
                    for k, bl in enumerate((slice(0, GB), slice(GB, NB6))):
                        last = act.activation(e_["mt"][n][:, bl, :], e_["zT"][:, bl, 1:T + 1], ACT.Copy,
                                              scale=col("mix_" + n, k))
                    last.then_inc(s["e_mt"], 1)

            def e_read(u):
                def banks(j):
                    return (PS[:, 2 + 2 * j, :].rearrange("p (b t) -> p b t", b=GB),
                            PS[:, 3 + 2 * j, 0:256].rearrange("p (b t) -> p b t", b=2))
                i = u.slot
                after(act, "e_projected", u, per=3, k=1)
                after(act, "e_rw", u, back=2)
                for k, bl in enumerate((slice(0, GB), slice(GB, NB6))):
                    act.copy(e_["K"][i][:, bl, 1:T + 1], banks(0)[k])
                    last = act.activation(e_["ku"][i][:, bl, :], banks(0)[k], ACT.Identity, bias=col("first", k))
                last.then_inc(s["e_read_k"], 1)
                after(act, "e_projected", u, per=3, k=2)
                for k, bl in enumerate((slice(0, GB), slice(GB, NB6))):
                    last = act.copy(e_["v"][i][:, bl, :], banks(1)[k])
                last.then_inc(s["e_read_v"], 1)
                after(act, "e_projected", u, per=3, k=3)
                for k, bl in enumerate((slice(0, GB), slice(GB, NB6))):
                    last = act.activation(e_["er"][i][:, bl, :], banks(2)[k], ACT.Exp, scale=-1.0)
                last.then_inc(s["e_read_r"], 1)

            def e_exp(u):
                for n, dst, src in (("c", e_["D1"][:, :, 1:T + 1], "c"), ("dd", e_["E2s"][:, :, 1:T + 1], "dd"),
                                    ("a", e_["e1"][:, :, :], "a"), ("b", e_["e2"][:, :, :], "b")):
                    after(act, "e_arg_" + n, u)
                    after(act, "e_rw", u, back=1)
                    act.activation(dst, e_[src][:, :, :], ACT.Exp).then_inc(s["e_exp_" + n], 1)

            pipelined(act, NG, 2, 2, [(e_zT, 0), (e_exp, 1), (e_read, 0)])
            phase_end(act, "act", 5)

            f_ = Fm

            def f_qT(u):
                tb = PS[:, 0, :].bitcast(BF16)
                after(act, "f_turned", u)
                after(act, "f_up", u, back=2)
                act.copy(f_["qT"][u.slot][:, 0, :], tb[:, 0:128])
                act.copy(f_["qT"][u.slot][0:C1, 1, :], tb[0:C1, 128:256]).then_inc(s["f_qT"], 1)

            def f_silu(u):
                after(act, "f_up", u)
                after(act, "f_y", u, back=2)
                act.activation(f_["sg"][u.slot][:, :], PS[:, 2 + 2 * u.slot, :], ACT.Silu,
                               scale=f_["rs"][u.slot][:, 6:7]).then_inc(s["f_silu"], 1)

            def f_square(u):
                after(act, "f_y", u)
                after(act, "o_ready", u, back=2)
                act.activation(f_["sq"][u.slot][:, :], f_["y"][u.slot][:, :], ACT.Square,
                               accum_out=f_["rs"][u.slot][:, 7:8]).then_inc(s["f_sq"], 1)

            def f_q2T(u):
                after(act, "f_turned2", u)
                after(act, "f_down", u, back=2)
                tb = PS[:, 5, :].bitcast(BF16)
                act.copy(f_["q2T"][u.slot][:, :, :], tb[:, 0:BH].rearrange("p (k t) -> p k t", k=BH // 128))\
                    .then_inc(s["f_q2T"], 1)

            pipelined(act, B, 2, 2, [(f_q2T, 2), (f_square, 1), (f_qT, 0), (f_silu, 0)])

        @block.vector
        def _(dve):
            def stt(o, i0, sc, i1, op0, op1, **kw):
                return dve.scalar_tensor_tensor(out=o, in0=i0, scalar=sc, in1=i1, op0=op0, op1=op1, **kw)

            def tt(o, i0, i1, op):
                return dve.tensor_tensor(o, i0, i1, op)

            a = A
            dve.wait_ge(s["in_x0"], 48)

            def a_taps(u):
                if u.lo == 2:
                    dve.wait_ge(s["in_x"], 32)
                after(dve, "tap0", u)
                for k in range(1, TAPS):
                    if k > 1:
                        after(dve, "tap_a", u, per=TAPS - 1, k=k - 1)
                    stt(a["cv0"][u.slot][:, :, :], a["x0"][:, u.v, :, k:k + S], cols[:, TAP + k:TAP + k + 1],
                        a["cv0"][u.slot][:, :, :], ALU.mult, ALU.add).then_inc(s["tap_a"], 1)
                    if k > 1:
                        after(dve, "tap_b", u, per=TAPS - 1, k=k - 1)
                    stt(a["cv1"][u.slot][:, :], a["x1"][:, u.v, k:k + S], cols[:, TAP + TAPS + k:TAP + TAPS + k + 1],
                        a["cv1"][u.slot][:, :], ALU.mult, ALU.add).then_inc(s["tap_b"], 1)

            def a_pool(u):
                for p in range(2):
                    i = 2 * u.slot + p
                    bank = PS[:, i, :]
                    after(dve, "pointwise", u, per=2, k=p + 1)
                    after(dve, "relu", u, back=2, per=2, k=p + 1)
                    dve.tensor_reduce(a["hp"][i][:, 0, :], bank[:, 0:S].rearrange("p (t two) -> p t two", two=2),
                                      AX.X, ALU.max)
                    dve.tensor_reduce(a["hp"][i][0:C1, 1, :],
                                      bank[0:C1, S:2 * S].rearrange("p (t two) -> p t two", two=2),
                                      AX.X, ALU.max).then_inc(s["pooled"], 1)

            def a_norm(u):
                for p in range(2):
                    i = 2 * u.slot + p
                    after(dve, "dft_t", u, per=2, k=p + 1, nop=True)
                    dve.bn_stats(a["st"][i][:, :], PS[:, 6 + p, 0:C]).then_inc(s["a_st"], 1)
                for p in range(2):
                    i = 2 * u.slot + p
                    after(dve, "a_st", u, per=2, k=p + 1, nop=True)
                    dve.bn_aggr(a["mv"][i][:, :], a["st"][i][:, :]).then_inc(s["a_mv"], 1)
                for p in range(2):
                    i = 2 * u.slot + p
                    after(dve, "a_rstd", u, per=2, k=p + 1)
                    after(dve, "h_A", u, back=2, per=2, k=p + 1)
                    dve.tensor_scalar(a["yn"][i][:, :], PS[:, 6 + p, 0:C], a["mv"][i][:, 0:1], a["rs"][i][:, 1:2],
                                      ALU.subtract, ALU.mult).then_inc(s["y_normed"], 1)

            pipelined(dve, B // 2, 2, 2, [(a_taps, 0), (a_pool, 1), (a_norm, 2)])
            phase_end(dve, "dve", 1)

            m_ = Bm

            def b_stats(u):
                i = u.slot
                dve.bn_stats(m_["st"][i][:, :], H[:, u.v, :]).then_inc(s["b_st"], 1)
                after(dve, "b_st", u, nop=True)
                dve.bn_aggr(m_["mv"][i][:, :], m_["st"][i][:, :]).then_inc(s["b_mv"], 1)

            def b_norm(u):
                i = u.slot
                after(dve, "b_rstd", u)
                after(dve, "b_turned", u, back=2)
                dve.tensor_scalar(m_["zn"][i][:, :], H[:, u.v, :], m_["mv"][i][:, 0:1], m_["rs"][i][:, 1:2],
                                  ALU.subtract, ALU.mult).then_inc(s["b_normed"], 1)

            def b_v(u):
                after(dve, "b_v_made", u)
                after(dve, "b_attended", u, back=2)
                tt(m_["v"][u.slot][:, :], PS[:, 2, 0:C], row("bv"), ALU.add).then_inc(s["b_v"], 1)

            def b_max(u):
                i = u.slot
                after(dve, "b_scored", u)
                dve.tensor_reduce(m_["nm"][i][:, 0:1], PS[:, 3, 0:T], AX.X, ALU.max).then_inc(s["b_rowmax"], 1)
                after(dve, "b_rowmax", u)
                dve.tensor_scalar(m_["nm"][i][:, 1:2], m_["nm"][i][:, 0:1], -(C ** -0.5), None, ALU.mult)\
                    .then_inc(s["b_max"], 1)

            def b_pT(u):
                after(dve, "b_p_turned", u)
                after(dve, "b_attended", u, back=2)
                dve.tensor_copy(m_["pT"][u.slot][:, :], PS[:, 4, 0:T]).then_inc(s["b_pT"], 1)
                dve.reciprocal(m_["sum"][u.slot][:, 1:2], m_["sum"][u.slot][:, 0:1]).then_inc(s["b_recip"], 1)

            def b_add(u):
                i = u.slot
                after(dve, "b_attended", u)
                after(dve, "b_recip", u)
                stt(H[:, u.v, :], PS[:, 5, 0:C], m_["sum"][i][:, 1:2], H[:, u.v, :], ALU.mult, ALU.add)\
                    .then_inc(s["b_added"], 1)

            pipelined(dve, B, 2, 2, [(b_stats, 0), (b_max, 2), (b_norm, 0), (b_v, 1), (b_pT, 2), (b_add, 2)])
            phase_end(dve, "dve", 2)

            c = Cm
            for i in range(2):
                dve.memset(c["v"][i][:, :, HD:HD + 1], 1.0).then_inc(s["c_ones"], 1)
            dve.wait_ge(s["c_ones"], 2)

            def c_stats(u):
                i = u.slot
                dve.bn_stats(c["st"][i][:, :], H[:, u.v, :]).then_inc(s["c_st"], 1)
                after(dve, "c_st", u, nop=True)
                dve.bn_aggr(c["mv"][i][:, :], c["st"][i][:, :]).then_inc(s["c_mv"], 1)

            def c_norm(u):
                i = u.slot
                after(dve, "c_rstd", u)
                dve.tensor_scalar(X[:, u.v, :], H[:, u.v, :], c["mv"][i][:, 0:1], c["rs"][i][:, 1:2],
                                  ALU.subtract, ALU.mult).then_inc(s["c_x"], 1)
                after(dve, "c_x", u)
                after(dve, "c_turned", u, back=2)
                dve.tensor_scalar(c["zn"][i][:, :], X[:, u.v, :], c["rs"][i][:, 5:6], None, ALU.mult)\
                    .then_inc(s["c_normed"], 1)

            def c_k(u):
                after(dve, "c_k_made", u)
                after(dve, "c_scored", u, back=2)
                tt(c["kT"][u.slot][:, :, :], PS[:, 7, 0:3 * T].rearrange("p (g t) -> p g t", g=3),
                   cols[:, KB:KB + 3].rearrange("p (g one) -> p g one", one=1).to_broadcast([128, 3, T]), ALU.add)\
                    .then_inc(s["c_k"], 1)
                after(dve, "c_v_made", u)
                after(dve, "c_attended", u, back=2)
                tt(c["v"][u.slot][:, :, 0:HD], PS[:, 5, 0:C].rearrange("p (h e) -> p h e", h=HEADS),
                   row("in_bv").rearrange("p (h e) -> p h e", h=HEADS), ALU.add).then_inc(s["c_v"], 1)

            def c_softmax(u):
                sc = PS[:, 0:4, 0:3 * T].rearrange("p j (g t) -> p j g t", g=3)
                after(dve, "c_scored", u)
                dve.tensor_reduce(c["mx"][u.slot][:, :].rearrange("p (j g) -> p j g", j=4), sc, AX.X, ALU.max)\
                    .then_inc(s["c_max"], 1)
                after(dve, "c_max", u)
                after(dve, "c_p_turned", u, back=1, per=3)
                tt(c["E"][:, :, :].rearrange("p (j g) t -> p j g t", j=4), sc,
                   c["mx"][u.slot][:, :].rearrange("p (j g one) -> p j g one", j=4, one=1).to_broadcast([128, 4, 3, T]),
                   ALU.subtract).then_inc(s["c_sub"], 1)

            def c_ctx(u):
                at = PS[:, 7, 0:HEADS * (HD + 1)].rearrange("p (h e) -> p h e", h=HEADS)
                after(dve, "c_attended", u)
                rd = c["rd"][u.slot][:, :].rearrange("p (h one) -> p h one", one=1)
                dve.reciprocal(rd, at[:, :, HD:HD + 1]).then_inc(s["c_recip"], 1)
                after(dve, "c_recip", u)
                after(dve, "c_ctx_turned", u, back=2)
                tt(c["cx"][u.slot][:, :].rearrange("p (h e) -> p h e", h=HEADS), at[:, :, 0:HD],
                   rd.to_broadcast([128, HEADS, HD]), ALU.mult).then_inc(s["c_ctx"], 1)

            def c_add(u):
                after(dve, "c_projected", u)
                after(dve, "c_xb", u)
                tt(X[:, u.v, :], PS[:, 6, 0:C], X[:, u.v, :], ALU.add).then_inc(s["c_added"], 1)

            pipelined(dve, B, 2, 3, [(c_stats, 0), (c_norm, 0), (c_softmax, 1), (c_k, 0), (c_add, 2), (c_ctx, 1)])
            phase_end(dve, "dve", 3)

            q = D

            def split_gelu(f):
                for m in range(HCH):
                    after(dve, "gelu", f, per=HCH, k=m + 1)
                    dve.tensor_copy(q["Gh"][:, m, :], q["G"][m % 2][:, :]).then_inc(s["gelu_hi"], 1)
                    after(dve, "gelu_hi", f, per=HCH, k=m + 1)
                    tt(q["Gl"][:, m, :], q["G"][m % 2][:, :], q["Gh"][:, m, :].bitcast(F32), ALU.subtract)\
                        .then_inc(s["gelu_split"], 1)

            def d_mlp(u):
                after(dve, "x_hi", u, per=2, k=1)
                tt(q["lA"][0][:, :], PS[:, 0, :], q["hA"][0][:, :].bitcast(F32), ALU.subtract)\
                    .then_inc(s["x_lo"], 1)
                after(dve, "x_hi", u, per=2, k=2)
                tt(q["sB"][0][64:128, :], PS[64:128, 1, :], q["sB"][0][64:128, :].bitcast(F32), ALU.subtract)\
                    .then_inc(s["x_split"], 1)
                split_gelu(u)
                for t in range(GB):
                    after(dve, "down", u, per=GB, k=t + 1)
                    after(dve, "xb_D", u, per=GB, k=t + 1)
                    tt(X[:, u.v * GB + t, :], PS[:, 4 + t, 0:C], X[:, u.v * GB + t, :], ALU.add)\
                        .then_inc(s["down_read"], 1)
                for t in range(GB):
                    after(dve, "down_read", u, per=GB, k=t + 1, nop=True)
                    dve.bn_stats(q["st"][:, t, :], X[:, u.v * GB + t, :]).then_inc(s["d_st"], 1)
                for t in range(GB):
                    after(dve, "d_st", u, per=GB, k=t + 1, nop=True)
                    dve.bn_aggr(q["mv"][:, t, :], q["st"][:, t, :]).then_inc(s["d_mv"], 1)
                after(dve, "d_rstd", u)
                for t in range(GB):
                    after(dve, "x_turned", u)
                    dve.tensor_scalar(q["xs"][t][:, 0:C], X[:, u.v * GB + t, :], q["mv"][:, t, 0:1],
                                      q["rs"][:, t, 1:2], ALU.subtract, ALU.mult).then_inc(s["xm"], 1)
                after(dve, "gated", u)
                tt(q["LG"][:, bass.ts(u.v, GB), :], PS[:, 0, 0:GB * NEXP].rearrange("p (t e) -> p t e", t=GB),
                   row("gate_b").rearrange("p (one e) -> p one e", one=1).to_broadcast([128, GB, NEXP]), ALU.add)\
                    .then_inc(s["gate_read"], 1)

            pipelined(dve, NG, 1, 2, [(d_mlp, 0)])

            n_link = [0]

            def link(ins):
                n_link[0] += 1
                ins.then_inc(s["gate_chain"], 1)
                dve.wait_ge(s["gate_chain"], n_link[0])

            LG, rank, cmp_, top, comb = q["LG"], q["rank"], q["cmp"], q["top"], q["comb"]
            dve.wait_ge(s["gate_read"], NG)
            for j in range(NEXP):
                lj = LG[:, :, j:j + 1].to_broadcast([128, B, NEXP])
                if j == 0:
                    link(tt(rank[:, :, :], lj, LG[:, :, :], ALU.is_gt))
                else:
                    link(tt(cmp_[:, :, :], lj, LG[:, :, :], ALU.is_gt))
                    link(tt(rank[:, :, :], rank[:, :, :], cmp_[:, :, :], ALU.add))
            for j in range(NEXP - 1):
                n = NEXP - 1 - j
                link(tt(cmp_[:, :, 0:n], LG[:, :, j:j + 1].to_broadcast([128, B, n]), LG[:, :, j + 1:NEXP], ALU.is_equal))
                link(tt(rank[:, :, j + 1:NEXP], rank[:, :, j + 1:NEXP], cmp_[:, :, 0:n], ALU.add))
            link(dve.tensor_reduce(top[:, :], LG[:, :, :], AX.X, ALU.max))
            tt(cmp_[:, :, :], LG[:, :, :], top[:, :].rearrange("p (b one) -> p b one", one=1).to_broadcast([128, B, NEXP]),
               ALU.subtract).then_inc(s["logit_sub"], 1)
            dve.wait_ge(s["gate_exp"], 1)
            link(stt(comb[:, :, :], rank[:, :, :], 2.0, comb[:, :, :], ALU.is_lt, ALU.mult))
            link(dve.tensor_reduce(top[:, :], comb[:, :, :], AX.X, ALU.add))
            link(dve.reciprocal(top[:, :], top[:, :]))
            tt(comb[:, :, :], comb[:, :, :], top[:, :].rearrange("p (b one) -> p b one", one=1).to_broadcast([128, B, NEXP]),
               ALU.mult).then_inc(s["comb"], 1)
            dve.wait_ge(s["comb"], 1)

            def d_split(u):
                i = u.slot
                hi0, hi1 = q["XF"][:, 0, u.v, :], q["XF"][:, 1, u.v, :]
                if u.lo == 0:
                    dve.wait_ge(s["xf_made"], 2 * NG)
                dve.tensor_copy(q["hA"][i][:, :], hi0).then_inc(s["xm_hi"], 1)
                dve.tensor_copy(q["sB"][i][:, :], hi1).then_inc(s["xm_hi"], 1)
                after(dve, "xm_hi", u, per=2, k=1)
                tt(q["lA"][i][:, :], hi0, q["hA"][i][:, :].bitcast(F32), ALU.subtract).then_inc(s["xm_lo"], 1)
                after(dve, "xm_hi", u, per=2, k=2)
                tt(q["sB"][i][64:128, :], hi1[64:128, :], q["sB"][i][64:128, :].bitcast(F32), ALU.subtract)\
                    .then_inc(s["xm_split"], 1)

            def d_experts(u):
                for e in range(NEXP):
                    f = Unit(u.v * NEXP + (NG + e), u.lo * NEXP + NG + e, 0)
                    split_gelu(f)
                    for t in range(GB):
                        after(dve, "down", f, per=GB, k=t + 1)
                        if e == 0:
                            after(dve, "acc0", u, per=GB, k=t + 1)
                        else:
                            after(dve, "down_read", f, back=1, per=GB, k=t + 1)
                        stt(q["acc"][t][:, :], PS[:, 4 + t, 0:C], comb[:, u.v * GB + t, e:e + 1], q["acc"][t][:, :],
                            ALU.mult, ALU.add).then_inc(s["down_read"], 1)

            pipelined(dve, NG, 2, 0, [(d_split, 0), (d_experts, 0)])
            phase_end(dve, "dve", 4)

            e_ = Em
            for n in "kvr":
                dve.tensor_scalar(e_["om"][n][:, :], cols[:, COL["mix_" + n]:COL["mix_" + n] + 2], -1.0, 1.0,
                                  ALU.mult, ALU.add).then_inc(s["e_consts"], 1)
            dve.memset(e_["zT"][:, :, 0:1], 0.0).then_inc(s["e_consts"], 1)
            for i in range(2):
                dve.memset(e_["K"][i][:, :, 0:1], FAR).then_inc(s["e_consts"], 1)
            for n in ("D1", "E2s", "EV"):
                dve.memset(e_[n][:, :, 0:1], 0.0).then_inc(s["e_consts"], 1)
            dve.wait_ge(s["e_consts"], 9)
            dve.wait_ge(s["e_decay"], 1)
            dve.memset(e_["WD"][:, :, :], 0.0).then_inc(s["e_wd"], 1)
            dve.tensor_scalar(e_["ndec"][:, :], e_["ndec"][:, :], -1.0, None, ALU.mult).then_inc(s["e_wd"], 1)
            dve.wait_ge(s["e_wd"], 2)
            for k, bl in enumerate((slice(0, GB), slice(GB, NB6))):
                dve.tensor_scalar(e_["WD"][:, bl, :], e_["WD"][:, bl, :], e_["ndec"][:, k:k + 1], None, ALU.add)\
                    .then_inc(s["e_wd"], 1)
            dve.wait_ge(s["e_wd"], 4)
            dve.memset(e_["WD"][:, :, 0:1], FAR).then_inc(s["e_wd"], 1)
            dve.wait_ge(s["e_wd"], 5)

            def e_norm(u):
                for t in range(GB):
                    dve.bn_stats(e_["st"][:, t, :], H[:, u.v * GB + t, :]).then_inc(s["e_st"], 1)
                for t in range(GB):
                    after(dve, "e_st", u, per=GB, k=t + 1, nop=True)
                    dve.bn_aggr(e_["mv"][:, t, :], e_["st"][:, t, :]).then_inc(s["e_mv"], 1)
                after(dve, "e_rstd", u)
                after(dve, "e_turned", u, back=1)
                for t in range(GB):
                    dve.tensor_scalar(e_["zn"][t][:, 0:C], H[:, u.v * GB + t, :], e_["mv"][:, t, 0:1],
                                      e_["rs"][:, t, 1:2], ALU.subtract, ALU.mult).then_inc(s["e_zn"], 1)

            def e_mix(u):
                for j, n in enumerate("kvr"):
                    after(dve, "e_mt", u, per=3, k=j + 1)
                    after(dve, "e_projected", u, back=1, per=3, k=j + 1)
                    for k, bl in enumerate((slice(0, GB), slice(GB, NB6))):
                        last = stt(e_["mx"][n][:, bl, :], e_["zT"][:, bl, 0:T], e_["om"][n][:, k:k + 1],
                                   e_["mt"][n][:, bl, :], ALU.mult, ALU.add)
                    last.then_inc(s["e_mixed"], 1)

            def flat(t):
                return t[:, :, :].rearrange("p b t -> p (b t)")

            def e_wkv(u):
                i = u.slot
                K, ku, v, er = e_["K"][i], e_["ku"][i], e_["v"][i], e_["er"][i]
                MX, D1, E2s, EV, NUM, DEN = (e_[n] for n in ("MX", "D1", "E2s", "EV", "NUM", "DEN"))
                prev, new = slice(0, T), slice(1, T + 1)
                after(dve, "e_read_k", u)
                dve.tensor_tensor_scan(flat(MX), flat(e_["WD"]), flat(K), FAR, ALU.add, ALU.max)\
                    .then_inc(s["e_mxscan"], 1)
                after(dve, "e_mxscan", u)
                tt(e_["mo"][:, :, :], ku[:, :, :], MX[:, :, prev], ALU.max).then_inc(s["e_mo"], 1)
                for k, bl in enumerate((slice(0, GB), slice(GB, NB6))):
                    last = stt(e_["c"][:, bl, :], MX[:, bl, prev], e_["ndec"][:, k:k + 1], MX[:, bl, new],
                               ALU.add, ALU.subtract)
                last.then_inc(s["e_arg_c"], 1)
                tt(e_["dd"][:, :, :], K[:, :, new], MX[:, :, new], ALU.subtract).then_inc(s["e_arg_dd"], 1)
                after(dve, "e_mo", u)
                tt(e_["a"][:, :, :], MX[:, :, prev], e_["mo"][:, :, :], ALU.subtract).then_inc(s["e_arg_a"], 1)
                tt(e_["b"][:, :, :], ku[:, :, :], e_["mo"][:, :, :], ALU.subtract).then_inc(s["e_arg_b"], 1)
                after(dve, "e_exp_dd", u)
                after(dve, "e_read_v", u)
                tt(EV[:, :, new], E2s[:, :, new], v[:, :, :], ALU.mult).then_inc(s["e_ev"], 1)
                after(dve, "e_exp_c", u)
                dve.tensor_tensor_scan(flat(DEN), flat(D1), flat(E2s), 0.0, ALU.mult, ALU.add)\
                    .then_inc(s["e_den"], 1)
                after(dve, "e_ev", u)
                dve.tensor_tensor_scan(flat(NUM), flat(D1), flat(EV), 0.0, ALU.mult, ALU.add)\
                    .then_inc(s["e_num"], 1)
                after(dve, "e_exp_b", u)
                after(dve, "e_exp_a", u)
                tt(e_["t2"][:, :, :], e_["e2"][:, :, :], v[:, :, :], ALU.mult).then_inc(s["e_t2"], 1)
                after(dve, "e_den", u)
                tt(e_["t3"][:, :, :], e_["e1"][:, :, :], DEN[:, :, prev], ALU.mult).then_inc(s["e_t3"], 1)
                after(dve, "e_num", u)
                tt(e_["t1"][:, :, :], e_["e1"][:, :, :], NUM[:, :, prev], ALU.mult).then_inc(s["e_t1"], 1)
                after(dve, "e_t3", u)
                tt(e_["t3"][:, :, :], e_["t3"][:, :, :], e_["e2"][:, :, :], ALU.add).then_inc(s["e_t3b"], 1)
                after(dve, "e_t1", u)
                after(dve, "e_t2", u)
                tt(e_["t1"][:, :, :], e_["t1"][:, :, :], e_["t2"][:, :, :], ALU.add).then_inc(s["e_t1b"], 1)
                after(dve, "e_t3b", u)
                after(dve, "e_read_r", u)
                stt(e_["t3"][:, :, :], er[:, :, :], 1.0, e_["t3"][:, :, :], ALU.add, ALU.mult)\
                    .then_inc(s["e_t3c"], 1)
                after(dve, "e_t3c", u)
                dve.reciprocal(e_["t3"][:, :, :], e_["t3"][:, :, :]).then_inc(s["e_t3d"], 1)
                after(dve, "e_t3d", u)
                after(dve, "e_t1b", u)
                after(dve, "e_out", u, back=2)
                tt(e_["rw"][i][:, :, :], e_["t1"][:, :, :], e_["t3"][:, :, :], ALU.mult).then_inc(s["e_rw"], 1)

            def e_add(u):
                after(dve, "e_out", u)
                for t in range(GB):
                    h = H[:, u.v * GB + t, :]
                    tt(h, PS[:, t // 2, (t % 2) * C:(t % 2) * C + C], h, ALU.add).then_inc(s["e_added"], 1)

            pipelined(dve, NG, 2, 2, [(e_norm, 0), (e_mix, 0), (e_wkv, 1), (e_add, 1)])
            dve.wait_ge(s["in_F"], 32)
            dve.wait_ge(s["pool_ones"], 1)
            dve.tensor_reduce(qs[:, 2:4], rawI[:, :, :], AX.X, ALU.add, apply_absolute_value=True)\
                .then_inc(s["f_prep"], 1)
            dve.tensor_reduce(qs[:, 1:2], rawO[:, :, :], AX.XY, ALU.add, apply_absolute_value=True)\
                .then_inc(s["f_prep"], 1)
            dve.wait_ge(s["f_prep"], 2)
            stt(qs[:, 0:1], qs[:, 3:4], 0.5, qs[:, 2:3], ALU.mult, ALU.add).then_inc(s["f_wsum"], 1)
            dve.wait_ge(s["f_wmean"], 1)
            dve.tensor_scalar(qs[:, 4:5], PS[:, 7, 256:257], 1.0 / (2 * BH * C), EPS_Q, ALU.mult, ALU.max)\
                .then_inc(s["f_prep"], 1)
            dve.tensor_scalar(qs[:, 5:6], PS[:, 7, 257:258], 1.0 / (BH * C), EPS_Q, ALU.mult, ALU.max)\
                .then_inc(s["f_prep"], 1)
            dve.wait_ge(s["f_prep"], 4)
            dve.reciprocal(qs[:, 6:8], qs[:, 4:6]).then_inc(s["f_prep"], 1)
            dve.wait_ge(s["f_prep"], 5)
            for j, (raw, w) in enumerate(((rawI, wI), (rawO, wO))):
                dve.tensor_scalar(raw[:, :, :], raw[:, :, :], qs[:, 6 + j:7 + j], MAGIC, ALU.mult, ALU.add)\
                    .then_inc(s["f_prep"], 1)
            for j, (raw, w) in enumerate(((rawI, wI), (rawO, wO))):
                dve.wait_ge(s["f_prep"], 6 + j)
                dve.tensor_scalar(raw[:, :, :], raw[:, :, :], MAGIC, 1.0, ALU.subtract, ALU.min)\
                    .then_inc(s["f_prep2"], 1)
            for j, (raw, w) in enumerate(((rawI, wI), (rawO, wO))):
                dve.wait_ge(s["f_prep2"], 1 + j)
                dve.tensor_scalar(w[:, :, :], raw[:, :, :], -1.0, None, ALU.max)
            phase_end(dve, "dve", 5)

            f_ = Fm

            def f_stats(u):
                i = u.slot
                dve.bn_stats(f_["st"][i][:, :], H[:, u.v, :]).then_inc(s["f_st"], 1)
                after(dve, "f_st", u)
                after(dve, "f_c", u, back=2, nop=True)
                dve.bn_aggr(f_["mv"][i][:, :], f_["st"][i][:, :]).then_inc(s["f_mv"], 1)

            def f_quant(u):
                i = u.slot
                rs = f_["rs"][i]
                after(dve, "f_rstd", u)
                dve.tensor_scalar(f_["xn"][i][:, :], H[:, u.v, :], f_["mv"][i][:, 0:1], rs[:, 2:3],
                                  ALU.subtract, ALU.mult).then_inc(s["f_xn"], 1)
                after(dve, "f_xn", u)
                tt(f_["xg"][i][:, :], f_["xn"][i][:, :], row("g_in"), ALU.mult).then_inc(s["f_xg"], 1)
                after(dve, "f_xg", u)
                dve.tensor_reduce(rs[:, 3:4], f_["xg"][i][:, :], AX.X, ALU.max, apply_absolute_value=True)\
                    .then_inc(s["f_amax"], 1)
                after(dve, "f_amax", u)
                dve.tensor_scalar(rs[:, 4:5], rs[:, 3:4], EPS_Q, 1.0 / 127.0, ALU.max, ALU.mult)\
                    .then_inc(s["f_step"], 1)
                after(dve, "f_step", u)
                dve.reciprocal(rs[:, 5:6], rs[:, 4:5]).then_inc(s["f_scale"], 1)
                dve.tensor_scalar(rs[:, 6:7], rs[:, 4:5], qs[:, 4:5], None, ALU.mult).then_inc(s["f_c"], 1)
                after(dve, "f_scale", u)
                dve.tensor_scalar(f_["xn"][i][:, :], f_["xg"][i][:, :], rs[:, 5:6], MAGIC, ALU.mult, ALU.add)\
                    .then_inc(s["f_round"], 1)
                after(dve, "f_round", u)
                dve.tensor_scalar(f_["xg"][i][:, :], f_["xn"][i][:, :], MAGIC, 127.0, ALU.subtract, ALU.min)\
                    .then_inc(s["f_sub"], 1)
                after(dve, "f_sub", u)
                after(dve, "f_turned", u, back=2)
                dve.tensor_scalar(f_["q"][i][:, :], f_["xg"][i][:, :], -128.0, None, ALU.max).then_inc(s["f_q"], 1)

            def f_gate(u):
                i = u.slot
                rs = f_["rs"][i]
                after(dve, "f_silu", u)
                stt(f_["y"][i][:, :], PS[:, 1 + 2 * i, :], rs[:, 6:7], f_["sg"][i][:, :], ALU.mult, ALU.mult)\
                    .then_inc(s["f_y"], 1)

            def f_quant2(u):
                i = u.slot
                rs = f_["rs"][i]
                after(dve, "f_yg", u)
                dve.tensor_reduce(rs[:, 8:9], f_["yg"][i][:, :], AX.X, ALU.max, apply_absolute_value=True)\
                    .then_inc(s["f_amax2"], 1)
                after(dve, "f_rms", u)
                after(dve, "f_amax2", u)
                dve.tensor_scalar(rs[:, 9:10], rs[:, 8:9], rs[:, 7:8], EPS_Q, ALU.mult, ALU.max)\
                    .then_inc(s["f_amax3"], 1)
                after(dve, "f_amax3", u)
                dve.reciprocal(rs[:, 10:11], rs[:, 9:10]).then_inc(s["f_inv"], 1)
                dve.tensor_scalar(rs[:, 11:12], rs[:, 9:10], qs[:, 5:6], 1.0 / 127.0, ALU.mult, ALU.mult)\
                    .then_inc(s["f_c2"], 1)
                after(dve, "f_inv", u)
                dve.tensor_scalar(rs[:, 10:11], rs[:, 10:11], rs[:, 7:8], 127.0, ALU.mult, ALU.mult)\
                    .then_inc(s["f_scale2"], 1)
                after(dve, "f_scale2", u)
                dve.tensor_scalar(f_["yg"][i][:, :], f_["yg"][i][:, :], rs[:, 10:11], MAGIC, ALU.mult, ALU.add)\
                    .then_inc(s["f_round2"], 1)
                after(dve, "f_round2", u)
                dve.tensor_scalar(f_["yg"][i][:, :], f_["yg"][i][:, :], MAGIC, 127.0, ALU.subtract, ALU.min)\
                    .then_inc(s["f_sub2"], 1)
                after(dve, "f_sub2", u)
                after(dve, "f_turned2", u, back=2)
                dve.tensor_scalar(f_["q2"][i][:, :], f_["yg"][i][:, :], -128.0, None, ALU.max)\
                    .then_inc(s["f_q2"], 1)

            def f_add(u):
                i = u.slot
                after(dve, "f_down", u)
                after(dve, "f_c2", u)
                stt(f_["o"][:, u.v, :], PS[:, 6, 0:C], f_["rs"][i][:, 11:12], H[:, u.v, :], ALU.mult, ALU.add)\
                    .then_inc(s["o_ready"], 1)

            pipelined(dve, B, 2, 2, [(f_stats, 0), (f_add, 2), (f_quant2, 1), (f_quant, 0), (f_gate, 0)])

        @block.gpsimd
        def _(pool):
            def rsqrt(dst, tmp, src, eps, sem, u, per=1, k=None):
                pool.tensor_scalar(tmp, src, eps, None, ALU.add).then_inc(s[sem + "_a"], 1)
                after(pool, sem + "_a", u, per=per, k=k)
                return pool.tensor_tensor(dst, tmp, expo[:, 0:1], ALU.pow)

            pool.memset(expo[:, :], -0.5).then_inc(s["expo"], 1)
            pool.wait_ge(s["expo"], 1)
            pool.wait_ge(s["in_A"], 16 * 5)
            pool.tensor_copy(identb[:, :], ident[:, :])

            def w_low(u):
                after(pool, "w_hi", u)
                pool.tensor_tensor(WL[:, bass.ts(u.v, PIECE)], raw[u.slot][:, :],
                                   WH[:, bass.ts(u.v, PIECE)].bitcast(F32), ALU.subtract).then_inc(s["w_lo"], 1)

            a = A

            def a_rstd(u):
                for p in range(2):
                    i = 2 * u.slot + p
                    after(pool, "a_mv", u, per=2, k=p + 1, nop=True)
                    rsqrt(a["rs"][i][:, 1:2], a["rs"][i][:, 0:1], a["mv"][i][:, 1:2], EPS, "a_rs", u, 2, p + 1)\
                        .then_inc(s["a_rstd"], 1)

            def a_affine(u):
                for p in range(2):
                    i = 2 * u.slot + p
                    h = H[:, u.v + p * (B // 2), :]
                    after(pool, "y_normed", u, per=2, k=p + 1)
                    pool.tensor_tensor(a["yn"][i][:, :], a["yn"][i][:, :], row("gamma"), ALU.mult)\
                        .then_inc(s["a_gamma"], 1)
                    after(pool, "a_gamma", u, per=2, k=p + 1)
                    pool.tensor_tensor(h, a["yn"][i][:, :], row("beta"), ALU.add).then_inc(s["h_A"], 1)

            pipelined(pool, B // 2, 2, 2, [(a_rstd, 2), (a_affine, 2)])
            phase_end(pool, "pool", 1)
            m_ = Bm

            def b_rstd(u):
                i = u.slot
                after(pool, "b_mv", u, nop=True)
                rsqrt(m_["rs"][i][:, 1:2], m_["rs"][i][:, 0:1], m_["mv"][i][:, 1:2], EPS, "b_rs", u)\
                    .then_inc(s["b_rstd"], 1)

            pipelined(pool, B, 2, 2, [(b_rstd, 0), (w_low, 0)])
            phase_end(pool, "pool", 2)
            c = Cm

            def c_rstd(u):
                i = u.slot
                rs, var = c["rs"][i], c["mv"][i][:, 1:2]
                after(pool, "c_mv", u)
                after(pool, "c_normed", u, back=2, nop=True)
                rsqrt(rs[:, 1:2], rs[:, 0:1], var, EPS, "c_rs", u).then_inc(s["c_rstd1"], 1)
                after(pool, "c_rstd1", u)
                pool.tensor_tensor(rs[:, 2:3], rs[:, 1:2], rs[:, 1:2], ALU.mult).then_inc(s["c_rr"], 1)
                after(pool, "c_rr", u)
                pool.tensor_tensor(rs[:, 3:4], rs[:, 2:3], var, ALU.mult).then_inc(s["c_var2"], 1)
                after(pool, "c_var2", u, nop=True)
                rsqrt(rs[:, 5:6], rs[:, 4:5], rs[:, 3:4], EPS, "c_rs2", u).then_inc(s["c_rstd"], 1)

            def c_xb(u):
                after(pool, "c_normed", u)
                pool.tensor_tensor(X[:, u.v, :], X[:, u.v, :], row("out_b"), ALU.add).then_inc(s["c_xb"], 1)

            pipelined(pool, B, 2, 3, [(c_rstd, 0), (c_xb, 0), (lambda u: w_low(shifted(u)), 0)])
            phase_end(pool, "pool", 3)
            q = D

            def d_copy(u):
                for t in range(GB):
                    x = X[:, u.v * GB + t, :]
                    after(pool, "xm_turned", u, back=1, nop=True)
                    pool.tensor_copy(q["xs"][t][:, 0:C], x).then_inc(s["x_copied1"], 1)
                    pool.tensor_copy(q["xs"][t][:, C:256], X[:, u.v * GB + t, 128:C]).then_inc(s["x_copied"], 1)
                for t in range(GB):
                    x = X[:, u.v * GB + t, :]
                    after(pool, "x_copied", u, per=GB, k=t + 1, nop=True)
                    pool.tensor_tensor(x, x, row("mlp_b2"), ALU.add).then_inc(s["xb_D"], 1)
                for t in range(GB):
                    after(pool, "d_mv", u, per=GB, k=t + 1, nop=True)
                    last = rsqrt(q["rs"][:, t, 1:2], q["rs"][:, t, 0:1], q["mv"][:, t, 1:2], EPS, "d_rs", u, GB, t + 1)
                last.then_inc(s["d_rstd"], 1)
                for t in range(GB):
                    after(pool, "xm", u, per=GB, k=t + 1, nop=True)
                    pool.tensor_copy(q["xs"][t][:, C:256], q["xs"][t][:, 128:C]).then_inc(s["xm_copied"], 1)

            pipelined(pool, NG, 1, 2, [(d_copy, 0)])
            pool.wait_ge(s["comb"], 1)

            def d_start(u):
                for t in range(GB):
                    g = u.v * GB + t
                    acc = q["acc"][t][:, :]
                    after(pool, "h_D", u, back=1, per=2 * GB)
                    for e in range(NEXP):
                        b2 = rows[:, ROW["exp_b2"][0] + e * C:ROW["exp_b2"][0] + (e + 1) * C]
                        if e == 0:
                            pool.tensor_scalar(acc, b2, q["comb"][:, g, 0:1], None, ALU.mult)\
                                .then_inc(s["acc_chain"], 1)
                        else:
                            tmp = q["tmp"][0][:, :]
                            pool.tensor_scalar(tmp, b2, q["comb"][:, g, e:e + 1], None, ALU.mult)\
                                .then_inc(s["acc_chain"], 1)
                            after(pool, "acc_chain", u, per=GB * 7, k=t * 7 + 2 * e)
                            add = pool.tensor_tensor(acc, acc, tmp, ALU.add).then_inc(s["acc_chain"], 1)
                            after(pool, "acc_chain", u, per=GB * 7, k=t * 7 + 2 * e + 1)
                    pool.tensor_tensor(H[:, g, :], H[:, g, :], X[:, g, :], ALU.add).then_inc(s["acc0"], 1)

            def d_finish(u):
                for t in range(GB):
                    g = u.v * GB + t
                    f = Unit(u.v * NEXP + (NG + NEXP - 1), u.lo * NEXP + NG + NEXP - 1, 0)
                    after(pool, "down_read", f, per=GB, k=t + 1)
                    pool.tensor_tensor(H[:, g, :], H[:, g, :], q["acc"][t][:, :], ALU.add).then_inc(s["h_D"], 2)

            pipelined(pool, NG, 2, 2, [(d_start, 0), (d_finish, 0)])
            phase_end(pool, "pool", 4)
            e_ = Em
            pool.memset(ones[:, :], 1.0).then_inc(s["pool_ones"], 1)

            def e_rstd(u):
                for t in range(GB):
                    after(pool, "e_mv", u, per=GB, k=t + 1, nop=True)
                    last = rsqrt(e_["rs"][:, t, 1:2], e_["rs"][:, t, 0:1], e_["mv"][:, t, 1:2], EPS, "e_rs", u,
                                 GB, t + 1)
                last.then_inc(s["e_rstd"], 1)
                for t in range(GB):
                    after(pool, "e_zn", u, per=GB, k=t + 1, nop=True)
                    pool.tensor_copy(e_["zn"][t][:, C:256], e_["zn"][t][:, 128:C]).then_inc(s["e_normed"], 1)

            pipelined(pool, NG, 2, 2, [(e_rstd, 0)])
            phase_end(pool, "pool", 5)
            f_ = Fm

            def f_rstd(u):
                i = u.slot
                rs, var = f_["rs"][i], f_["mv"][i][:, 1:2]
                after(pool, "f_mv", u)
                after(pool, "o_ready", u, back=2, nop=True)
                rsqrt(rs[:, 1:2], rs[:, 0:1], var, EPS, "f_rs", u).then_inc(s["f_rstd1"], 1)
                after(pool, "f_rstd1", u)
                pool.tensor_tensor(rs[:, 2:3], rs[:, 1:2], rs[:, 1:2], ALU.mult).then_inc(s["f_rr"], 1)
                after(pool, "f_rr", u)
                pool.tensor_tensor(rs[:, 3:4], rs[:, 2:3], var, ALU.mult).then_inc(s["f_ms"], 1)
                after(pool, "f_ms", u, nop=True)
                rsqrt(rs[:, 5:6], rs[:, 4:5], rs[:, 3:4], EPS_RMS, "f_rs2", u).then_inc(s["f_rstd2"], 1)
                after(pool, "f_rstd2", u)
                pool.tensor_tensor(rs[:, 2:3], rs[:, 5:6], rs[:, 1:2], ALU.mult).then_inc(s["f_rstd"], 1)

            def f_rms(u):
                i = u.slot
                rs = f_["rs"][i]
                after(pool, "f_y", u)
                after(pool, "f_q2", u, back=2)
                pool.tensor_tensor(f_["yg"][i][:, :], f_["y"][i][:, :], row("g_out"), ALU.mult)\
                    .then_inc(s["f_yg"], 1)
                after(pool, "f_sq", u, nop=True)
                pool.tensor_scalar(rs[:, 7:8], rs[:, 7:8], 1.0 / BH, EPS_RMS, ALU.mult, ALU.add)\
                    .then_inc(s["f_ms2"], 1)
                after(pool, "f_ms2", u)
                pool.tensor_tensor(rs[:, 7:8], rs[:, 7:8], expo[:, 0:1], ALU.pow).then_inc(s["f_rms"], 1)

            pipelined(pool, B, 2, 2, [(f_rstd, 0), (f_rms, 1)])


def _chunk(wT):
    return np.ascontiguousarray(np.stack([wT[:128], np.concatenate([wT[128:], wT[128:]])], axis=1))


def _vec(v):
    return np.stack([v[:128], np.concatenate([v[128:], v[128:]])], axis=1)


def _headpad(w):
    out = np.zeros((3, 4, 32) + w.shape[1:], w.dtype)
    out[:, :, :HD] = w.reshape(3, 4, HD, *w.shape[1:])
    return out.reshape(384, *w.shape[1:])


def kernel(**inputs):
    import concourse.bacc as _bacc
    from concourse import mybir as _mybir
    from concourse.bass_utils import run_bass_kernel_spmd as _run

    i = {k: np.asarray(v) for k, v in inputs.items()}
    a = {}
    xT = np.pad(i["x"].transpose(2, 0, 1), ((0, 0), (0, 0), (TAPS // 2, TAPS // 2)))
    pair = xT.reshape(C, 2, B // 2, S + TAPS - 1).transpose(0, 2, 1, 3)
    x0 = pair[:128]
    x1 = pair[128:].transpose(2, 0, 1, 3).reshape(128, B // 2, S + TAPS - 1)
    a["x0a"], a["x0b"], a["x1a"], a["x1b"] = x0[:, :2], x0[:, 2:], x1[:, :2], x1[:, 2:]
    a["wpw"] = _chunk(i["L0_tok_w_pw"][:, :, 0].T)
    f32 = np.float32
    ang_c = 2 * np.pi * (np.outer(np.arange(C), np.arange(C)) % C) / C
    ang_t = 2 * np.pi * (np.outer(np.arange(T), np.arange(T)) % T) / T
    a["fd"] = _chunk(np.concatenate([np.cos(ang_c), -np.sin(ang_c)], axis=1).astype(f32))
    a["fs"] = np.stack([np.cos(ang_t), np.sin(ang_t)], axis=1).astype(f32)
    a["ident"] = np.eye(128, dtype=f32)
    a["wq"], a["wk"], a["wv"] = (_chunk(i[f"L0_attn_W{n}"].T) for n in "qkv")
    inw, inb = i["L0_ffn_in_w"], i["L0_ffn_in_b"]
    a["wqC"], a["wkC"] = _chunk(_headpad(inw[:C]).T), _chunk(_headpad(inw[C:2 * C]).T)
    a["wvC"] = _chunk(inw[2 * C:].T)
    a["woC"] = _chunk(i["L0_ffn_out_w"].T)
    ups = [i["L0_ffn_mlp_w1"]] + list(i["L0_ffn_exp_w1"])
    dns = [i["L0_ffn_mlp_w2"]] + list(i["L0_ffn_exp_w2"])
    a["w_ffn"] = np.concatenate([p for f in range(NEXP + 1) for p in (
        _chunk(ups[f]).reshape(128, -1), dns[f].reshape(HCH, 128, C).transpose(1, 0, 2).reshape(128, -1))], axis=1)
    a["wg"] = _chunk(i["L0_ffn_gate_w"].T)
    for n in "kvro":
        a[f"w{n}E"] = _chunk(i[f"L1_attn_W{n}"].T)
    a["w_in"] = _chunk(i["L1_ffn_w_in"].T)
    a["w_out"] = i["L1_ffn_w_out"].T.reshape(BH // 128, 128, C).transpose(1, 0, 2)
    vec = {"b_dw": "L0_tok_b_dw", "b_pw": "L0_tok_b_pw", "bq": "L0_attn_bq", "bk": "L0_attn_bk",
           "ln1_g": "L0_ffn_ln1_g", "ln1_b": "L0_ffn_ln1_b", "ln2_g": "L0_ffn_ln2_g", "ln2_b": "L0_ffn_ln2_b",
           "decay": "L1_attn_time_decay", "first": "L1_attn_time_first", "mix_k": "L1_attn_mix_k",
           "mix_v": "L1_attn_mix_v", "mix_r": "L1_attn_mix_r"}
    parts = [_vec(i[vec[n]]) for n in COLS]
    parts += [_headpad(inb[:C]).reshape(3, 128).T, _headpad(inb[C:2 * C]).reshape(3, 128).T]
    taps = _chunk(i["L0_tok_w_dw"][:, 0, :])
    parts += [taps[:, 0], taps[:, 1]]
    parts += [i["L0_ffn_mlp_b1"].reshape(HCH, 128).T] + [b.reshape(HCH, 128).T for b in i["L0_ffn_exp_b1"]]
    a["cols"] = np.concatenate(parts, axis=1)
    assert a["cols"].shape == (128, NCOL)
    rowv = {"gamma": i["L0_tok_gamma"], "beta": i["L0_tok_beta"], "bv": i["L0_attn_bv"], "in_bv": inb[2 * C:],
            "out_b": i["L0_ffn_out_b"], "mlp_b2": i["L0_ffn_mlp_b2"], "exp_b2": i["L0_ffn_exp_b2"].reshape(-1),
            "g_in": i["L1_ffn_g_in"], "gate_b": i["L0_ffn_gate_b"], "g_out": i["L1_ffn_g_out"]}
    a["rows"] = np.broadcast_to(np.concatenate([rowv[n] for n, _ in ROWS]), (128, NROW))

    nc = _bacc.Bacc("TRN2", target_bir_lowering=False, num_devices=1)
    arrays, aps = {}, {}
    for name, v in a.items():
        v = np.ascontiguousarray(v)
        arrays["in_" + name] = v
        aps[name] = nc.dram_tensor("in_" + name, v.shape, _mybir.dt.from_np(v.dtype), kind="ExternalInput").ap()
    o = nc.dram_tensor("out_0", (B, T, C), _mybir.dt.float32, kind="ExternalOutput").ap()
    audio_tower(nc, aps, o)
    r = _run(nc, [arrays], core_ids=[0])
    return r.results[0]["out_0"]
```

```python
from contextlib import ExitStack

import numpy as np
import concourse.bass as bass
from concourse import mybir

ALU = mybir.AluOpType
ACT = mybir.ActivationFunctionType
AX = mybir.AxisListType
F32 = mybir.dt.float32
F32R = mybir.dt.float32r
BF16 = mybir.dt.bfloat16

B, S, C = 16, 256, 192
T = S // 2
C1 = C - 128
TAPS = 7
HEADS, HD = 12, 16
HID, HCH = 768, 6
NEXP = 4
BH = 512
GB = 4
NG = B // GB
EPS = 1e-5
EPS_RMS = 1e-6
EPS_Q = 1e-5
MAGIC = 12582912.0
FAR = -1e38
WEACH = 2 * HID + HCH * C
PIECE = (NEXP + 1) * WEACH // (2 * B)

COLS = ["b_dw", "b_pw", "bq", "bk", "ln1_g", "ln1_b", "ln2_g", "ln2_b", "decay", "first", "mix_k", "mix_v", "mix_r"]
COL = {n: 2 * i for i, n in enumerate(COLS)}
QB = 2 * len(COLS)
KB = QB + 3
TAP = KB + 3
HB = TAP + 2 * TAPS
NCOL = HB + HCH * (NEXP + 1)
ROWS = [("gamma", C), ("beta", C), ("bv", C), ("in_bv", C), ("out_b", C), ("mlp_b2", C), ("exp_b2", NEXP * C),
        ("g_in", C), ("gate_b", NEXP), ("g_out", BH)]
ROW = {}
NROW = 0
for _n, _w in ROWS:
    ROW[_n] = (NROW, NROW + _w)
    NROW += _w


RETIRED = ["b_" + n for n in ("st mv rs_a rstd normed turned zT qk_made qk v_made v scored rowmax max exp p_turned pT "
                              "recip attended added").split()] + \
          ["c_" + n for n in ("st mv rs_a rstd1 var2 rs2_a rstd x normed xb turned zT q_made q k_made k v_made v "
                              "scored rowmax max exp recip scaled attended cT projected added").split()]


PLAIN = ("e_consts", "e_decay", "e_wd", "f_prep", "f_prep2", "f_wsum", "f_wmean")


class Unit:

    def __init__(self, v, lo, slot):
        self.v, self.lo, self.slot = v, lo, slot


def pipelined(eng, n, unroll, ahead, stages):
    lag_max = max(k for _, k in stages)
    first = -(-(lag_max + ahead) // unroll) * unroll
    rounds = max(0, (n - first) // unroll)

    def step(t, lo, j, hi):
        for fn, lag in stages:
            if lo - lag >= 0 and hi - lag < n:
                fn(Unit(t - lag if lag else t, lo - lag, (j - lag) % unroll))

    if rounds < 2:
        for t in range(n + lag_max):
            step(t, t, t, t)
        return
    for t in range(first):
        step(t, t, t, t)
    with eng.Fori(0, rounds) as i:
        for j in range(unroll):
            step(i * unroll + (first + j), first + j, j, n - 1)
    for t in range(first + rounds * unroll, n + lag_max):
        step(t, t, t, t)


def audio_tower(nc, d, out):
    with ExitStack() as ctx:
        scope = [ctx]

        def sb(name, shape, dt=F32):
            return scope[-1].enter_context(nc.sbuf_tensor(name, shape, dt))

        start = {}
        retired = list(RETIRED)

        class Sems(dict):
            def __missing__(self, name):
                if name[:2] in ("e_", "f_") and name not in PLAIN and retired:
                    self[name] = self[retired.pop(0)]
                    start[name] = B
                else:
                    self[name] = ctx.enter_context(nc.semaphore(name))
                return self[name]

        s = Sems()

        def after(eng, name, u, back=0, per=1, k=None, nop=False):
            k = per if k is None else k
            if u.lo - back < 0:
                assert isinstance(u.v, int)
                return
            sem = s[name]
            eng.wait_ge(sem, u.v * per + (k - back * per + start.get(name, 0)))
            if nop:
                eng.nop(nofuse=True)

        PS = ctx.enter_context(nc.psum_tensor("PS", [128, 8, 512], F32))

        H = sb("H", [128, B, C])
        cols = sb("cols", [128, NCOL])
        rows = sb("rows", [128, NROW])
        ident = sb("ident", [128, 128])
        identb = sb("identb", [128, 128], BF16)
        expo = sb("expo", [128, 2])
        magic = sb("magic", [128, 2])

        def col(name, c, n=128):
            return cols[0:n, COL[name] + c:COL[name] + c + 1]

        def row(name):
            return rows[:, ROW[name][0]:ROW[name][1]]

        mem_w = ExitStack()
        scope.append(mem_w)
        NF = NEXP + 1
        WH = sb("WH", [128, NF * WEACH], F32R)
        WL = sb("WL", [128, NF * WEACH], F32R)

        def w_up(w, f):
            return w[:, f * WEACH:f * WEACH + 2 * HID].rearrange("p (k n) -> p k n", k=2)

        def w_down(w, f):
            return w[:, f * WEACH + 2 * HID:(f + 1) * WEACH].rearrange("p (m n) -> p m n", m=HCH)

        X = sb("X", [128, B, C])

        mem_abc = ExitStack()
        scope.append(mem_abc)
        raw = [sb(f"raw{i}", [128, PIECE]) for i in range(2)]
        mem = ExitStack()
        scope.append(mem)
        x0 = sb("x0", [128, B // 2, 2, S + TAPS - 1])
        x1 = sb("x1", [128, B // 2, S + TAPS - 1])
        wpw = sb("wpw", [128, 2, C])
        fd = sb("fd", [128, 2, 2 * C])
        fs = sb("fs", [128, 2, T])
        cv0 = [sb(f"cv0{i}", [128, 2, S]) for i in range(2)]
        cv1 = [sb(f"cv1{i}", [128, S]) for i in range(2)]
        hp = [sb(f"hp{i}", [128, 2, T]) for i in range(4)]
        hT = [sb(f"hT{i}", [128, 2, T]) for i in range(4)]
        Z = [sb(f"Z{i}", [128, 2 * C]) for i in range(2)]
        yn = [sb(f"yn{i}", [128, C]) for i in range(4)]
        st = [sb(f"stA{i}", [128, 6]) for i in range(4)]
        mv = [sb(f"mvA{i}", [128, 2]) for i in range(4)]
        rs = [sb(f"rsA{i}", [128, 2]) for i in range(4)]
        A = dict(x0=x0, x1=x1, wpw=wpw, fd=fd, fs=fs, cv0=cv0, cv1=cv1, hp=hp, hT=hT, Z=Z, yn=yn, st=st, mv=mv, rs=rs)
        scope.pop().close()

        mem = ExitStack()
        scope.append(mem)
        Bm = dict(wq=sb("wq", [128, 2, C]), wk=sb("wk", [128, 2, C]), wv=sb("wv", [128, 2, C]),
                  **{n: [sb(f"{n}B{i}", sh) for i in range(2)] for n, sh in (
                      ("st", [128, 6]), ("mv", [128, 2]), ("rs", [128, 2]), ("zn", [128, C]), ("zT", [128, 2, T]),
                      ("qT", [128, 2, T]), ("kT", [128, 2, T]), ("v", [128, C]), ("p", [128, T]), ("pT", [128, T]),
                      ("nm", [128, 2]), ("sum", [128, 2]), ("un", [128, C]))})
        scope.pop().close()

        mem = ExitStack()
        scope.append(mem)
        Cm = dict(wq=sb("wqC", [128, 2, 384]), wk=sb("wkC", [128, 2, 384]), wv=sb("wvC", [128, 2, C]),
                  wo=sb("woC", [128, 3, C]), E=[sb(f"E{i}", [128, HEADS, T]) for i in range(2)], PT=sb("PT", [128, HEADS, T]),
                  **{n: [sb(f"{n}C{i}", sh) for i in range(2)] for n, sh in (
                      ("st", [128, 6]), ("mv", [128, 2]), ("rs", [128, 6]), ("zn", [128, C]), ("zT", [128, 2, T]),
                      ("qT", [128, 3, T]), ("kT", [128, 3, T]), ("v", [128, HEADS, 32]), ("mx", [128, HEADS]),
                      ("nm", [128, HEADS]), ("sum", [128, HEADS]), ("rd", [128, HEADS]), ("cT", [128, 3, T]))})
        scope.pop().close()
        scope.pop().close()

        mem = ExitStack()
        scope.append(mem)
        wg = sb("wg", [128, 2, NEXP])
        D = dict(
            xs=[sb(f"xs{t}", [128, 256]) for t in range(GB)],
            XF=sb("XF", [128, 2, NG, GB * T]),
            hA=[sb(f"hA{i}", [128, GB * T], F32R) for i in range(2)],
            lA=[sb(f"lA{i}", [128, GB * T], F32R) for i in range(2)],
            sB=[sb(f"sB{i}", [128, GB * T], F32R) for i in range(2)],
            G=[sb(f"G{i}", [128, GB * T]) for i in range(2)],
            Gh=sb("Gh", [128, HCH, GB * T], F32R), Gl=sb("Gl", [128, HCH, GB * T], F32R),
            st=sb("stD", [128, GB, 6]), mv=sb("mvD", [128, GB, 2]), rs=sb("rsD", [128, GB, 2]),
            LG=sb("LG", [128, B, NEXP]), rank=sb("rank", [128, B, NEXP]), cmp=sb("cmp", [128, B, NEXP]),
            top=sb("top", [128, B]), comb=sb("comb", [128, B, NEXP]),
            acc=[sb(f"acc{t}", [128, C]) for t in range(GB)], tmp=[sb(f"tmpD{t}", [128, C]) for t in range(2)])
        scope.pop().close()
        scope.pop().close()

        mem_ef = ExitStack()
        scope.append(mem_ef)
        rawI = sb("rawI", [128, 2, 2 * BH])
        rawO = sb("rawO", [128, BH // 128, C])
        wI = sb("wI", [128, 2, 2 * BH], BF16)
        wO = sb("wO", [128, BH // 128, C], BF16)
        qs = sb("qs", [128, 8])
        ones = sb("ones", [128, 128])
        mem = ExitStack()
        scope.append(mem)
        NB6 = GB + GB // 2
        Em = dict(
            w={n: sb(f"w{n}E", [128, 2, C]) for n in "kvro"},
            om={n: sb(f"om{n}", [128, 2]) for n in "kvr"}, ndec=sb("ndec", [128, 2]),
            WD=sb("WD", [128, NB6, T + 1]),
            zn=[sb(f"znE{t}", [128, 256]) for t in range(GB)],
            st=sb("stE", [128, GB, 6]), mv=sb("mvE", [128, GB, 2]), rs=sb("rsE", [128, GB, 2]),
            zT=sb("zTE", [128, NB6, T + 1]), mt={n: sb(f"mt{n}", [128, NB6, T]) for n in "kvr"},
            mx={n: sb(f"mixed{n}", [128, NB6, T]) for n in "kvr"},
            **{n: [sb(f"{n}E{i}", [128, NB6, T]) for i in range(2)] for n in ("ku", "v", "er")},
            K=[sb(f"KE{i}", [128, NB6, T + 1]) for i in range(2)],
            **{n: sb(f"{n}E", [128, NB6, T + 1]) for n in ("MX", "D1", "E2s", "EV", "NUM", "DEN")},
            **{n: sb(f"{n}E", [128, NB6, T]) for n in ("mo", "a", "b", "c", "dd", "e1", "e2", "t1", "t2", "t3")},
            rw=[sb(f"rw{i}", [128, NB6, T]) for i in range(2)])
        scope.pop().close()
        mem = ExitStack()
        scope.append(mem)
        Fm = dict(**{n: [sb(f"{n}F{i}", sh, dt) for i in range(2)] for n, sh, dt in (
            ("st", [128, 6], F32), ("mv", [128, 2], F32), ("rs", [128, 12], F32), ("xn", [128, C], F32),
            ("xg", [128, C], F32), ("q", [128, C], BF16), ("qT", [128, 2, T], BF16), ("sg", [128, BH], F32),
            ("y", [128, BH], F32), ("yg", [128, BH], F32), ("sq", [128, BH], F32), ("q2", [128, BH], BF16),
            ("q2T", [128, BH // 128, T], BF16))}, o=sb("o", [128, B, C]))
        scope.pop().close()
        scope.pop().close()

        block = ctx.enter_context(nc.Block())
        def shifted(u):
            return Unit(u.v + B, u.lo + B, u.slot)

        def later(u, k):
            return Unit(u.v + k, u.lo + k, 0) if not isinstance(u.v, int) or u.v + k < B else None

        def arrived(eng, u):
            eng.wait_ge(s[f"in_w{u.slot}"], u.v // 2 * 16 + 16 if isinstance(u.v, int) else (u.v - u.slot) * 8 + 16)

        def phase_end(eng, name, k):
            eng.drain().then_inc(s["phase_" + name], 1)
            for n in ("pe", "act", "dve", "pool"):
                eng.wait_ge(s["phase_" + n], k)

        @block.sync
        def _(sp):
            def load(dst, name, sem):
                sp.dma_start(dst, d[name]).then_inc(s[sem], 16)
            load(A["x0"][:, 0:2], "x0a", "in_x0")
            load(A["x1"][:, 0:2], "x1a", "in_x0")
            load(cols[:, :], "cols", "in_x0")
            load(A["x0"][:, 2:8], "x0b", "in_x")
            load(A["x1"][:, 2:8], "x1b", "in_x")
            load(A["wpw"][:, :, :], "wpw", "in_A")
            load(A["fd"][:, :, :], "fd", "in_A")
            load(A["fs"][:, :, :], "fs", "in_A")
            load(rows[:, :], "rows", "in_A")
            load(ident[:, :], "ident", "in_A")

            def ended(k):
                for n in ("pe", "act", "dve", "pool"):
                    sp.wait_ge(s["phase_" + n], k)

            ended(1)
            for n in ("wq", "wk", "wv"):
                load(Bm[n][:, :, :], n, "in_B")

            def load_piece(u):
                after(sp, "w_lo", u, back=2)
                sp.dma_start(raw[u.slot][:, :], d["w_ffn"][:, bass.ts(u.v, PIECE)]).then_inc(s[f"in_w{u.slot}"], 16)

            pipelined(sp, B, 2, 2, [(load_piece, 0)])
            ended(2)
            for n in ("wq", "wk", "wv", "wo"):
                load(Cm[n][:, :, :], n + "C", "in_C")
            pipelined(sp, B, 2, 2, [(lambda u: load_piece(shifted(u)), 0)])
            ended(3)
            load(wg[:, :, :], "wg", "in_D")
            ended(4)
            for n in "kvro":
                load(Em["w"][n][:, :, :], f"w{n}E", "in_E")
            load(rawI[:, :, :], "w_in", "in_F")
            load(rawO[:, :, :], "w_out", "in_F")
            for g in range(NG):
                sp.wait_ge(s["o_ready"], GB * (g + 1))
                sp.dma_start(out[GB * g:GB * g + GB].rearrange("b t c -> t b c"),
                             Fm["o"][:, GB * g:GB * g + GB, :]).then_inc(s["stored"], 16)
            sp.wait_ge(s["stored"], 16 * NG)

        def mm(o, l, r, start, stop, **kw):
            return nc.tensor.matmul(o, l, r, start=start, stop=stop, **kw)

        @block.tensor
        def _(pe):
            a = A

            def a_pointwise(u):
                after(pe, "tap_a", u, per=TAPS - 1)
                after(pe, "tap_b", u, per=TAPS - 1)
                for p in range(2):
                    bank = PS[:, 2 * u.slot + p, :]
                    after(pe, "pooled", u, back=2, per=2, k=p + 1)
                    for m, (lo, hi) in enumerate(((0, 128), (128, C))):
                        o = bank[0:hi - lo, m * S:m * S + S]
                        mm(o, a["wpw"][:, 0, lo:hi], a["cv0"][u.slot][:, p, :], True, False)
                        last = mm(o, a["wpw"][64 * p:64 * p + 64, 1, lo:hi],
                                  a["cv1"][u.slot][64 * p:64 * p + 64, :], False, True)
                    last.then_inc(s["pointwise"], 1)

            def a_dft(u):
                for p in range(2):
                    h = a["hT"][2 * u.slot + p]
                    after(pe, "relu", u, per=2, k=p + 1)
                    after(pe, "z_copied", u, back=1, per=2, k=p + 1)
                    mm(PS[:, 4 + p, 0:2 * C], h[:, 0, :], a["fd"][:, 0, :], True, False)
                    mm(PS[:, 4 + p, 0:2 * C], h[0:C1, 1, :], a["fd"][0:C1, 1, :], False, True)\
                        .then_inc(s["dft_c"], 1)
                for p in range(2):
                    after(pe, "z_copied", u, per=2, k=p + 1)
                    after(pe, "y_normed", u, back=1, per=2, k=p + 1)
                    mm(PS[:, 6 + p, 0:C], a["fs"][:, 0, :], a["Z"][p][:, 0:C], True, False)
                    mm(PS[:, 6 + p, 0:C], a["fs"][:, 1, :], a["Z"][p][:, C:2 * C], False, True)\
                        .then_inc(s["dft_t"], 1)

            pe.wait_ge(s["in_A"], 16 * 5)
            pipelined(pe, B // 2, 2, 2, [(a_pointwise, 1), (a_dft, 2)])
            phase_end(pe, "pe", 1)

            m_ = Bm

            def b_turn(u):
                after(pe, "b_normed", u)
                after(pe, "b_zT", u, back=1)
                pe.transpose(PS[:, 0, 0:128], m_["zn"][u.slot][:, 0:128], ident[:, :])
                pe.transpose(PS[0:C1, 0, 128:256], m_["zn"][u.slot][:, 128:C], ident[:, :]).then_inc(s["b_turned"], 1)

            def b_qkv(u):
                z = m_["zT"][u.slot]
                after(pe, "b_zT", u)
                after(pe, "b_qk", u, back=1)
                for j, w in enumerate((m_["wq"], m_["wk"])):
                    for m, (lo, hi) in enumerate(((0, 128), (128, C))):
                        o = PS[0:hi - lo, 1, (2 * j + m) * T:(2 * j + m + 1) * T]
                        mm(o, w[:, 0, lo:hi], z[:, 0, :], True, False)
                        last = mm(o, w[0:C1, 1, lo:hi], z[0:C1, 1, :], False, True)
                last.then_inc(s["b_qk_made"], 1)
                after(pe, "b_v", u, back=1)
                mm(PS[:, 2, 0:C], z[:, 0, :], m_["wv"][:, 0, :], True, False)
                mm(PS[:, 2, 0:C], z[0:C1, 1, :], m_["wv"][0:C1, 1, :], False, True).then_inc(s["b_v_made"], 1)

            def b_scores(u):
                q, k = m_["qT"][u.slot], m_["kT"][u.slot]
                after(pe, "b_qk", u)
                after(pe, "b_exp", u, back=1)
                mm(PS[:, 3, 0:T], q[:, 0, :], k[:, 0, :], True, False)
                mm(PS[:, 3, 0:T], q[0:C1, 1, :], k[0:C1, 1, :], False, True).then_inc(s["b_scored"], 1)

            def b_turn_p(u):
                after(pe, "b_exp", u)
                after(pe, "b_pT", u, back=1)
                pe.transpose(PS[:, 4, 0:T], m_["p"][u.slot][:, :], ident[:, :]).then_inc(s["b_p_turned"], 1)

            def b_values(u):
                after(pe, "b_pT", u)
                after(pe, "b_v", u)
                after(pe, "b_added", u, back=1)
                mm(PS[:, 5, 0:C], m_["pT"][u.slot][:, :], m_["v"][u.slot][:, :], True, True)\
                    .then_inc(s["b_attended"], 1)

            pe.wait_ge(s["in_B"], 48)
            pipelined(pe, B, 2, 2, [(b_scores, 2), (b_qkv, 1), (b_turn_p, 2), (b_turn, 0), (b_values, 2)])
            phase_end(pe, "pe", 2)

            c = Cm

            def c_turn(u):
                after(pe, "c_normed", u)
                after(pe, "c_q", u, back=1)
                after(pe, "c_added", u, back=4)
                pe.transpose(PS[:, 6, 0:128], c["zn"][u.slot][:, 0:128], ident[:, :])
                pe.transpose(PS[0:C1, 6, 128:256], c["zn"][u.slot][:, 128:C], ident[:, :]).then_inc(s["c_turned"], 1)

            def c_queries(u):
                z = c["zT"][u.slot]
                after(pe, "c_zT", u)
                for g in range(3):
                    o, k = PS[:, 6, g * T:(g + 1) * T], slice(g * 128, (g + 1) * 128)
                    mm(o, c["wq"][:, 0, k], z[:, 0, :], True, False)
                    last = mm(o, c["wq"][0:C1, 1, k], z[0:C1, 1, :], False, True)
                last.then_inc(s["c_q_made"], 1)

            def c_keys(u):
                z = c["zT"][u.slot]
                after(pe, "c_zT", u)
                after(pe, "c_k", u, back=1)
                after(pe, "c_cT", u, back=3)
                for g in range(3):
                    o, k = PS[:, 7, g * T:(g + 1) * T], slice(g * 128, (g + 1) * 128)
                    mm(o, c["wk"][:, 0, k], z[:, 0, :], True, False)
                    last = mm(o, c["wk"][0:C1, 1, k], z[0:C1, 1, :], False, True)
                last.then_inc(s["c_k_made"], 1)

            def c_values(u):
                z = c["zT"][u.slot]
                after(pe, "c_pT", u, back=1, per=2, k=2)
                after(pe, "c_v", u, back=1)
                mm(PS[:, 5, 0:C], z[:, 0, :], c["wv"][:, 0, :], True, False)
                mm(PS[:, 5, 0:C], z[0:C1, 1, :], c["wv"][0:C1, 1, :], False, True).then_inc(s["c_v_made"], 1)

            def c_scores(u):
                after(pe, "c_q", u)
                after(pe, "c_k", u)
                after(pe, "c_exp", u, back=1)
                for g in range(3):
                    for j in range(4):
                        last = mm(PS[:, j, g * T:(g + 1) * T], c["qT"][u.slot][32 * j:32 * j + HD, g, :],
                                  c["kT"][u.slot][32 * j:32 * j + HD, g, :], True, True)
                last.then_inc(s["c_scored"], 1)

            def turn_weights(u, r):
                for j in range(4):
                    last = pe.transpose(PS[:, 4 + r % 2, j * T:(j + 1) * T], c["E"][u.slot][:, 4 * r + j, :], ident[:, :])
                last.then_inc(s["c_p_turned"], 1)

            def c_turn_p01(u):
                after(pe, "c_scaled", u)
                after(pe, "c_pT2", u, back=1)
                turn_weights(u, 0)
                after(pe, "c_v", u)
                turn_weights(u, 1)

            def c_turn_p2(u):
                after(pe, "c_pT", u, per=2, k=1)
                turn_weights(u, 2)

            def c_attend(u):
                after(pe, "c_pT", u, per=2)
                after(pe, "c_pT2", u)
                after(pe, "c_v", u)
                after(pe, "c_cT", u, back=1)
                if later(u, 2):
                    after(pe, "c_k", later(u, 2))
                for h in range(HEADS):
                    j, g = h % 4, h // 4
                    last = mm(PS[32 * j:32 * j + 32, 7, g * T:(g + 1) * T], c["v"][u.slot][:, h, :],
                              c["PT"][:, j * 3 + g, :], True, True)
                last.then_inc(s["c_attended"], 1)

            def c_project(u):
                t = c["cT"][u.slot]
                after(pe, "c_cT", u)
                after(pe, "c_added", u, back=1)
                if later(u, 3):
                    after(pe, "c_q", later(u, 3))
                for g in range(3):
                    last = mm(PS[:, 6, 0:C], t[:, g, :], c["wo"][:, g, :], g == 0, g == 2)
                last.then_inc(s["c_projected"], 1)

            pe.wait_ge(s["in_C"], 64)
            pipelined(pe, B, 2, 3, [(c_scores, 2), (c_turn, 1), (c_turn_p01, 3), (c_queries, 1), (c_turn_p2, 3),
                                    (c_keys, 1), (c_values, 2), (c_project, 4), (c_attend, 3)])
            phase_end(pe, "pe", 3)

            q = D

            def ups(f, weights, sl):
                wh, wl = weights
                for m in range(HCH):
                    after(pe, "gelu", f, back=1, per=HCH, k=HCH + m - 1) if m < 2 else \
                        after(pe, "gelu", f, per=HCH, k=m - 1)
                    o, k = PS[:, 2 + m % 2, :], slice(m * 128, m * 128 + 128)
                    mm(o, wh[:, 0, k], q["hA"][sl][:, :], True, False)
                    mm(o, wl[:, 0, k], q["hA"][sl][:, :], False, False)
                    mm(o, wh[:, 0, k], q["lA"][sl][:, :], False, False)
                    mm(o, wh[:, 1, k], q["sB"][sl][:, :], False, False)
                    mm(o, wl[0:C1, 1, k], q["sB"][sl][0:C1, :], False, True).then_inc(s["up"], 1)

            def downs(f, weights):
                wh, wl = weights
                for m in range(HCH):
                    after(pe, "gelu_split", f, per=HCH, k=m + 1)
                    if m == 0:
                        after(pe, "down_read", f, back=1, per=GB)
                    for t in range(GB):
                        o, k = PS[:, 4 + t, 0:C], slice(t * T, t * T + T)
                        mm(o, q["Gh"][:, m, k], wh[:, m, :], m == 0, False)
                        mm(o, q["Gh"][:, m, k], wl[:, m, :], False, False)
                        last = mm(o, q["Gl"][:, m, k], wh[:, m, :], False, m == HCH - 1)
                        if m == HCH - 1:
                            last.then_inc(s["down"], 1)

            def turn_group(sem_in, u, sem_free, sem_out):
                after(pe, sem_in, u, per=GB)
                if sem_free is not None:
                    sem_free()
                for t in range(GB):
                    pe.transpose(PS[:, 0, t * T:(t + 1) * T], q["xs"][t][:, 0:128], ident[:, :])
                for t in range(GB):
                    last = pe.transpose(PS[:, 1, t * T:(t + 1) * T], q["xs"][t][:, 128:256], ident[:, :])
                last.then_inc(sem_out, 1)

            def d_mlp(u):
                turn_group("x_copied", u, lambda: after(pe, "gate_read", u, back=1), s["x_turned"])
                after(pe, "x_split", u)
                ups(u, (w_up(WH, 0), w_up(WL, 0)), 0)
                downs(u, (w_down(WH, 0), w_down(WL, 0)))
                turn_group("xm_copied", u, None, s["xm_turned"])
                after(pe, "xm_scaled", u, per=2)
                for t in range(GB):
                    o = PS[:, 0, t * NEXP:(t + 1) * NEXP]
                    mm(o, q["G"][0][:, t * T:(t + 1) * T], wg[:, 0, :], True, False)
                    last = mm(o, q["G"][1][0:C1, t * T:(t + 1) * T], wg[0:C1, 1, :], False, True)
                last.then_inc(s["gated"], 1)

            pe.wait_ge(s["in_D"], 16)
            pipelined(pe, NG, 1, 2, [(d_mlp, 0)])

            def d_experts(u):
                after(pe, "xm_split", u)
                for e in range(NEXP):
                    f = Unit(u.v * NEXP + (NG + e), u.lo * NEXP + NG + e, 0)
                    ups(f, (w_up(WH, 1 + e), w_up(WL, 1 + e)), u.slot)
                    downs(f, (w_down(WH, 1 + e), w_down(WL, 1 + e)))

            pipelined(pe, NG, 2, 0, [(d_experts, 0)])
            phase_end(pe, "pe", 4)

            e_ = Em
            pe.wait_ge(s["in_E"], 64)

            def e_turn(u):
                after(pe, "e_normed", u, per=GB)
                after(pe, "e_added", u, back=2, per=GB)
                for t in range(GB):
                    pe.transpose(PS[:, 0, t * T:(t + 1) * T], e_["zn"][t][:, 0:128], ident[:, :])
                for t in range(GB):
                    last = pe.transpose(PS[:, 1, t * T:(t + 1) * T], e_["zn"][t][:, 128:256], ident[:, :])
                last.then_inc(s["e_turned"], 1)

            def e_project(u):
                for j, n in enumerate("kvr"):
                    w, x = e_["w"][n], e_["mx"][n]
                    after(pe, "e_mixed", u, per=3, k=j + 1)
                    after(pe, f"e_read_{n}", u, back=1)
                    b0, b1 = PS[:, 2 + 2 * j, :], PS[:, 3 + 2 * j, :]
                    mm(b0, w[:, 0, 0:128], x[:, 0:GB, :], True, False)

                    def rest(p):
                        return mm(b0[:, 256 * p:256 * p + 256], w[64 * p:64 * p + 64, 1, 0:128],
                                  x[64 * p:64 * p + 64, GB:NB6, :], False, p == 1)

                    rest(0).then_inc(s["e_half"], 1)
                    for p in range(2):
                        mm(b1[64 * p:64 * p + 64, 0:256], w[:, 0, 128:C], x[:, 2 * p:2 * p + 2, :], True, False)
                    for p in range(2):
                        mm(b1[64 * p:64 * p + 64, 0:256], w[64 * p:64 * p + 64, 1, 128:C],
                           x[64 * p:64 * p + 64, GB:NB6, :], False, True)
                    after(pe, "e_half", u, per=3, k=j + 1)
                    last = rest(1)
                    last.then_inc(s["e_projected"], 1)

            def e_out(u):
                after(pe, "e_rw", u)
                nxt_read = (not isinstance(u.v, int)) or u.v + 1 < NG
                if nxt_read:
                    after(pe, "e_zT", Unit(u.v + 1, u.lo + 1, 0), per=3)
                for t in range(GB):
                    o = PS[:, t // 2, (t % 2) * C:(t % 2) * C + C]
                    p = t // 2
                    mm(o, e_["rw"][u.slot][:, t, :], e_["w"]["o"][:, 0, :], True, False)
                    last = mm(o, e_["rw"][u.slot][64 * p:64 * p + 64, GB + t % 2, :],
                              e_["w"]["o"][64 * p:64 * p + 64, 1, :], False, True)
                last.then_inc(s["e_out"], 1)

            pipelined(pe, NG, 2, 2, [(e_turn, 0), (e_project, 0), (e_out, 1)])
            pe.wait_ge(s["f_wsum"], 1)
            mm(PS[:, 7, 256:258], ones[:, :], qs[:, 0:2], True, True).then_inc(s["f_wmean"], 1)
            phase_end(pe, "pe", 5)

            f_ = Fm

            def f_turn(u):
                after(pe, "f_q", u)
                after(pe, "f_qT", u, back=1)
                tb = PS[:, 0, :].bitcast(BF16)
                pe.transpose(tb[:, 0:128], f_["q"][u.slot][:, 0:128], identb[:, :])
                pe.transpose(tb[0:C1, 128:256], f_["q"][u.slot][:, 128:C], identb[:, :]).then_inc(s["f_turned"], 1)

            def f_up(u):
                after(pe, "f_qT", u)
                for j in range(2):
                    o = PS[:, 1 + 2 * u.slot + j, :]
                    if j == 0:
                        after(pe, "f_y", u, back=2)
                    for k in range(2):
                        n = 128 if k == 0 else C1
                        last = mm(o, f_["qT"][u.slot][0:n, k, :], wI[0:n, k, j * BH:(j + 1) * BH], k == 0, k == 1)
                last.then_inc(s["f_up"], 1)

            def f_turn2(u):
                after(pe, "f_q2", u)
                after(pe, "f_q2T", u, back=1)
                tb = PS[:, 5, :].bitcast(BF16)
                for k in range(BH // 128):
                    last = pe.transpose(tb[:, k * T:(k + 1) * T], f_["q2"][u.slot][:, k * 128:(k + 1) * 128],
                                        identb[:, :])
                last.then_inc(s["f_turned2"], 1)

            def f_down(u):
                after(pe, "f_q2T", u)
                after(pe, "o_ready", u, back=1)
                for k in range(BH // 128):
                    last = mm(PS[:, 6, 0:C], f_["q2T"][u.slot][:, k, :], wO[:, k, :], k == 0, k == BH // 128 - 1)
                last.then_inc(s["f_down"], 1)

            pipelined(pe, B, 2, 2, [(f_up, 2), (f_turn, 1), (f_turn2, 3), (f_down, 3)])

        @block.scalar
        def _(act):
            def w_high(u):
                arrived(act, u)
                act.copy(WH[:, bass.ts(u.v, PIECE)], raw[u.slot][:, :]).then_inc(s["w_hi"], 1)

            a = A
            act.wait_ge(s["in_x0"], 48)

            def a_tap(u):
                after(act, "pointwise", u, back=2, per=2)
                act.activation(a["cv0"][u.slot][:, :, :], a["x0"][:, u.v, :, 0:S], ACT.Identity,
                               bias=col("b_dw", 0), scale=cols[:, TAP:TAP + 1])
                act.activation(a["cv1"][u.slot][:, :], a["x1"][:, u.v, 0:S], ACT.Identity,
                               bias=col("b_dw", 1), scale=cols[:, TAP + TAPS:TAP + TAPS + 1]).then_inc(s["tap0"], 1)

            def a_tap_(u):
                if u.lo == 2:
                    act.wait_ge(s["in_x"], 32)
                a_tap(u)

            def a_relu(u):
                for p in range(2):
                    i = 2 * u.slot + p
                    after(act, "pooled", u, per=2, k=p + 1)
                    after(act, "dft_c", u, back=2, per=2, k=p + 1)
                    act.activation(a["hT"][i][:, 0, :], a["hp"][i][:, 0, :], ACT.Relu, bias=col("b_pw", 0))
                    act.activation(a["hT"][i][0:C1, 1, :], a["hp"][i][0:C1, 1, :], ACT.Relu,
                                   bias=col("b_pw", 1, C1)).then_inc(s["relu"], 1)

            def a_copy(u):
                for p in range(2):
                    after(act, "dft_c", u, per=2, k=p + 1)
                    after(act, "dft_t", u, back=1, per=2, k=p + 1)
                    act.copy(a["Z"][p][:, :], PS[:, 4 + p, 0:2 * C]).then_inc(s["z_copied"], 1)

            pipelined(act, B // 2, 2, 2, [(a_tap_, 0), (a_relu, 1), (a_copy, 2)])
            phase_end(act, "act", 1)

            m_ = Bm

            def b_zT(u):
                after(act, "b_turned", u)
                after(act, "b_v_made", u, back=2)
                act.copy(m_["zT"][u.slot][:, 0, :], PS[:, 0, 0:128])
                act.copy(m_["zT"][u.slot][0:C1, 1, :], PS[0:C1, 0, 128:256]).then_inc(s["b_zT"], 1)

            def b_qk(u):
                after(act, "b_qk_made", u)
                after(act, "b_scored", u, back=2)
                for j, (n, bias) in enumerate((("qT", "bq"), ("kT", "bk"))):
                    act.activation(m_[n][u.slot][:, 0, :], PS[:, 1, 2 * j * T:(2 * j + 1) * T], ACT.Identity,
                                   bias=col(bias, 0))
                    last = act.activation(m_[n][u.slot][0:C1, 1, :], PS[0:C1, 1, (2 * j + 1) * T:(2 * j + 2) * T],
                                          ACT.Identity, bias=col(bias, 1, C1))
                last.then_inc(s["b_qk"], 1)

            def b_exp(u):
                after(act, "b_max", u)
                after(act, "b_p_turned", u, back=2)
                act.activation(m_["p"][u.slot][:, :], PS[:, 3, 0:T], ACT.Exp, bias=m_["nm"][u.slot][:, 1:2],
                               scale=C ** -0.5, accum_out=m_["sum"][u.slot][:, 0:1]).then_inc(s["b_exp"], 1)

            pipelined(act, B, 2, 2, [(b_exp, 2), (b_qk, 1), (b_zT, 0), (w_high, 0)])
            phase_end(act, "act", 2)

            c = Cm

            def c_zT(u):
                after(act, "c_turned", u)
                after(act, "c_v_made", u, back=2)
                act.activation(c["zT"][u.slot][:, 0, :], PS[:, 6, 0:128], ACT.Identity, bias=col("ln1_b", 0),
                               scale=col("ln1_g", 0))
                act.activation(c["zT"][u.slot][0:C1, 1, :], PS[0:C1, 6, 128:256], ACT.Identity,
                               bias=col("ln1_b", 1, C1), scale=col("ln1_g", 1, C1)).then_inc(s["c_zT"], 1)

            def c_exp(u):
                after(act, "c_max", u)
                after(act, "c_p_turned", u, back=2, per=3)
                i = u.slot
                for j in range(4):
                    for g in range(3):
                        h = 3 * j + g
                        last = act.activation(c["E"][i][:, h, :], PS[:, j, g * T:(g + 1) * T], ACT.Exp,
                                              bias=c["nm"][i][:, h:h + 1], scale=HD ** -0.5,
                                              accum_out=c["sum"][i][:, h:h + 1])
                last.then_inc(s["c_exp"], 1)

            def c_pT01(u):
                after(act, "c_attended", u, back=1)
                for r in range(2):
                    after(act, "c_p_turned", u, per=3, k=r + 1)
                    act.copy(c["PT"][:, 4 * r:4 * r + 4, :],
                             PS[:, 4 + r, :].rearrange("p (h t) -> p h t", h=4)).then_inc(s["c_pT"], 1)

            def c_cT(u):
                after(act, "c_attended", u)
                after(act, "c_projected", u, back=2)
                act.copy(c["cT"][u.slot][:, :, :], PS[:, 7, 0:3 * T].rearrange("p (g t) -> p g t", g=3))\
                    .then_inc(s["c_cT"], 1)

            pipelined(act, B, 2, 3, [(c_cT, 4), (c_zT, 1), (c_pT01, 3), (c_exp, 2),
                                     (lambda u: w_high(shifted(u)), 0)])
            phase_end(act, "act", 3)

            q = D

            def gelus(f, fi):
                for m in range(HCH):
                    after(act, "up", f, per=HCH, k=m + 1)
                    after(act, "gelu_split", f, back=1, per=HCH, k=HCH + m - 1) if m < 2 else \
                        after(act, "gelu_split", f, per=HCH, k=m - 1)
                    act.activation(q["G"][m % 2][:, :], PS[:, 2 + m % 2, :], ACT.Gelu,
                                   bias=cols[:, HB + fi * HCH + m:HB + fi * HCH + m + 1]).then_inc(s["gelu"], 1)

            def d_mlp(u):
                after(act, "x_turned", u)
                act.copy(q["hA"][0][:, :], PS[:, 0, :]).then_inc(s["x_hi"], 1)
                act.copy(q["sB"][0][:, :], PS[:, 1, :]).then_inc(s["x_hi"], 1)
                after(act, "gated", u, back=1)
                gelus(u, 0)
                after(act, "xm_turned", u)
                after(act, "gelu_split", u, per=HCH)
                for k in range(2):
                    last = act.activation(q["G"][k][:, :], PS[:, k, :], ACT.Identity, bias=col("ln2_b", k),
                                          scale=col("ln2_g", k)).then_inc(s["xm_scaled"], 1)
                after(act, "xm_scaled", u, per=2)
                for k in range(2):
                    act.copy(q["XF"][:, k, u.v, :], q["G"][k][:, :]).then_inc(s["xf_made"], 1)

            pipelined(act, NG, 1, 2, [(d_mlp, 0)])
            act.wait_ge(s["logit_sub"], 1)
            act.wait_ge(s["gated"], NG)
            act.activation(q["comb"][:, :, :], q["cmp"][:, :, :], ACT.Exp).then_inc(s["gate_exp"], 1)

            def d_experts(u):
                for e in range(NEXP):
                    gelus(Unit(u.v * NEXP + (NG + e), u.lo * NEXP + NG + e, 0), 1 + e)

            pipelined(act, NG, 2, 0, [(d_experts, 0)])
            phase_end(act, "act", 4)

            e_ = Em
            act.wait_ge(s["e_consts"], 9)
            act.activation(e_["ndec"][:, :], cols[:, COL["decay"]:COL["decay"] + 2], ACT.Exp)\
                .then_inc(s["e_decay"], 1)

            def e_zT(u):
                after(act, "e_turned", u)
                after(act, "e_mixed", u, back=1, per=3)
                act.copy(e_["zT"][:, 0:GB, 1:T + 1], PS[:, 0, :].rearrange("p (b t) -> p b t", b=GB))\
                    .then_inc(s["e_zT"], 1)
                for p in range(2):
                    act.copy(e_["zT"][64 * p:64 * p + 64, GB:NB6, 1:T + 1],
                             PS[64 * p:64 * p + 64, 1, 256 * p:256 * p + 256].rearrange("p (b t) -> p b t", b=2))\
                        .then_inc(s["e_zT"], 1)
                after(act, "e_zT", u, per=3)
                for n in "kvr":
                    for k, bl in enumerate((slice(0, GB), slice(GB, NB6))):
                        last = act.activation(e_["mt"][n][:, bl, :], e_["zT"][:, bl, 1:T + 1], ACT.Copy,
                                              scale=col("mix_" + n, k))
                    last.then_inc(s["e_mt"], 1)

            def e_read(u):
                def banks(j):
                    return (PS[:, 2 + 2 * j, :].rearrange("p (b t) -> p b t", b=GB),
                            PS[:, 3 + 2 * j, 0:256].rearrange("p (b t) -> p b t", b=2))
                i = u.slot
                after(act, "e_projected", u, per=3, k=1)
                after(act, "e_rw", u, back=2)
                for k, bl in enumerate((slice(0, GB), slice(GB, NB6))):
                    act.copy(e_["K"][i][:, bl, 1:T + 1], banks(0)[k])
                    last = act.activation(e_["ku"][i][:, bl, :], banks(0)[k], ACT.Identity, bias=col("first", k))
                last.then_inc(s["e_read_k"], 1)
                after(act, "e_projected", u, per=3, k=2)
                for k, bl in enumerate((slice(0, GB), slice(GB, NB6))):
                    last = act.copy(e_["v"][i][:, bl, :], banks(1)[k])
                last.then_inc(s["e_read_v"], 1)
                after(act, "e_projected", u, per=3, k=3)
                for k, bl in enumerate((slice(0, GB), slice(GB, NB6))):
                    last = act.activation(e_["er"][i][:, bl, :], banks(2)[k], ACT.Exp, scale=-1.0)
                last.then_inc(s["e_read_r"], 1)

            def e_exp(u):
                for n, dst, src in (("c", e_["D1"][:, :, 1:T + 1], "c"), ("dd", e_["E2s"][:, :, 1:T + 1], "dd"),
                                    ("a", e_["e1"][:, :, :], "a"), ("b", e_["e2"][:, :, :], "b")):
                    after(act, "e_arg_" + n, u)
                    after(act, "e_rw", u, back=1)
                    act.activation(dst, e_[src][:, :, :], ACT.Exp).then_inc(s["e_exp_" + n], 1)

            pipelined(act, NG, 2, 2, [(e_zT, 0), (e_exp, 1), (e_read, 0)])
            phase_end(act, "act", 5)

            f_ = Fm

            def f_unmagic(u):
                after(act, "f_clip", u)
                after(act, "f_turned", u, back=2)
                act.activation(f_["q"][u.slot][:, :], f_["xg"][u.slot][:, :], ACT.Identity, bias=magic[:, 0:1])\
                    .then_inc(s["f_q"], 1)

            def f_unmagic2(u):
                after(act, "f_clip2", u)
                after(act, "f_turned2", u, back=2)
                act.activation(f_["q2"][u.slot][:, :], f_["yg"][u.slot][:, :], ACT.Identity, bias=magic[:, 0:1])\
                    .then_inc(s["f_q2"], 1)

            def f_qT(u):
                tb = PS[:, 0, :].bitcast(BF16)
                after(act, "f_turned", u)
                after(act, "f_up", u, back=2)
                act.copy(f_["qT"][u.slot][:, 0, :], tb[:, 0:128])
                act.copy(f_["qT"][u.slot][0:C1, 1, :], tb[0:C1, 128:256]).then_inc(s["f_qT"], 1)

            def f_silu(u):
                after(act, "f_up", u)
                after(act, "f_y", u, back=2)
                act.activation(f_["sg"][u.slot][:, :], PS[:, 2 + 2 * u.slot, :], ACT.Silu,
                               scale=f_["rs"][u.slot][:, 6:7]).then_inc(s["f_silu"], 1)

            def f_square(u):
                after(act, "f_y", u)
                after(act, "f_scale2", u, back=2)
                act.activation(f_["sq"][u.slot][:, :], f_["y"][u.slot][:, :], ACT.Square,
                               accum_out=f_["rs"][u.slot][:, 7:8]).then_inc(s["f_sq"], 1)

            def f_q2T(u):
                after(act, "f_turned2", u)
                after(act, "f_down", u, back=2)
                tb = PS[:, 5, :].bitcast(BF16)
                act.copy(f_["q2T"][u.slot][:, :, :], tb[:, 0:BH].rearrange("p (k t) -> p k t", k=BH // 128))\
                    .then_inc(s["f_q2T"], 1)

            pipelined(act, B, 2, 2, [(f_square, 3), (f_silu, 2), (f_unmagic, 1), (f_unmagic2, 3), (f_qT, 1), (f_q2T, 3)])

        @block.vector
        def _(dve):
            def stt(o, i0, sc, i1, op0, op1, **kw):
                return dve.scalar_tensor_tensor(out=o, in0=i0, scalar=sc, in1=i1, op0=op0, op1=op1, **kw)

            def tt(o, i0, i1, op):
                return dve.tensor_tensor(o, i0, i1, op)

            a = A
            dve.wait_ge(s["in_x0"], 48)

            def a_taps(u):
                if u.lo == 2:
                    dve.wait_ge(s["in_x"], 32)
                after(dve, "tap0", u)
                for k in range(1, TAPS):
                    if k > 1:
                        after(dve, "tap_a", u, per=TAPS - 1, k=k - 1)
                    stt(a["cv0"][u.slot][:, :, :], a["x0"][:, u.v, :, k:k + S], cols[:, TAP + k:TAP + k + 1],
                        a["cv0"][u.slot][:, :, :], ALU.mult, ALU.add).then_inc(s["tap_a"], 1)
                    if k > 1:
                        after(dve, "tap_b", u, per=TAPS - 1, k=k - 1)
                    stt(a["cv1"][u.slot][:, :], a["x1"][:, u.v, k:k + S], cols[:, TAP + TAPS + k:TAP + TAPS + k + 1],
                        a["cv1"][u.slot][:, :], ALU.mult, ALU.add).then_inc(s["tap_b"], 1)

            def a_pool(u):
                for p in range(2):
                    i = 2 * u.slot + p
                    bank = PS[:, i, :]
                    after(dve, "pointwise", u, per=2, k=p + 1)
                    after(dve, "relu", u, back=2, per=2, k=p + 1)
                    dve.tensor_reduce(a["hp"][i][:, 0, :], bank[:, 0:S].rearrange("p (t two) -> p t two", two=2),
                                      AX.X, ALU.max)
                    dve.tensor_reduce(a["hp"][i][0:C1, 1, :],
                                      bank[0:C1, S:2 * S].rearrange("p (t two) -> p t two", two=2),
                                      AX.X, ALU.max).then_inc(s["pooled"], 1)

            def a_norm(u):
                for p in range(2):
                    i = 2 * u.slot + p
                    after(dve, "dft_t", u, per=2, k=p + 1, nop=True)
                    dve.bn_stats(a["st"][i][:, :], PS[:, 6 + p, 0:C]).then_inc(s["a_st"], 1)
                for p in range(2):
                    i = 2 * u.slot + p
                    after(dve, "a_st", u, per=2, k=p + 1, nop=True)
                    dve.bn_aggr(a["mv"][i][:, :], a["st"][i][:, :]).then_inc(s["a_mv"], 1)
                for p in range(2):
                    i = 2 * u.slot + p
                    after(dve, "a_rstd", u, per=2, k=p + 1)
                    after(dve, "h_A", u, back=2, per=2, k=p + 1)
                    dve.tensor_scalar(a["yn"][i][:, :], PS[:, 6 + p, 0:C], a["mv"][i][:, 0:1], a["rs"][i][:, 1:2],
                                      ALU.subtract, ALU.mult).then_inc(s["y_normed"], 1)

            pipelined(dve, B // 2, 2, 2, [(a_taps, 0), (a_pool, 1), (a_norm, 2)])
            phase_end(dve, "dve", 1)

            m_ = Bm

            def b_stats(u):
                i = u.slot
                dve.bn_stats(m_["st"][i][:, :], H[:, u.v, :]).then_inc(s["b_st"], 1)
                after(dve, "b_st", u, nop=True)
                dve.bn_aggr(m_["mv"][i][:, :], m_["st"][i][:, :]).then_inc(s["b_mv"], 1)

            def b_norm(u):
                i = u.slot
                after(dve, "b_rstd", u)
                after(dve, "b_turned", u, back=2)
                dve.tensor_scalar(m_["zn"][i][:, :], H[:, u.v, :], m_["mv"][i][:, 0:1], m_["rs"][i][:, 1:2],
                                  ALU.subtract, ALU.mult).then_inc(s["b_normed"], 1)

            def b_v(u):
                after(dve, "b_v_made", u)
                after(dve, "b_attended", u, back=2)
                tt(m_["v"][u.slot][:, :], PS[:, 2, 0:C], row("bv"), ALU.add).then_inc(s["b_v"], 1)

            def b_max(u):
                i = u.slot
                after(dve, "b_scored", u)
                dve.tensor_reduce(m_["nm"][i][:, 0:1], PS[:, 3, 0:T], AX.X, ALU.max).then_inc(s["b_rowmax"], 1)
                after(dve, "b_rowmax", u)
                dve.tensor_scalar(m_["nm"][i][:, 1:2], m_["nm"][i][:, 0:1], -(C ** -0.5), None, ALU.mult)\
                    .then_inc(s["b_max"], 1)

            def b_pT(u):
                after(dve, "b_p_turned", u)
                after(dve, "b_attended", u, back=2)
                dve.tensor_copy(m_["pT"][u.slot][:, :], PS[:, 4, 0:T]).then_inc(s["b_pT"], 1)
                dve.reciprocal(m_["sum"][u.slot][:, 1:2], m_["sum"][u.slot][:, 0:1]).then_inc(s["b_recip"], 1)

            def b_add(u):
                i = u.slot
                after(dve, "b_attended", u)
                after(dve, "b_recip", u)
                stt(H[:, u.v, :], PS[:, 5, 0:C], m_["sum"][i][:, 1:2], H[:, u.v, :], ALU.mult, ALU.add)\
                    .then_inc(s["b_added"], 1)

            pipelined(dve, B, 2, 2, [(b_stats, 0), (b_max, 2), (b_norm, 0), (b_v, 1), (b_pT, 2), (b_add, 2)])
            phase_end(dve, "dve", 2)

            c = Cm
            for i in range(2):
                dve.memset(c["v"][i][:, :, HD:32], 0.0).then_inc(s["c_zeros"], 1)
            dve.wait_ge(s["c_zeros"], 2)

            def c_stats(u):
                i = u.slot
                dve.bn_stats(c["st"][i][:, :], H[:, u.v, :]).then_inc(s["c_st"], 1)

            def c_aggr(u):
                i = u.slot
                after(dve, "c_st", u, nop=True)
                dve.bn_aggr(c["mv"][i][:, :], c["st"][i][:, :]).then_inc(s["c_mv"], 1)

            def c_norm_x(u):
                i = u.slot
                after(dve, "c_rstd", u)
                dve.tensor_scalar(X[:, u.v, :], H[:, u.v, :], c["mv"][i][:, 0:1], c["rs"][i][:, 1:2],
                                  ALU.subtract, ALU.mult).then_inc(s["c_x"], 1)

            def c_norm(u):
                i = u.slot
                after(dve, "c_x", u)
                after(dve, "c_turned", u, back=2)
                dve.tensor_scalar(c["zn"][i][:, :], X[:, u.v, :], c["rs"][i][:, 5:6], None, ALU.mult)\
                    .then_inc(s["c_normed"], 1)

            def c_q(u):
                after(dve, "c_q_made", u)
                after(dve, "c_scored", u, back=2)
                tt(c["qT"][u.slot][:, :, :], PS[:, 6, 0:3 * T].rearrange("p (g t) -> p g t", g=3),
                   cols[:, QB:QB + 3].rearrange("p (g one) -> p g one", one=1).to_broadcast([128, 3, T]), ALU.add)\
                    .then_inc(s["c_q"], 1)

            def c_pT2(u):
                after(dve, "c_p_turned", u, per=3)
                after(dve, "c_attended", u, back=1)
                dve.tensor_copy(c["PT"][:, 8:12, :], PS[:, 4, :].rearrange("p (h t) -> p h t", h=4))\
                    .then_inc(s["c_pT2"], 1)

            def c_k(u):
                after(dve, "c_k_made", u)
                after(dve, "c_scored", u, back=2)
                tt(c["kT"][u.slot][:, :, :], PS[:, 7, 0:3 * T].rearrange("p (g t) -> p g t", g=3),
                   cols[:, KB:KB + 3].rearrange("p (g one) -> p g one", one=1).to_broadcast([128, 3, T]), ALU.add)\
                    .then_inc(s["c_k"], 1)

            def c_v(u):
                after(dve, "c_v_made", u)
                after(dve, "c_attended", u, back=2)
                tt(c["v"][u.slot][:, :, 0:HD], PS[:, 5, 0:C].rearrange("p (h e) -> p h e", h=HEADS),
                   row("in_bv").rearrange("p (h e) -> p h e", h=HEADS), ALU.add).then_inc(s["c_v"], 1)

            def c_rowmax(u):
                after(dve, "c_scored", u)
                dve.tensor_reduce(c["mx"][u.slot][:, :].rearrange("p (j g) -> p j g", j=4),
                                  PS[:, 0:4, 0:3 * T].rearrange("p j (g t) -> p j g t", g=3), AX.X, ALU.max)\
                    .then_inc(s["c_rowmax"], 1)

            def c_max(u):
                after(dve, "c_rowmax", u)
                dve.tensor_scalar(c["nm"][u.slot][:, :], c["mx"][u.slot][:, :], -(HD ** -0.5), None, ALU.mult)\
                    .then_inc(s["c_max"], 1)

            def c_recip(u):
                after(dve, "c_exp", u)
                dve.reciprocal(c["rd"][u.slot][:, :], c["sum"][u.slot][:, :]).then_inc(s["c_recip"], 1)

            def c_scale(u):
                e = c["E"][u.slot][:, :, :]
                after(dve, "c_recip", u)
                tt(e, e, c["rd"][u.slot][:, :].rearrange("p (h one) -> p h one", one=1).to_broadcast([128, HEADS, T]),
                   ALU.mult).then_inc(s["c_scaled"], 1)

            def c_add(u):
                after(dve, "c_projected", u)
                after(dve, "c_xb", u)
                tt(X[:, u.v, :], PS[:, 6, 0:C], X[:, u.v, :], ALU.add).then_inc(s["c_added"], 1)

            pipelined(dve, B, 2, 3, [(c_norm_x, 1), (c_stats, 0), (c_norm, 1), (c_aggr, 0), (c_recip, 3), (c_scale, 3),
                                     (c_add, 5), (c_rowmax, 2), (c_max, 2), (c_q, 1), (c_pT2, 3), (c_k, 1), (c_v, 2)])
            phase_end(dve, "dve", 3)

            q = D

            def split_gelu(f):
                for m in range(HCH):
                    after(dve, "gelu", f, per=HCH, k=m + 1)
                    dve.tensor_copy(q["Gh"][:, m, :], q["G"][m % 2][:, :]).then_inc(s["gelu_hi"], 1)
                    after(dve, "gelu_hi", f, per=HCH, k=m + 1)
                    tt(q["Gl"][:, m, :], q["G"][m % 2][:, :], q["Gh"][:, m, :].bitcast(F32), ALU.subtract)\
                        .then_inc(s["gelu_split"], 1)

            def d_mlp(u):
                after(dve, "x_hi", u, per=2, k=1)
                tt(q["lA"][0][:, :], PS[:, 0, :], q["hA"][0][:, :].bitcast(F32), ALU.subtract)\
                    .then_inc(s["x_lo"], 1)
                after(dve, "x_hi", u, per=2, k=2)
                tt(q["sB"][0][64:128, :], PS[64:128, 1, :], q["sB"][0][64:128, :].bitcast(F32), ALU.subtract)\
                    .then_inc(s["x_split"], 1)
                split_gelu(u)
                for t in range(GB):
                    after(dve, "down", u, per=GB, k=t + 1)
                    after(dve, "xb_D", u, per=GB, k=t + 1)
                    tt(X[:, u.v * GB + t, :], PS[:, 4 + t, 0:C], X[:, u.v * GB + t, :], ALU.add)\
                        .then_inc(s["down_read"], 1)
                for t in range(GB):
                    after(dve, "down_read", u, per=GB, k=t + 1, nop=True)
                    dve.bn_stats(q["st"][:, t, :], X[:, u.v * GB + t, :]).then_inc(s["d_st"], 1)
                for t in range(GB):
                    after(dve, "d_st", u, per=GB, k=t + 1, nop=True)
                    dve.bn_aggr(q["mv"][:, t, :], q["st"][:, t, :]).then_inc(s["d_mv"], 1)
                after(dve, "d_rstd", u)
                for t in range(GB):
                    after(dve, "x_turned", u)
                    dve.tensor_scalar(q["xs"][t][:, 0:C], X[:, u.v * GB + t, :], q["mv"][:, t, 0:1],
                                      q["rs"][:, t, 1:2], ALU.subtract, ALU.mult).then_inc(s["xm"], 1)
                after(dve, "gated", u)
                tt(q["LG"][:, bass.ts(u.v, GB), :], PS[:, 0, 0:GB * NEXP].rearrange("p (t e) -> p t e", t=GB),
                   row("gate_b").rearrange("p (one e) -> p one e", one=1).to_broadcast([128, GB, NEXP]), ALU.add)\
                    .then_inc(s["gate_read"], 1)

            pipelined(dve, NG, 1, 2, [(d_mlp, 0)])

            n_link = [0]

            def link(ins):
                n_link[0] += 1
                ins.then_inc(s["gate_chain"], 1)
                dve.wait_ge(s["gate_chain"], n_link[0])

            LG, rank, cmp_, top, comb = q["LG"], q["rank"], q["cmp"], q["top"], q["comb"]
            dve.wait_ge(s["gate_read"], NG)
            for j in range(NEXP):
                lj = LG[:, :, j:j + 1].to_broadcast([128, B, NEXP])
                if j == 0:
                    link(tt(rank[:, :, :], lj, LG[:, :, :], ALU.is_gt))
                else:
                    link(tt(cmp_[:, :, :], lj, LG[:, :, :], ALU.is_gt))
                    link(tt(rank[:, :, :], rank[:, :, :], cmp_[:, :, :], ALU.add))
            for j in range(NEXP - 1):
                n = NEXP - 1 - j
                link(tt(cmp_[:, :, 0:n], LG[:, :, j:j + 1].to_broadcast([128, B, n]), LG[:, :, j + 1:NEXP], ALU.is_equal))
                link(tt(rank[:, :, j + 1:NEXP], rank[:, :, j + 1:NEXP], cmp_[:, :, 0:n], ALU.add))
            link(dve.tensor_reduce(top[:, :], LG[:, :, :], AX.X, ALU.max))
            tt(cmp_[:, :, :], LG[:, :, :], top[:, :].rearrange("p (b one) -> p b one", one=1).to_broadcast([128, B, NEXP]),
               ALU.subtract).then_inc(s["logit_sub"], 1)
            dve.wait_ge(s["gate_exp"], 1)
            link(stt(comb[:, :, :], rank[:, :, :], 2.0, comb[:, :, :], ALU.is_lt, ALU.mult))
            link(dve.tensor_reduce(top[:, :], comb[:, :, :], AX.X, ALU.add))
            link(dve.reciprocal(top[:, :], top[:, :]))
            tt(comb[:, :, :], comb[:, :, :], top[:, :].rearrange("p (b one) -> p b one", one=1).to_broadcast([128, B, NEXP]),
               ALU.mult).then_inc(s["comb"], 1)
            dve.wait_ge(s["comb"], 1)

            def d_split(u):
                i = u.slot
                hi0, hi1 = q["XF"][:, 0, u.v, :], q["XF"][:, 1, u.v, :]
                if u.lo == 0:
                    dve.wait_ge(s["xf_made"], 2 * NG)
                dve.tensor_copy(q["hA"][i][:, :], hi0).then_inc(s["xm_hi"], 1)
                dve.tensor_copy(q["sB"][i][:, :], hi1).then_inc(s["xm_hi"], 1)
                after(dve, "xm_hi", u, per=2, k=1)
                tt(q["lA"][i][:, :], hi0, q["hA"][i][:, :].bitcast(F32), ALU.subtract).then_inc(s["xm_lo"], 1)
                after(dve, "xm_hi", u, per=2, k=2)
                tt(q["sB"][i][64:128, :], hi1[64:128, :], q["sB"][i][64:128, :].bitcast(F32), ALU.subtract)\
                    .then_inc(s["xm_split"], 1)

            def d_experts(u):
                for e in range(NEXP):
                    f = Unit(u.v * NEXP + (NG + e), u.lo * NEXP + NG + e, 0)
                    split_gelu(f)
                    for t in range(GB):
                        after(dve, "down", f, per=GB, k=t + 1)
                        if e == 0:
                            after(dve, "acc0", u, per=GB, k=t + 1)
                        else:
                            after(dve, "down_read", f, back=1, per=GB, k=t + 1)
                        stt(q["acc"][t][:, :], PS[:, 4 + t, 0:C], comb[:, u.v * GB + t, e:e + 1], q["acc"][t][:, :],
                            ALU.mult, ALU.add).then_inc(s["down_read"], 1)

            pipelined(dve, NG, 2, 0, [(d_split, 0), (d_experts, 0)])
            phase_end(dve, "dve", 4)

            e_ = Em
            for n in "kvr":
                dve.tensor_scalar(e_["om"][n][:, :], cols[:, COL["mix_" + n]:COL["mix_" + n] + 2], -1.0, 1.0,
                                  ALU.mult, ALU.add).then_inc(s["e_consts"], 1)
            dve.memset(e_["zT"][:, :, 0:1], 0.0).then_inc(s["e_consts"], 1)
            for i in range(2):
                dve.memset(e_["K"][i][:, :, 0:1], FAR).then_inc(s["e_consts"], 1)
            for n in ("D1", "E2s", "EV"):
                dve.memset(e_[n][:, :, 0:1], 0.0).then_inc(s["e_consts"], 1)
            dve.wait_ge(s["e_consts"], 9)
            dve.wait_ge(s["e_decay"], 1)
            dve.memset(e_["WD"][:, :, :], 0.0).then_inc(s["e_wd"], 1)
            dve.tensor_scalar(e_["ndec"][:, :], e_["ndec"][:, :], -1.0, None, ALU.mult).then_inc(s["e_wd"], 1)
            dve.wait_ge(s["e_wd"], 2)
            for k, bl in enumerate((slice(0, GB), slice(GB, NB6))):
                dve.tensor_scalar(e_["WD"][:, bl, :], e_["WD"][:, bl, :], e_["ndec"][:, k:k + 1], None, ALU.add)\
                    .then_inc(s["e_wd"], 1)
            dve.wait_ge(s["e_wd"], 4)
            dve.memset(e_["WD"][:, :, 0:1], FAR).then_inc(s["e_wd"], 1)
            dve.wait_ge(s["e_wd"], 5)

            def e_norm(u):
                for t in range(GB):
                    dve.bn_stats(e_["st"][:, t, :], H[:, u.v * GB + t, :]).then_inc(s["e_st"], 1)
                for t in range(GB):
                    after(dve, "e_st", u, per=GB, k=t + 1, nop=True)
                    dve.bn_aggr(e_["mv"][:, t, :], e_["st"][:, t, :]).then_inc(s["e_mv"], 1)
                after(dve, "e_rstd", u)
                after(dve, "e_turned", u, back=1)
                for t in range(GB):
                    dve.tensor_scalar(e_["zn"][t][:, 0:C], H[:, u.v * GB + t, :], e_["mv"][:, t, 0:1],
                                      e_["rs"][:, t, 1:2], ALU.subtract, ALU.mult).then_inc(s["e_zn"], 1)

            def e_mix(u):
                for j, n in enumerate("kvr"):
                    after(dve, "e_mt", u, per=3, k=j + 1)
                    after(dve, "e_projected", u, back=1, per=3, k=j + 1)
                    for k, bl in enumerate((slice(0, GB), slice(GB, NB6))):
                        last = stt(e_["mx"][n][:, bl, :], e_["zT"][:, bl, 0:T], e_["om"][n][:, k:k + 1],
                                   e_["mt"][n][:, bl, :], ALU.mult, ALU.add)
                    last.then_inc(s["e_mixed"], 1)

            def flat(t):
                return t[:, :, :].rearrange("p b t -> p (b t)")

            def e_wkv(u):
                i = u.slot
                K, ku, v, er = e_["K"][i], e_["ku"][i], e_["v"][i], e_["er"][i]
                MX, D1, E2s, EV, NUM, DEN = (e_[n] for n in ("MX", "D1", "E2s", "EV", "NUM", "DEN"))
                prev, new = slice(0, T), slice(1, T + 1)
                after(dve, "e_read_k", u)
                dve.tensor_tensor_scan(flat(MX), flat(e_["WD"]), flat(K), FAR, ALU.add, ALU.max)\
                    .then_inc(s["e_mxscan"], 1)
                after(dve, "e_mxscan", u)
                tt(e_["mo"][:, :, :], ku[:, :, :], MX[:, :, prev], ALU.max).then_inc(s["e_mo"], 1)
                for k, bl in enumerate((slice(0, GB), slice(GB, NB6))):
                    last = stt(e_["c"][:, bl, :], MX[:, bl, prev], e_["ndec"][:, k:k + 1], MX[:, bl, new],
                               ALU.add, ALU.subtract)
                last.then_inc(s["e_arg_c"], 1)
                tt(e_["dd"][:, :, :], K[:, :, new], MX[:, :, new], ALU.subtract).then_inc(s["e_arg_dd"], 1)
                after(dve, "e_mo", u)
                tt(e_["a"][:, :, :], MX[:, :, prev], e_["mo"][:, :, :], ALU.subtract).then_inc(s["e_arg_a"], 1)
                tt(e_["b"][:, :, :], ku[:, :, :], e_["mo"][:, :, :], ALU.subtract).then_inc(s["e_arg_b"], 1)
                after(dve, "e_exp_dd", u)
                after(dve, "e_read_v", u)
                tt(EV[:, :, new], E2s[:, :, new], v[:, :, :], ALU.mult).then_inc(s["e_ev"], 1)
                after(dve, "e_exp_c", u)
                dve.tensor_tensor_scan(flat(DEN), flat(D1), flat(E2s), 0.0, ALU.mult, ALU.add)\
                    .then_inc(s["e_den"], 1)
                after(dve, "e_ev", u)
                dve.tensor_tensor_scan(flat(NUM), flat(D1), flat(EV), 0.0, ALU.mult, ALU.add)\
                    .then_inc(s["e_num"], 1)
                after(dve, "e_exp_b", u)
                after(dve, "e_exp_a", u)
                tt(e_["t2"][:, :, :], e_["e2"][:, :, :], v[:, :, :], ALU.mult).then_inc(s["e_t2"], 1)
                after(dve, "e_den", u)
                tt(e_["t3"][:, :, :], e_["e1"][:, :, :], DEN[:, :, prev], ALU.mult).then_inc(s["e_t3"], 1)
                after(dve, "e_num", u)
                tt(e_["t1"][:, :, :], e_["e1"][:, :, :], NUM[:, :, prev], ALU.mult).then_inc(s["e_t1"], 1)
                after(dve, "e_t3", u)
                tt(e_["t3"][:, :, :], e_["t3"][:, :, :], e_["e2"][:, :, :], ALU.add).then_inc(s["e_t3b"], 1)
                after(dve, "e_t1", u)
                after(dve, "e_t2", u)
                tt(e_["t1"][:, :, :], e_["t1"][:, :, :], e_["t2"][:, :, :], ALU.add).then_inc(s["e_t1b"], 1)
                after(dve, "e_t3b", u)
                after(dve, "e_read_r", u)
                stt(e_["t3"][:, :, :], er[:, :, :], 1.0, e_["t3"][:, :, :], ALU.add, ALU.mult)\
                    .then_inc(s["e_t3c"], 1)
                after(dve, "e_t3c", u)
                dve.reciprocal(e_["t3"][:, :, :], e_["t3"][:, :, :]).then_inc(s["e_t3d"], 1)
                after(dve, "e_t3d", u)
                after(dve, "e_t1b", u)
                after(dve, "e_out", u, back=2)
                tt(e_["rw"][i][:, :, :], e_["t1"][:, :, :], e_["t3"][:, :, :], ALU.mult).then_inc(s["e_rw"], 1)

            def e_add(u):
                after(dve, "e_out", u)
                for t in range(GB):
                    h = H[:, u.v * GB + t, :]
                    tt(h, PS[:, t // 2, (t % 2) * C:(t % 2) * C + C], h, ALU.add).then_inc(s["e_added"], 1)

            pipelined(dve, NG, 2, 2, [(e_norm, 0), (e_mix, 0), (e_wkv, 1), (e_add, 1)])
            dve.wait_ge(s["in_F"], 32)
            dve.wait_ge(s["pool_ones"], 1)
            dve.tensor_reduce(qs[:, 2:4], rawI[:, :, :], AX.X, ALU.add, apply_absolute_value=True)\
                .then_inc(s["f_prep"], 1)
            dve.tensor_reduce(qs[:, 1:2], rawO[:, :, :], AX.XY, ALU.add, apply_absolute_value=True)\
                .then_inc(s["f_prep"], 1)
            dve.wait_ge(s["f_prep"], 2)
            stt(qs[:, 0:1], qs[:, 3:4], 0.5, qs[:, 2:3], ALU.mult, ALU.add).then_inc(s["f_wsum"], 1)
            dve.wait_ge(s["f_wmean"], 1)
            dve.tensor_scalar(qs[:, 4:5], PS[:, 7, 256:257], 1.0 / (2 * BH * C), EPS_Q, ALU.mult, ALU.max)\
                .then_inc(s["f_prep"], 1)
            dve.tensor_scalar(qs[:, 5:6], PS[:, 7, 257:258], 1.0 / (BH * C), EPS_Q, ALU.mult, ALU.max)\
                .then_inc(s["f_prep"], 1)
            dve.wait_ge(s["f_prep"], 4)
            dve.reciprocal(qs[:, 6:8], qs[:, 4:6]).then_inc(s["f_prep"], 1)
            dve.wait_ge(s["f_prep"], 5)
            for j, (raw, w) in enumerate(((rawI, wI), (rawO, wO))):
                dve.tensor_scalar(raw[:, :, :], raw[:, :, :], qs[:, 6 + j:7 + j], MAGIC, ALU.mult, ALU.add)\
                    .then_inc(s["f_prep"], 1)
            for j, (raw, w) in enumerate(((rawI, wI), (rawO, wO))):
                dve.wait_ge(s["f_prep"], 6 + j)
                dve.tensor_scalar(raw[:, :, :], raw[:, :, :], MAGIC, 1.0, ALU.subtract, ALU.min)\
                    .then_inc(s["f_prep2"], 1)
            for j, (raw, w) in enumerate(((rawI, wI), (rawO, wO))):
                dve.wait_ge(s["f_prep2"], 1 + j)
                dve.tensor_scalar(w[:, :, :], raw[:, :, :], -1.0, None, ALU.max)
            phase_end(dve, "dve", 5)

            f_ = Fm

            def f_stats(u):
                i = u.slot
                dve.bn_stats(f_["st"][i][:, :], H[:, u.v, :]).then_inc(s["f_st"], 1)

            def f_aggr(u):
                i = u.slot
                after(dve, "f_st", u)
                after(dve, "f_c", u, back=2, nop=True)
                dve.bn_aggr(f_["mv"][i][:, :], f_["st"][i][:, :]).then_inc(s["f_mv"], 1)

            def f_norm(u):
                i = u.slot
                after(dve, "f_rstd", u)
                dve.tensor_scalar(f_["xn"][i][:, :], H[:, u.v, :], f_["mv"][i][:, 0:1], f_["rs"][i][:, 2:3],
                                  ALU.subtract, ALU.mult).then_inc(s["f_xn"], 1)

            def f_gain(u):
                i = u.slot
                after(dve, "f_xn", u)
                after(dve, "f_q", u, back=2)
                tt(f_["xg"][i][:, :], f_["xn"][i][:, :], row("g_in"), ALU.mult).then_inc(s["f_xg"], 1)

            def f_amax(u):
                i = u.slot
                after(dve, "f_xg", u)
                dve.tensor_reduce(f_["rs"][i][:, 3:4], f_["xg"][i][:, :], AX.X, ALU.max, apply_absolute_value=True)\
                    .then_inc(s["f_amax"], 1)

            def f_step(u):
                rs = f_["rs"][u.slot]
                after(dve, "f_amax", u)
                dve.tensor_scalar(rs[:, 4:5], rs[:, 3:4], EPS_Q, 1.0 / 127.0, ALU.max, ALU.mult)\
                    .then_inc(s["f_step"], 1)

            def f_scale(u):
                rs = f_["rs"][u.slot]
                after(dve, "f_step", u)
                dve.reciprocal(rs[:, 5:6], rs[:, 4:5]).then_inc(s["f_scale"], 1)
                dve.tensor_scalar(rs[:, 6:7], rs[:, 4:5], qs[:, 4:5], None, ALU.mult).then_inc(s["f_c"], 1)

            def f_round(u):
                i = u.slot
                after(dve, "f_scale", u)
                dve.tensor_scalar(f_["xn"][i][:, :], f_["xg"][i][:, :], f_["rs"][i][:, 5:6], MAGIC,
                                  ALU.mult, ALU.add).then_inc(s["f_round"], 1)

            def f_clip(u):
                i = u.slot
                after(dve, "f_round", u)
                dve.tensor_scalar(f_["xg"][i][:, :], f_["xn"][i][:, :], MAGIC + 127.0, MAGIC - 128.0,
                                  ALU.min, ALU.max).then_inc(s["f_clip"], 1)

            def f_gate(u):
                i = u.slot
                rs = f_["rs"][i]
                after(dve, "f_silu", u)
                stt(f_["y"][i][:, :], PS[:, 1 + 2 * i, :], rs[:, 6:7], f_["sg"][i][:, :], ALU.mult, ALU.mult)\
                    .then_inc(s["f_y"], 1)

            def f_amax2(u):
                i = u.slot
                after(dve, "f_yg", u)
                dve.tensor_reduce(f_["rs"][i][:, 8:9], f_["yg"][i][:, :], AX.X, ALU.max, apply_absolute_value=True)\
                    .then_inc(s["f_amax2"], 1)

            def f_norm_max(u):
                rs = f_["rs"][u.slot]
                after(dve, "f_rms", u)
                after(dve, "f_amax2", u)
                dve.tensor_scalar(rs[:, 9:10], rs[:, 8:9], rs[:, 7:8], EPS_Q, ALU.mult, ALU.max)\
                    .then_inc(s["f_amax3"], 1)

            def f_inv(u):
                rs = f_["rs"][u.slot]
                after(dve, "f_amax3", u)
                dve.reciprocal(rs[:, 10:11], rs[:, 9:10]).then_inc(s["f_inv"], 1)
                dve.tensor_scalar(rs[:, 11:12], rs[:, 9:10], qs[:, 5:6], 1.0 / 127.0, ALU.mult, ALU.mult)\
                    .then_inc(s["f_c2"], 1)

            def f_scale2(u):
                rs = f_["rs"][u.slot]
                after(dve, "f_inv", u)
                dve.tensor_scalar(rs[:, 10:11], rs[:, 10:11], rs[:, 7:8], 127.0, ALU.mult, ALU.mult)\
                    .then_inc(s["f_scale2"], 1)

            def f_round2(u):
                i = u.slot
                after(dve, "f_scale2", u)
                dve.tensor_scalar(f_["yg"][i][:, :], f_["yg"][i][:, :], f_["rs"][i][:, 10:11], MAGIC,
                                  ALU.mult, ALU.add).then_inc(s["f_round2"], 1)

            def f_clip2(u):
                i = u.slot
                after(dve, "f_round2", u)
                dve.tensor_scalar(f_["yg"][i][:, :], f_["yg"][i][:, :], MAGIC + 127.0, MAGIC - 128.0,
                                  ALU.min, ALU.max).then_inc(s["f_clip2"], 1)

            def f_add(u):
                i = u.slot
                after(dve, "f_down", u)
                after(dve, "f_c2", u)
                stt(f_["o"][:, u.v, :], PS[:, 6, 0:C], f_["rs"][i][:, 11:12], H[:, u.v, :], ALU.mult, ALU.add)\
                    .then_inc(s["o_ready"], 1)

            pipelined(dve, B, 2, 2, [(f_norm, 1), (f_stats, 0), (f_gain, 1), (f_aggr, 0), (f_amax, 1), (f_amax2, 3),
                                    (f_step, 1), (f_norm_max, 3), (f_scale, 1), (f_inv, 3), (f_round, 1),
                                    (f_scale2, 3), (f_clip, 1), (f_round2, 3), (f_add, 4), (f_clip2, 3), (f_gate, 2)])

        @block.gpsimd
        def _(pool):
            def rsqrt(dst, tmp, src, eps, sem, u, per=1, k=None):
                pool.tensor_scalar(tmp, src, eps, None, ALU.add).then_inc(s[sem + "_a"], 1)
                after(pool, sem + "_a", u, per=per, k=k)
                return pool.tensor_tensor(dst, tmp, expo[:, 0:1], ALU.pow)

            pool.memset(expo[:, :], -0.5).then_inc(s["expo"], 1)
            pool.memset(magic[:, :], -MAGIC).then_inc(s["expo"], 1)
            pool.wait_ge(s["expo"], 2)
            pool.wait_ge(s["in_A"], 16 * 5)
            pool.tensor_copy(identb[:, :], ident[:, :])

            def w_low(u):
                after(pool, "w_hi", u)
                pool.tensor_tensor(WL[:, bass.ts(u.v, PIECE)], raw[u.slot][:, :],
                                   WH[:, bass.ts(u.v, PIECE)].bitcast(F32), ALU.subtract).then_inc(s["w_lo"], 1)

            a = A

            def a_rstd(u):
                for p in range(2):
                    i = 2 * u.slot + p
                    after(pool, "a_mv", u, per=2, k=p + 1, nop=True)
                    rsqrt(a["rs"][i][:, 1:2], a["rs"][i][:, 0:1], a["mv"][i][:, 1:2], EPS, "a_rs", u, 2, p + 1)\
                        .then_inc(s["a_rstd"], 1)

            def a_affine(u):
                for p in range(2):
                    i = 2 * u.slot + p
                    h = H[:, u.v + p * (B // 2), :]
                    after(pool, "y_normed", u, per=2, k=p + 1)
                    pool.tensor_tensor(a["yn"][i][:, :], a["yn"][i][:, :], row("gamma"), ALU.mult)\
                        .then_inc(s["a_gamma"], 1)
                    after(pool, "a_gamma", u, per=2, k=p + 1)
                    pool.tensor_tensor(h, a["yn"][i][:, :], row("beta"), ALU.add).then_inc(s["h_A"], 1)

            pipelined(pool, B // 2, 2, 2, [(a_rstd, 2), (a_affine, 2)])
            phase_end(pool, "pool", 1)
            m_ = Bm

            def b_rstd(u):
                i = u.slot
                after(pool, "b_mv", u, nop=True)
                rsqrt(m_["rs"][i][:, 1:2], m_["rs"][i][:, 0:1], m_["mv"][i][:, 1:2], EPS, "b_rs", u)\
                    .then_inc(s["b_rstd"], 1)

            pipelined(pool, B, 2, 2, [(b_rstd, 0), (w_low, 0)])
            phase_end(pool, "pool", 2)
            c = Cm

            def c_rstd(u):
                i = u.slot
                rs, var = c["rs"][i], c["mv"][i][:, 1:2]
                after(pool, "c_mv", u)
                after(pool, "c_normed", u, back=2, nop=True)
                rsqrt(rs[:, 1:2], rs[:, 0:1], var, EPS, "c_rs", u).then_inc(s["c_rstd1"], 1)
                after(pool, "c_rstd1", u)
                pool.nop(nofuse=True)
                pool.tensor_scalar(rs[:, 3:4], rs[:, 1:2], rs[:, 1:2], var, ALU.mult, ALU.mult)\
                    .then_inc(s["c_var2"], 1)
                after(pool, "c_var2", u, nop=True)
                rsqrt(rs[:, 5:6], rs[:, 4:5], rs[:, 3:4], EPS, "c_rs2", u).then_inc(s["c_rstd"], 1)

            def c_xb(u):
                after(pool, "c_normed", u)
                pool.tensor_tensor(X[:, u.v, :], X[:, u.v, :], row("out_b"), ALU.add).then_inc(s["c_xb"], 1)

            pipelined(pool, B, 2, 3, [(c_rstd, 0), (c_xb, 1), (lambda u: w_low(shifted(u)), 0)])
            phase_end(pool, "pool", 3)
            q = D

            def d_copy(u):
                for t in range(GB):
                    x = X[:, u.v * GB + t, :]
                    after(pool, "xm_turned", u, back=1, nop=True)
                    pool.tensor_copy(q["xs"][t][:, 0:C], x).then_inc(s["x_copied1"], 1)
                    pool.tensor_copy(q["xs"][t][:, C:256], X[:, u.v * GB + t, 128:C]).then_inc(s["x_copied"], 1)
                for t in range(GB):
                    x = X[:, u.v * GB + t, :]
                    after(pool, "x_copied", u, per=GB, k=t + 1, nop=True)
                    pool.tensor_tensor(x, x, row("mlp_b2"), ALU.add).then_inc(s["xb_D"], 1)
                for t in range(GB):
                    after(pool, "d_mv", u, per=GB, k=t + 1, nop=True)
                    last = rsqrt(q["rs"][:, t, 1:2], q["rs"][:, t, 0:1], q["mv"][:, t, 1:2], EPS, "d_rs", u, GB, t + 1)
                last.then_inc(s["d_rstd"], 1)
                for t in range(GB):
                    after(pool, "xm", u, per=GB, k=t + 1, nop=True)
                    pool.tensor_copy(q["xs"][t][:, C:256], q["xs"][t][:, 128:C]).then_inc(s["xm_copied"], 1)

            pipelined(pool, NG, 1, 2, [(d_copy, 0)])
            pool.wait_ge(s["comb"], 1)

            def d_start(u):
                for t in range(GB):
                    g = u.v * GB + t
                    acc = q["acc"][t][:, :]
                    after(pool, "h_D", u, back=1, per=2 * GB)
                    for e in range(NEXP):
                        b2 = rows[:, ROW["exp_b2"][0] + e * C:ROW["exp_b2"][0] + (e + 1) * C]
                        if e == 0:
                            pool.tensor_scalar(acc, b2, q["comb"][:, g, 0:1], None, ALU.mult)\
                                .then_inc(s["acc_chain"], 1)
                        else:
                            tmp = q["tmp"][0][:, :]
                            pool.tensor_scalar(tmp, b2, q["comb"][:, g, e:e + 1], None, ALU.mult)\
                                .then_inc(s["acc_chain"], 1)
                            after(pool, "acc_chain", u, per=GB * 7, k=t * 7 + 2 * e)
                            add = pool.tensor_tensor(acc, acc, tmp, ALU.add).then_inc(s["acc_chain"], 1)
                            after(pool, "acc_chain", u, per=GB * 7, k=t * 7 + 2 * e + 1)
                    pool.tensor_tensor(H[:, g, :], H[:, g, :], X[:, g, :], ALU.add).then_inc(s["acc0"], 1)

            def d_finish(u):
                for t in range(GB):
                    g = u.v * GB + t
                    f = Unit(u.v * NEXP + (NG + NEXP - 1), u.lo * NEXP + NG + NEXP - 1, 0)
                    after(pool, "down_read", f, per=GB, k=t + 1)
                    pool.tensor_tensor(H[:, g, :], H[:, g, :], q["acc"][t][:, :], ALU.add).then_inc(s["h_D"], 2)

            pipelined(pool, NG, 2, 2, [(d_start, 0), (d_finish, 0)])
            phase_end(pool, "pool", 4)
            e_ = Em
            pool.memset(ones[:, :], 1.0).then_inc(s["pool_ones"], 1)

            def e_rstd(u):
                for t in range(GB):
                    after(pool, "e_mv", u, per=GB, k=t + 1, nop=True)
                    last = rsqrt(e_["rs"][:, t, 1:2], e_["rs"][:, t, 0:1], e_["mv"][:, t, 1:2], EPS, "e_rs", u,
                                 GB, t + 1)
                last.then_inc(s["e_rstd"], 1)
                for t in range(GB):
                    after(pool, "e_zn", u, per=GB, k=t + 1, nop=True)
                    pool.tensor_copy(e_["zn"][t][:, C:256], e_["zn"][t][:, 128:C]).then_inc(s["e_normed"], 1)

            pipelined(pool, NG, 2, 2, [(e_rstd, 0)])
            phase_end(pool, "pool", 5)
            f_ = Fm

            def f_rstd(u):
                i = u.slot
                rs, var = f_["rs"][i], f_["mv"][i][:, 1:2]
                after(pool, "f_mv", u)
                after(pool, "f_round", u, back=2, nop=True)
                rsqrt(rs[:, 1:2], rs[:, 0:1], var, EPS, "f_rs", u).then_inc(s["f_rstd1"], 1)
                after(pool, "f_rstd1", u)
                pool.nop(nofuse=True)
                pool.tensor_scalar(rs[:, 3:4], rs[:, 1:2], rs[:, 1:2], var, ALU.mult, ALU.mult).then_inc(s["f_ms"], 1)
                after(pool, "f_ms", u, nop=True)
                rsqrt(rs[:, 5:6], rs[:, 4:5], rs[:, 3:4], EPS_RMS, "f_rs2", u).then_inc(s["f_rstd2"], 1)
                after(pool, "f_rstd2", u)
                pool.tensor_tensor(rs[:, 2:3], rs[:, 5:6], rs[:, 1:2], ALU.mult).then_inc(s["f_rstd"], 1)

            def f_rms(u):
                i = u.slot
                rs = f_["rs"][i]
                after(pool, "f_y", u)
                after(pool, "f_q2", u, back=2)
                pool.tensor_tensor(f_["yg"][i][:, :], f_["y"][i][:, :], row("g_out"), ALU.mult)\
                    .then_inc(s["f_yg"], 1)
                after(pool, "f_sq", u, nop=True)
                pool.tensor_scalar(rs[:, 7:8], rs[:, 7:8], 1.0 / BH, EPS_RMS, ALU.mult, ALU.add)\
                    .then_inc(s["f_ms2"], 1)
                after(pool, "f_ms2", u)
                pool.tensor_tensor(rs[:, 7:8], rs[:, 7:8], expo[:, 0:1], ALU.pow).then_inc(s["f_rms"], 1)

            pipelined(pool, B, 2, 2, [(f_rms, 3), (f_rstd, 0)])


def _chunk(wT):
    return np.ascontiguousarray(np.stack([wT[:128], np.concatenate([wT[128:], wT[128:]])], axis=1))


def _vec(v):
    return np.stack([v[:128], np.concatenate([v[128:], v[128:]])], axis=1)


def _headpad(w):
    out = np.zeros((3, 4, 32) + w.shape[1:], w.dtype)
    out[:, :, :HD] = w.reshape(3, 4, HD, *w.shape[1:])
    return out.reshape(384, *w.shape[1:])


def kernel(**inputs):
    import concourse.bacc as _bacc
    from concourse import mybir as _mybir
    from concourse.bass_utils import run_bass_kernel_spmd as _run

    i = {k: np.asarray(v) for k, v in inputs.items()}
    a = {}
    xT = np.pad(i["x"].transpose(2, 0, 1), ((0, 0), (0, 0), (TAPS // 2, TAPS // 2)))
    pair = xT.reshape(C, 2, B // 2, S + TAPS - 1).transpose(0, 2, 1, 3)
    x0 = pair[:128]
    x1 = pair[128:].transpose(2, 0, 1, 3).reshape(128, B // 2, S + TAPS - 1)
    a["x0a"], a["x0b"], a["x1a"], a["x1b"] = x0[:, :2], x0[:, 2:], x1[:, :2], x1[:, 2:]
    a["wpw"] = _chunk(i["L0_tok_w_pw"][:, :, 0].T)
    f32 = np.float32
    ang_c = 2 * np.pi * (np.outer(np.arange(C), np.arange(C)) % C) / C
    ang_t = 2 * np.pi * (np.outer(np.arange(T), np.arange(T)) % T) / T
    a["fd"] = _chunk(np.concatenate([np.cos(ang_c), -np.sin(ang_c)], axis=1).astype(f32))
    a["fs"] = np.stack([np.cos(ang_t), np.sin(ang_t)], axis=1).astype(f32)
    a["ident"] = np.eye(128, dtype=f32)
    a["wq"], a["wk"], a["wv"] = (_chunk(i[f"L0_attn_W{n}"].T) for n in "qkv")
    inw, inb = i["L0_ffn_in_w"], i["L0_ffn_in_b"]
    a["wqC"], a["wkC"] = _chunk(_headpad(inw[:C]).T), _chunk(_headpad(inw[C:2 * C]).T)
    a["wvC"] = _chunk(inw[2 * C:].T)
    a["woC"] = _headpad(i["L0_ffn_out_w"].T).reshape(3, 128, C).transpose(1, 0, 2)
    ups = [i["L0_ffn_mlp_w1"]] + list(i["L0_ffn_exp_w1"])
    dns = [i["L0_ffn_mlp_w2"]] + list(i["L0_ffn_exp_w2"])
    a["w_ffn"] = np.concatenate([p for f in range(NEXP + 1) for p in (
        _chunk(ups[f]).reshape(128, -1), dns[f].reshape(HCH, 128, C).transpose(1, 0, 2).reshape(128, -1))], axis=1)
    a["wg"] = _chunk(i["L0_ffn_gate_w"].T)
    for n in "kvro":
        a[f"w{n}E"] = _chunk(i[f"L1_attn_W{n}"].T)
    a["w_in"] = _chunk(i["L1_ffn_w_in"].T)
    a["w_out"] = i["L1_ffn_w_out"].T.reshape(BH // 128, 128, C).transpose(1, 0, 2)
    vec = {"b_dw": "L0_tok_b_dw", "b_pw": "L0_tok_b_pw", "bq": "L0_attn_bq", "bk": "L0_attn_bk",
           "ln1_g": "L0_ffn_ln1_g", "ln1_b": "L0_ffn_ln1_b", "ln2_g": "L0_ffn_ln2_g", "ln2_b": "L0_ffn_ln2_b",
           "decay": "L1_attn_time_decay", "first": "L1_attn_time_first", "mix_k": "L1_attn_mix_k",
           "mix_v": "L1_attn_mix_v", "mix_r": "L1_attn_mix_r"}
    parts = [_vec(i[vec[n]]) for n in COLS]
    parts += [_headpad(inb[:C]).reshape(3, 128).T, _headpad(inb[C:2 * C]).reshape(3, 128).T]
    taps = _chunk(i["L0_tok_w_dw"][:, 0, :])
    parts += [taps[:, 0], taps[:, 1]]
    parts += [i["L0_ffn_mlp_b1"].reshape(HCH, 128).T] + [b.reshape(HCH, 128).T for b in i["L0_ffn_exp_b1"]]
    a["cols"] = np.concatenate(parts, axis=1)
    assert a["cols"].shape == (128, NCOL)
    rowv = {"gamma": i["L0_tok_gamma"], "beta": i["L0_tok_beta"], "bv": i["L0_attn_bv"], "in_bv": inb[2 * C:],
            "out_b": i["L0_ffn_out_b"], "mlp_b2": i["L0_ffn_mlp_b2"], "exp_b2": i["L0_ffn_exp_b2"].reshape(-1),
            "g_in": i["L1_ffn_g_in"], "gate_b": i["L0_ffn_gate_b"], "g_out": i["L1_ffn_g_out"]}
    a["rows"] = np.broadcast_to(np.concatenate([rowv[n] for n, _ in ROWS]), (128, NROW))

    nc = _bacc.Bacc("TRN2", target_bir_lowering=False, num_devices=1)
    arrays, aps = {}, {}
    for name, v in a.items():
        v = np.ascontiguousarray(v)
        arrays["in_" + name] = v
        aps[name] = nc.dram_tensor("in_" + name, v.shape, _mybir.dt.from_np(v.dtype), kind="ExternalInput").ap()
    o = nc.dram_tensor("out_0", (B, T, C), _mybir.dt.float32, kind="ExternalOutput").ap()
    audio_tower(nc, aps, o)
    r = _run(nc, [arrays], core_ids=[0])
    return r.results[0]["out_0"]
```

```python
from contextlib import ExitStack

import numpy as np
import concourse.bass as bass
from concourse import mybir

ALU = mybir.AluOpType
ACT = mybir.ActivationFunctionType
AX = mybir.AxisListType
F32 = mybir.dt.float32
F32R = mybir.dt.float32r
BF16 = mybir.dt.bfloat16

B, S, C = 16, 256, 192
T = S // 2
C1 = C - 128
TAPS = 7
HEADS, HD = 12, 16
HID, HCH = 768, 6
NEXP = 4
BH = 512
GB = 4
NG = B // GB
EPS = 1e-5
EPS_RMS = 1e-6
EPS_Q = 1e-5
MAGIC = 12582912.0
FAR = -1e38
WEACH = 2 * HID + HCH * C
PIECE = (NEXP + 1) * WEACH // (2 * B)

COLS = ["b_dw", "b_pw", "bq", "bk", "ln1_g", "ln1_b", "ln2_g", "ln2_b", "decay", "first", "mix_k", "mix_v", "mix_r"]
COL = {n: 2 * i for i, n in enumerate(COLS)}
QB = 2 * len(COLS)
KB = QB + 3
TAP = KB + 3
HB = TAP + 2 * TAPS
NCOL = HB + HCH * (NEXP + 1)
ROWS = [("gamma", C), ("beta", C), ("bv", C), ("in_bv", C), ("out_b", C), ("mlp_b2", C), ("exp_b2", NEXP * C),
        ("g_in", C), ("gate_b", NEXP), ("g_out", BH)]
ROW = {}
NROW = 0
for _n, _w in ROWS:
    ROW[_n] = (NROW, NROW + _w)
    NROW += _w


RETIRED = ["b_" + n for n in ("st mv rs_a rstd normed turned zT qk_made qk v_made v scored rowmax max exp p_turned pT "
                              "recip attended added").split()] + \
          ["c_" + n for n in ("st mv rs_a rstd1 var2 rs2_a rstd x normed xb turned zT q_made q k_made k v_made v "
                              "scored rowmax max exp recip scaled attended cT projected added").split()]


PLAIN = ("f_weights", "e_consts", "e_decay", "e_wd", "f_prep", "f_prep2", "f_wsum", "f_wmean")


class Unit:

    def __init__(self, v, lo, slot):
        self.v, self.lo, self.slot = v, lo, slot


def pipelined(eng, n, unroll, ahead, stages):
    lag_max = max(k for _, k in stages)
    first = -(-(lag_max + ahead) // unroll) * unroll
    rounds = max(0, (n - first) // unroll)

    def step(t, lo, j, hi):
        for fn, lag in stages:
            if lo - lag >= 0 and hi - lag < n:
                fn(Unit(t - lag if lag else t, lo - lag, (j - lag) % unroll))

    if rounds < 2:
        for t in range(n + lag_max):
            step(t, t, t, t)
        return
    for t in range(first):
        step(t, t, t, t)
    with eng.Fori(0, rounds) as i:
        for j in range(unroll):
            step(i * unroll + (first + j), first + j, j, n - 1)
    for t in range(first + rounds * unroll, n + lag_max):
        step(t, t, t, t)


def audio_tower(nc, d, out):
    with ExitStack() as ctx:
        scope = [ctx]

        def sb(name, shape, dt=F32):
            return scope[-1].enter_context(nc.sbuf_tensor(name, shape, dt))

        start = {}
        retired = list(RETIRED)

        class Sems(dict):
            def __missing__(self, name):
                if name[:2] in ("e_", "f_") and name not in PLAIN and retired:
                    self[name] = self[retired.pop(0)]
                    start[name] = B
                else:
                    self[name] = ctx.enter_context(nc.semaphore(name))
                return self[name]

        s = Sems()

        def after(eng, name, u, back=0, per=1, k=None, nop=False):
            k = per if k is None else k
            if u.lo - back < 0:
                assert isinstance(u.v, int)
                return
            sem = s[name]
            eng.wait_ge(sem, u.v * per + (k - back * per + start.get(name, 0)))
            if nop:
                eng.nop(nofuse=True)

        PS = ctx.enter_context(nc.psum_tensor("PS", [128, 8, 512], F32))

        H = sb("H", [128, B, C])
        cols = sb("cols", [128, NCOL])
        rows = sb("rows", [128, NROW])
        ident = sb("ident", [128, 128])
        identb = sb("identb", [128, 128], BF16)
        expo = sb("expo", [128, 2])
        magic = sb("magic", [128, 2])

        def col(name, c, n=128):
            return cols[0:n, COL[name] + c:COL[name] + c + 1]

        def row(name):
            return rows[:, ROW[name][0]:ROW[name][1]]

        turning = dict(xs=[sb(f"xs{t}", [128, 256]) for t in range(GB)],
                       st=sb("st_group", [128, GB, 6]), mv=sb("mv_group", [128, GB, 2]), rs=sb("rs_group", [128, GB, 2]))
        mem_w = ExitStack()
        scope.append(mem_w)
        NF = NEXP + 1
        WW = sb("WW", [128, 2, NF * WEACH], F32R)

        def w_up(f, part):
            return WW[:, part, f * WEACH:f * WEACH + 2 * HID].rearrange("p (k n) -> p k n", k=2)

        def w_down(f):
            return WW[:, :, f * WEACH + 2 * HID:(f + 1) * WEACH].rearrange("p part (m n) -> p part m n", m=HCH)

        X = sb("X", [128, B, C])

        mem_abc = ExitStack()
        scope.append(mem_abc)
        raw = [sb(f"raw{i}", [128, PIECE]) for i in range(2)]

        def normed_rows(phase, n_rs):
            return {n: [sb(f"{n}{phase}{i}", sh) for i in range(2)] for n, sh in (
                ("st", [128, 6]), ("mv", [128, 2]), ("rs", [128, n_rs]), ("zn", [128, C]))}

        Bm = dict(wq=sb("wq", [128, 2, C]), wk=sb("wk", [128, 2, C]), wv=sb("wv", [128, 2, C]), **normed_rows("B", 2))
        mem = ExitStack()
        scope.append(mem)
        x0 = sb("x0", [128, B // 2, 2, S + TAPS - 1])
        x1 = sb("x1", [128, B // 2, S + TAPS - 1])
        wpw = sb("wpw", [128, 2, C])
        fd = sb("fd", [128, 2, 2 * C])
        fs = sb("fs", [128, 2, T])
        cv0 = [sb(f"cv0{i}", [128, 2, S]) for i in range(2)]
        cv1 = [sb(f"cv1{i}", [128, S]) for i in range(2)]
        lt0 = sb("lt0", [128, 2, S])
        lt1 = sb("lt1", [128, S])
        hp = [sb(f"hp{i}", [128, 2, T]) for i in range(4)]
        hT = [sb(f"hT{i}", [128, 2, T]) for i in range(4)]
        Z = [sb(f"Z{i}", [128, 2 * C]) for i in range(2)]
        yn = [sb(f"yn{i}", [128, C]) for i in range(4)]
        st = [sb(f"stA{i}", [128, 6]) for i in range(4)]
        mv = [sb(f"mvA{i}", [128, 2]) for i in range(4)]
        rs = [sb(f"rsA{i}", [128, 2]) for i in range(4)]
        A = dict(lt0=lt0, lt1=lt1, x0=x0, x1=x1, wpw=wpw, fd=fd, fs=fs, cv0=cv0, cv1=cv1, hp=hp, hT=hT, Z=Z, yn=yn, st=st, mv=mv, rs=rs)
        scope.pop().close()

        Cm = dict(wq=sb("wqC", [128, 2, 384]), wk=sb("wkC", [128, 2, 384]), wv=sb("wvC", [128, 2, C]),
                  wo=sb("woC", [128, 3, C]), **normed_rows("C", 6))
        mem = ExitStack()
        scope.append(mem)
        Bm.update({n: [sb(f"{n}B{i}", sh) for i in range(2)] for n, sh in (
                      ("zT", [128, 2, T]),
                      ("qT", [128, 2, T]), ("kT", [128, 2, T]), ("v", [128, C]), ("p", [128, T]), ("pT", [128, T]),
                      ("nm", [128, 2]), ("sum", [128, 2]))})
        scope.pop().close()

        mem = ExitStack()
        scope.append(mem)
        Cm.update(E=[sb(f"E{i}", [128, HEADS, T]) for i in range(2)], PT=sb("PT", [128, HEADS, T]),
                  **{n: [sb(f"{n}C{i}", sh) for i in range(2)] for n, sh in (
                      ("zT", [128, 2, T]),
                      ("qT", [128, 3, T]), ("kT", [128, 3, T]), ("v", [128, HEADS, 32]), ("mx", [128, HEADS]),
                      ("nm", [128, HEADS]), ("sum", [128, HEADS]), ("rd", [128, HEADS]), ("cT", [128, 3, T]))})
        scope.pop().close()
        scope.pop().close()

        mem = ExitStack()
        scope.append(mem)
        wg = sb("wg", [128, 2, NEXP])
        D = dict(
            **turning,
            XH=sb("XH", [128, NG, GB * T], F32R), XL=sb("XL", [128, NG, GB * T], F32R),
            XS=sb("XS", [128, NG, GB * T], F32R),
            XM=[sb(f"XM{k}", [128, GB * T]) for k in range(2)],
            G=[sb(f"G{i}", [128, GB * T]) for i in range(3)],
            Gh=sb("Gh", [128, HCH, GB * T], F32R), Gl=sb("Gl", [128, HCH, GB * T], F32R),
            LG=sb("LG", [128, B, NEXP]), rank=sb("rank", [128, B, NEXP]), cmp=sb("cmp", [128, B, NEXP]),
            top=sb("top", [128, B]), comb=sb("comb", [128, B, NEXP]))
        scope.pop().close()
        scope.pop().close()

        mem_ef = ExitStack()
        scope.append(mem_ef)
        rawI = sb("rawI", [128, 2, 2 * BH])
        rawO = sb("rawO", [128, BH // 128, C])
        wI = sb("wI", [128, 2, 2 * BH], BF16)
        wO = sb("wO", [128, BH // 128, C], BF16)
        qs = sb("qs", [128, 8])
        ones = sb("ones", [128, 128])
        mem = ExitStack()
        scope.append(mem)
        NB6 = GB + GB // 2
        Em = dict(
            w={n: sb(f"w{n}E", [128, 2, C]) for n in "kvro"},
            om={n: sb(f"om{n}", [128, 2]) for n in "kvr"}, ndec=sb("ndec", [128, 2]),
            WD=sb("WD", [128, NB6, T + 1]),
            zn=turning["xs"], **{n: turning[n] for n in ("st", "mv", "rs")},
            zT=sb("zTE", [128, NB6, T + 1]), mt={n: sb(f"mt{n}", [128, NB6, T]) for n in "kvr"},
            mx={n: sb(f"mixed{n}", [128, NB6, T]) for n in "kvr"},
            **{n: [sb(f"{n}E{i}", [128, NB6, T]) for i in range(2)] for n in ("ku", "v", "er")},
            K=[sb(f"KE{i}", [128, NB6, T + 1]) for i in range(2)],
            **{n: sb(f"{n}E", [128, NB6, T + 1]) for n in ("MX", "D1", "E2s", "EV", "NUM", "DEN")},
            **{n: sb(f"{n}E", [128, NB6, T]) for n in ("mo", "a", "b", "c", "dd", "e1", "e2", "t1", "t2", "t3")},
            rw=[sb(f"rw{i}", [128, NB6, T]) for i in range(2)])
        Fm = dict(**{n: [sb(f"{n}F{i}", sh, dt) for i in range(2)] for n, sh, dt in (
            ("st", [128, 6], F32), ("mv", [128, 2], F32), ("rs", [128, 12], F32), ("xn", [128, C], F32),
            ("xg", [128, C], F32), ("q", [128, C], BF16), ("qT", [128, 2, T], BF16), ("sg", [128, BH], F32),
            ("y", [128, BH], F32), ("yg", [128, BH], F32), ("sq", [128, BH], F32), ("q2", [128, BH], BF16),
            ("q2T", [128, BH // 128, T], BF16))}, o=sb("o", [128, B, C]))
        scope.pop().close()
        scope.pop().close()

        block = ctx.enter_context(nc.Block())
        def shifted(u):
            return Unit(u.v + B, u.lo + B, u.slot)

        def later(u, k):
            return Unit(u.v + k, u.lo + k, 0) if not isinstance(u.v, int) or u.v + k < B else None

        def from_second(fn):
            return lambda u: fn(u) if u.lo else None

        def early(k, fn):
            return lambda u: fn() if isinstance(u.v, int) and u.v == B - 4 + k else None

        def arrived(eng, u):
            eng.wait_ge(s[f"in_w{u.slot}"], u.v // 2 * 16 + 16 if isinstance(u.v, int) else (u.v - u.slot) * 8 + 16)

        def phase_end(eng, name, k):
            eng.drain().then_inc(s["phase_" + name], 1)
            for n in ("pe", "act", "dve", "pool"):
                eng.wait_ge(s["phase_" + n], k)

        @block.sync
        def _(sp):
            def load(dst, name, sem):
                sp.dma_start(dst, d[name]).then_inc(s[sem], 16)
            load(A["x0"][:, 0:2], "x0a", "in_x0")
            load(A["x1"][:, 0:2], "x1a", "in_x0")
            load(cols[:, :], "cols", "in_x0")
            load(A["x0"][:, 2:8], "x0b", "in_x")
            load(A["x1"][:, 2:8], "x1b", "in_x")
            load(A["wpw"][:, :, :], "wpw", "in_A")
            load(A["fd"][:, :, :], "fd", "in_A")
            load(A["fs"][:, :, :], "fs", "in_A")
            load(rows[:, :], "rows", "in_A")
            load(ident[:, :], "ident", "in_A")

            for n in ("wq", "wk", "wv"):
                load(Bm[n][:, :, :], n, "in_B")

            def ended(k):
                for n in ("pe", "act", "dve", "pool"):
                    sp.wait_ge(s["phase_" + n], k)

            ended(1)

            def load_piece(u):
                after(sp, "w_lo", u, back=2)
                sp.dma_start(raw[u.slot][:, :], d["w_ffn"][:, bass.ts(u.v, PIECE)]).then_inc(s[f"in_w{u.slot}"], 16)

            pipelined(sp, B, 2, 2, [(load_piece, 0)])
            for n in ("wq", "wk", "wv", "wo"):
                load(Cm[n][:, :, :], n + "C", "in_C")
            ended(2)
            pipelined(sp, B, 2, 2, [(lambda u: load_piece(shifted(u)), 0)])
            ended(3)
            load(wg[:, :, :], "wg", "in_D")
            ended(4)
            for n in "kvro":
                load(Em["w"][n][:, :, :], f"w{n}E", "in_E")
            load(rawI[:, :, :], "w_in", "in_F")
            load(rawO[:, :, :], "w_out", "in_F")
            for g in range(NG):
                sp.wait_ge(s["o_ready"], GB * (g + 1))
                sp.dma_start(out[GB * g:GB * g + GB].rearrange("b t c -> t b c"),
                             Fm["o"][:, GB * g:GB * g + GB, :]).then_inc(s["stored"], 16)
            sp.wait_ge(s["stored"], 16 * NG)

        def mm(o, l, r, start, stop, **kw):
            return nc.tensor.matmul(o, l, r, start=start, stop=stop, **kw)

        @block.tensor
        def _(pe):
            a = A

            def a_pointwise(u):
                after(pe, "last_tap", u, per=2)
                for p in range(2):
                    bank = PS[:, 2 * u.slot + p, :]
                    after(pe, "pooled", u, back=2, per=2, k=p + 1)
                    for m, (lo, hi) in enumerate(((0, 128), (128, C))):
                        o = bank[0:hi - lo, m * S:m * S + S]
                        mm(o, a["wpw"][:, 0, lo:hi], a["cv0"][u.slot][:, p, :], True, False)
                        last = mm(o, a["wpw"][64 * p:64 * p + 64, 1, lo:hi],
                                  a["cv1"][u.slot][64 * p:64 * p + 64, :], False, True)
                    last.then_inc(s["pointwise"], 1)

            def a_dft_c(u):
                for p in range(2):
                    h = a["hT"][2 * u.slot + p]
                    after(pe, "relu", u, per=2, k=p + 1)
                    after(pe, "z_copied", u, back=1, per=2, k=p + 1)
                    mm(PS[:, 4 + p, 0:2 * C], h[:, 0, :], a["fd"][:, 0, :], True, False)
                    mm(PS[:, 4 + p, 0:2 * C], h[0:C1, 1, :], a["fd"][0:C1, 1, :], False, True)\
                        .then_inc(s["dft_c"], 1)

            def a_dft_t(u):
                for p in range(2):
                    after(pe, "z_copied", u, per=2, k=p + 1)
                    after(pe, "y_normed", u, back=1, per=2, k=p + 1)
                    mm(PS[:, 6 + p, 0:C], a["fs"][:, 0, :], a["Z"][p][:, 0:C], True, False)
                    mm(PS[:, 6 + p, 0:C], a["fs"][:, 1, :], a["Z"][p][:, C:2 * C], False, True)\
                        .then_inc(s["dft_t"], 1)

            pe.wait_ge(s["in_A"], 16 * 5)
            pipelined(pe, B // 2, 2, 2, [(a_dft_c, 3), (a_pointwise, 2), (a_dft_t, 3)])
            m_ = Bm

            def b_turn(u):
                after(pe, "b_normed", u)
                if u.lo == 0:
                    pe.wait_ge(s["pooled"], B)
                after(pe, "b_zT", u, back=1)
                pe.transpose(PS[:, 0, 0:128], m_["zn"][u.slot][:, 0:128], ident[:, :])
                pe.transpose(PS[0:C1, 0, 128:256], m_["zn"][u.slot][:, 128:C], ident[:, :]).then_inc(s["b_turned"], 1)

            b_turn(Unit(0, 0, 0))
            phase_end(pe, "pe", 1)

            m_ = Bm

            def b_qk(u):
                z = m_["zT"][u.slot]
                after(pe, "b_zT", u)
                after(pe, "b_qk", u, back=1)
                for j, w in enumerate((m_["wq"], m_["wk"])):
                    for m, (lo, hi) in enumerate(((0, 128), (128, C))):
                        o = PS[0:hi - lo, 1, (2 * j + m) * T:(2 * j + m + 1) * T]
                        mm(o, w[:, 0, lo:hi], z[:, 0, :], True, False)
                        last = mm(o, w[0:C1, 1, lo:hi], z[0:C1, 1, :], False, True)
                last.then_inc(s["b_qk_made"], 1)

            def b_values(u):
                z = m_["zT"][u.slot]
                after(pe, "b_zT", u)
                after(pe, "b_v", u, back=1)
                mm(PS[:, 2, 0:C], z[:, 0, :], m_["wv"][:, 0, :], True, False)
                mm(PS[:, 2, 0:C], z[0:C1, 1, :], m_["wv"][0:C1, 1, :], False, True).then_inc(s["b_v_made"], 1)

            def b_scores(u):
                q, k = m_["qT"][u.slot], m_["kT"][u.slot]
                after(pe, "b_qk", u)
                after(pe, "b_exp", u, back=1)
                mm(PS[:, 3, 0:T], q[:, 0, :], k[:, 0, :], True, False)
                mm(PS[:, 3, 0:T], q[0:C1, 1, :], k[0:C1, 1, :], False, True).then_inc(s["b_scored"], 1)

            def b_turn_p(u):
                after(pe, "b_exp", u)
                after(pe, "b_pT", u, back=1)
                pe.transpose(PS[:, 4, 0:T], m_["p"][u.slot][:, :], ident[:, :]).then_inc(s["b_p_turned"], 1)

            def b_attend(u):
                after(pe, "b_pT", u)
                after(pe, "b_v", u)
                after(pe, "b_added", u, back=1)
                mm(PS[:, 5, 0:C], m_["pT"][u.slot][:, :], m_["v"][u.slot][:, :], True, True)\
                    .then_inc(s["b_attended"], 1)

            pe.wait_ge(s["in_B"], 48)
            c = Cm

            def c_turn(u):
                after(pe, "c_normed", u)
                after(pe, "c_q", u, back=1)
                after(pe, "c_added", u, back=4)
                pe.transpose(PS[:, 6, 0:128], c["zn"][u.slot][:, 0:128], ident[:, :])
                pe.transpose(PS[0:C1, 6, 128:256], c["zn"][u.slot][:, 128:C], ident[:, :]).then_inc(s["c_turned"], 1)

            pipelined(pe, B, 2, 2, [(from_second(b_turn), 1), (b_turn_p, 3), (b_attend, 4), (b_scores, 2), (b_qk, 1),
                                    (b_values, 2), (early(2, lambda: c_turn(Unit(0, 0, 0))), 4)])
            phase_end(pe, "pe", 2)

            c = Cm

            def c_queries(u):
                z = c["zT"][u.slot]
                after(pe, "c_zT", u)
                for g in range(3):
                    o, k = PS[:, 6, g * T:(g + 1) * T], slice(g * 128, (g + 1) * 128)
                    mm(o, c["wq"][:, 0, k], z[:, 0, :], True, False)
                    last = mm(o, c["wq"][0:C1, 1, k], z[0:C1, 1, :], False, True)
                last.then_inc(s["c_q_made"], 1)

            def c_keys(u):
                z = c["zT"][u.slot]
                after(pe, "c_zT", u)
                after(pe, "c_k", u, back=1)
                after(pe, "c_cT", u, back=3)
                for g in range(3):
                    o, k = PS[:, 7, g * T:(g + 1) * T], slice(g * 128, (g + 1) * 128)
                    mm(o, c["wk"][:, 0, k], z[:, 0, :], True, False)
                    last = mm(o, c["wk"][0:C1, 1, k], z[0:C1, 1, :], False, True)
                last.then_inc(s["c_k_made"], 1)

            def c_values(u):
                z = c["zT"][u.slot]
                after(pe, "c_pT", u, back=1, per=2, k=2)
                after(pe, "c_v", u, back=1)
                mm(PS[:, 5, 0:C], z[:, 0, :], c["wv"][:, 0, :], True, False)
                mm(PS[:, 5, 0:C], z[0:C1, 1, :], c["wv"][0:C1, 1, :], False, True).then_inc(s["c_v_made"], 1)

            def c_scores(u):
                after(pe, "c_q", u)
                after(pe, "c_k", u)
                after(pe, "c_exp", u, back=1)
                for g in range(3):
                    for j in range(4):
                        last = mm(PS[:, j, g * T:(g + 1) * T], c["qT"][u.slot][32 * j:32 * j + HD, g, :],
                                  c["kT"][u.slot][32 * j:32 * j + HD, g, :], True, True)
                last.then_inc(s["c_scored"], 1)

            def turn_weights(u, r):
                for j in range(4):
                    last = pe.transpose(PS[:, 4 + r % 2, j * T:(j + 1) * T], c["E"][u.slot][:, 4 * r + j, :], ident[:, :])
                last.then_inc(s["c_p_turned"], 1)

            def c_turn_p01(u):
                after(pe, "c_scaled", u)
                after(pe, "c_pT2", u, back=1)
                turn_weights(u, 0)
                after(pe, "c_v", u)
                turn_weights(u, 1)

            def c_turn_p2(u):
                after(pe, "c_pT", u, per=2, k=1)
                turn_weights(u, 2)

            def c_attend(u):
                after(pe, "c_pT", u, per=2)
                after(pe, "c_pT2", u)
                after(pe, "c_v", u)
                after(pe, "c_cT", u, back=1)
                if later(u, 2):
                    after(pe, "c_k", later(u, 2))
                for h in range(HEADS):
                    j, g = h % 4, h // 4
                    last = mm(PS[32 * j:32 * j + 32, 7, g * T:(g + 1) * T], c["v"][u.slot][:, h, :],
                              c["PT"][:, j * 3 + g, :], True, True)
                last.then_inc(s["c_attended"], 1)

            def c_project(u):
                t = c["cT"][u.slot]
                after(pe, "c_cT", u)
                after(pe, "c_added", u, back=1)
                if later(u, 3):
                    after(pe, "c_q", later(u, 3))
                for g in range(3):
                    last = mm(PS[:, 6, 0:C], t[:, g, :], c["wo"][:, g, :], g == 0, g == 2)
                last.then_inc(s["c_projected"], 1)

            pe.wait_ge(s["in_C"], 64)
            pipelined(pe, B, 2, 3, [(c_scores, 2), (from_second(c_turn), 1), (c_turn_p01, 3), (c_queries, 1), (c_turn_p2, 3),
                                    (c_keys, 1), (c_values, 2), (c_project, 4), (c_attend, 3)])
            def turn_group(sem, g=None):
                for t in range(GB):
                    pe.transpose(PS[:, 0, t * T:(t + 1) * T],
                                 turning["xs"][t][:, 0:128] if g is None else X[:, g * GB + t, 0:128], ident[:, :])
                for t in range(GB):
                    last = pe.transpose(PS[:, 1, t * T:(t + 1) * T], turning["xs"][t][:, 128:256], ident[:, :])
                last.then_inc(s[sem], 1)

            def turn_x(g):
                pe.wait_ge(s["x_copied"], GB * (g + 1))
                if g == 0:
                    pe.wait_ge(s["c_exp"], B)
                    pe.wait_ge(s["c_added"], GB)
                if g > 0:
                    pe.wait_ge(s["x_split"], g)
                if g > 1:
                    pe.wait_ge(s["gate_read"], g - 1)
                turn_group("x_turned", g)

            turn_x(0)
            phase_end(pe, "pe", 3)

            q = D

            def ups(f, g, w):
                wh, wl = w_up(w, 0), w_up(w, 1)
                for m in range(HCH):
                    after(pe, "gelu", f, back=1, per=HCH, k=HCH + m - 1) if m < 2 else \
                        after(pe, "gelu", f, per=HCH, k=m - 1)
                    o, k = PS[:, 2 + m % 2, :], slice(m * 128, m * 128 + 128)
                    mm(o, wh[:, 0, k], q["XH"][:, g, :], True, False)
                    mm(o, wl[:, 0, k], q["XH"][:, g, :], False, False)
                    mm(o, wh[:, 0, k], q["XL"][:, g, :], False, False)
                    mm(o, wh[:, 1, k], q["XS"][:, g, :], False, False)
                    mm(o, wl[0:C1, 1, k], q["XS"][0:C1, g, :], False, True).then_inc(s["up"], 1)

            def downs(f, w, between=None, later_=None):
                wd = w_down(w)
                for m in range(HCH):
                    if m == 2 and between:
                        between()
                    if m == 4 and later_:
                        later_()
                    after(pe, "gelu_split", f, per=HCH, k=m + 1)
                    for t in range(GB):
                        if m == 0:
                            after(pe, "down_read", f, back=1, per=GB, k=t + 1)
                        k = slice(t * T, t * T + T)

                        def high():
                            return mm(PS[:, 4 + t, 0:2 * C].rearrange("p (two c) -> p two c", two=2), q["Gh"][:, m, k],
                                      wd[:, :, m, :], m == 0, m == HCH - 1)

                        def low():
                            return mm(PS[:, 4 + t, 0:C], q["Gl"][:, m, k], wd[:, 0, m, :], False, False)

                        if m < HCH - 1:
                            high()
                            low()
                        else:
                            low()
                            high().then_inc(s["down"], 1)

            pe.wait_ge(s["in_D"], 16)
            for g in range(NG + 1):
                pe.wait_ge(s["x_split"], g + 1) if g < NG else pe.wait_ge(s["xm_split"], 1)
                f = Unit(g, g, 0)
                ups(f, g % NG, 0 if g < NG else 1)
                if g > 0:
                    pe.wait_ge(s["xm_copied"], GB * g)
                    if g < NG:
                        pe.wait_ge(s["x_split"], g + 1)
                    turn_group("xm_turned")

                def gate():
                    pe.wait_ge(s["xm_scaled"], 2 * g)
                    for t in range(GB):
                        o = PS[:, 0, t * NEXP:(t + 1) * NEXP]
                        mm(o, q["XM"][0][:, t * T:(t + 1) * T], wg[:, 0, :], True, False)
                        last = mm(o, q["XM"][1][0:C1, t * T:(t + 1) * T], wg[0:C1, 1, :], False, True)
                    last.then_inc(s["gated"], 1)

                downs(f, 0 if g < NG else 1, gate if g > 0 else None, (lambda: turn_x(g + 1)) if g + 1 < NG else None)

            def d_experts(u, first):
                for e in range(first, NEXP):
                    f = Unit(u.v * NEXP + (NG + e), u.lo * NEXP + NG + e, 0)
                    if u.lo == 1 and e == 0:
                        pe.wait_ge(s["xm_split"], NG)
                    ups(f, u.v, 1 + e)
                    downs(f, 1 + e)

            d_experts(Unit(0, 0, 0), 1)
            with pe.Fori(0, NG - 1) as i:
                d_experts(Unit(i + 1, 1, 0), 0)
            e_ = Em

            def e_turn(u):
                after(pe, "e_normed", u, per=GB)
                if u.v == 0:
                    pe.wait_ge(s["gate_read"], NG)
                after(pe, "e_zT", u, back=1, per=3)
                for t in range(GB):
                    pe.transpose(PS[:, 0, t * T:(t + 1) * T], e_["zn"][t][:, 0:128], ident[:, :])
                for t in range(GB):
                    last = pe.transpose(PS[:, 1, t * T:(t + 1) * T], e_["zn"][t][:, 128:256], ident[:, :])
                last.then_inc(s["e_turned"], 1)

            e_turn(Unit(0, 0, 0))
            phase_end(pe, "pe", 4)

            pe.wait_ge(s["in_E"], 64)

            def e_project(u):
                for j, n in enumerate("kvr"):
                    w, x = e_["w"][n], e_["mx"][n]
                    after(pe, "e_mixed", u, per=3, k=j + 1)
                    after(pe, f"e_read_{n}", u, back=1)
                    if n == "r":
                        after(pe, "e_added", u, back=2, per=GB)
                    b0, b1 = PS[:, 2 + 2 * j, :], PS[:, 3 + 2 * j, :]
                    mm(b0, w[:, 0, 0:128], x[:, 0:GB, :], True, False)

                    def rest(p):
                        return mm(b0[:, 256 * p:256 * p + 256], w[64 * p:64 * p + 64, 1, 0:128],
                                  x[64 * p:64 * p + 64, GB:NB6, :], False, p == 1)

                    rest(0).then_inc(s["e_half"], 1)
                    for p in range(2):
                        mm(b1[64 * p:64 * p + 64, 0:256], w[:, 0, 128:C], x[:, 2 * p:2 * p + 2, :], True, False)
                    for p in range(2):
                        mm(b1[64 * p:64 * p + 64, 0:256], w[64 * p:64 * p + 64, 1, 128:C],
                           x[64 * p:64 * p + 64, GB:NB6, :], False, True)
                    after(pe, "e_half", u, per=3, k=j + 1)
                    last = rest(1)
                    last.then_inc(s["e_projected"], 1)

            def e_out(u):
                after(pe, "e_rw", u)
                if u.v + 1 < NG:
                    after(pe, "e_read_r", Unit(u.v + 1, u.lo + 1, 0))
                for t in range(GB):
                    o = PS[:, 6 + t // 2, (t % 2) * C:(t % 2) * C + C]
                    p = t // 2
                    mm(o, e_["rw"][u.slot][:, t, :], e_["w"]["o"][:, 0, :], True, False)
                    last = mm(o, e_["rw"][u.slot][64 * p:64 * p + 64, GB + t % 2, :],
                              e_["w"]["o"][64 * p:64 * p + 64, 1, :], False, True)
                last.then_inc(s["e_out"], 1)

            def w_means(u):
                if u.v == 0:
                    pe.wait_ge(s["f_wsum"], 1)
                    after(pe, "e_read_r", u)
                    mm(PS[:, 7, 256:258], ones[:, :], qs[:, 0:2], True, True).then_inc(s["f_wmean"], 1)
                    pe.wait_ge(s["f_prep"], 4)

            pipelined(pe, NG, 2, 2, [(lambda u: u.v and e_turn(u), 1), (w_means, 2), (e_out, 3), (e_project, 1)])

            f_ = Fm

            def f_turn(u):
                after(pe, "f_q", u)
                after(pe, "f_qT", u, back=1)
                tb = PS[:, 0, :].bitcast(BF16)
                pe.transpose(tb[:, 0:128], f_["q"][u.slot][:, 0:128], identb[:, :])
                pe.transpose(tb[0:C1, 128:256], f_["q"][u.slot][:, 128:C], identb[:, :]).then_inc(s["f_turned"], 1)

            def f_up(u):
                after(pe, "f_qT", u)
                for j in range(2):
                    o = PS[:, 1 + 2 * u.slot + j, :]
                    if j == 0:
                        after(pe, "f_y", u, back=2)
                    for k in range(2):
                        n = 128 if k == 0 else C1
                        last = mm(o, f_["qT"][u.slot][0:n, k, :], wI[0:n, k, j * BH:(j + 1) * BH], k == 0, k == 1)
                last.then_inc(s["f_up"], 1)

            def f_turn2(u):
                after(pe, "f_q2", u)
                after(pe, "f_q2T", u, back=1)
                tb = PS[:, 5, :].bitcast(BF16)
                for k in range(BH // 128):
                    last = pe.transpose(tb[:, k * T:(k + 1) * T], f_["q2"][u.slot][:, k * 128:(k + 1) * 128],
                                        identb[:, :])
                last.then_inc(s["f_turned2"], 1)

            def f_down(u):
                if u.lo == 0:
                    after(pe, "e_added", Unit(NG - 1, NG - 1, 0), per=GB)
                after(pe, "f_q2T", u)
                after(pe, "o_ready", u, back=1)
                for k in range(BH // 128):
                    last = mm(PS[:, 6, 0:C], f_["q2T"][u.slot][:, k, :], wO[:, k, :], k == 0, k == BH // 128 - 1)
                last.then_inc(s["f_down"], 1)

            pe.wait_ge(s["f_weights"], 2)
            last = Unit(NG - 1, NG - 1, 0)
            after(pe, "e_zT", last, per=3)
            for n in "kvr":
                after(pe, f"e_read_{n}", last)
            pipelined(pe, B, 2, 2, [(f_up, 2), (f_turn, 1), (f_turn2, 3), (f_down, 3)])

        @block.scalar
        def _(act):
            def w_high(u):
                arrived(act, u)
                act.copy(WW[:, 0, bass.ts(u.v, PIECE)], raw[u.slot][:, :]).then_inc(s["w_hi"], 1)

            a = A
            act.wait_ge(s["in_x0"], 48)

            def a_tap(u):
                after(act, "pointwise", u, back=2, per=2)
                act.activation(a["cv0"][u.slot][:, :, :], a["x0"][:, u.v, :, 0:S], ACT.Identity,
                               bias=col("b_dw", 0), scale=cols[:, TAP:TAP + 1])
                act.activation(a["cv1"][u.slot][:, :], a["x1"][:, u.v, 0:S], ACT.Identity,
                               bias=col("b_dw", 1), scale=cols[:, TAP + TAPS:TAP + TAPS + 1]).then_inc(s["tap0"], 1)

            def a_last_product(u):
                k = TAPS - 1
                after(act, "last_tap", u, back=1, per=2)
                act.activation(a["lt0"][:, :, :], a["x0"][:, u.v, :, k:k + S], ACT.Copy,
                               scale=cols[:, TAP + k:TAP + k + 1])
                act.activation(a["lt1"][:, :], a["x1"][:, u.v, k:k + S], ACT.Copy,
                               scale=cols[:, TAP + TAPS + k:TAP + TAPS + k + 1]).then_inc(s["last_product"], 1)

            def a_tap_(u):
                if u.lo == 2:
                    act.wait_ge(s["in_x"], 32)
                a_tap(u)

            def a_relu(u):
                for p in range(2):
                    i = 2 * u.slot + p
                    after(act, "pooled", u, per=2, k=p + 1)
                    after(act, "dft_c", u, back=2, per=2, k=p + 1)
                    act.activation(a["hT"][i][:, 0, :], a["hp"][i][:, 0, :], ACT.Relu, bias=col("b_pw", 0))
                    act.activation(a["hT"][i][0:C1, 1, :], a["hp"][i][0:C1, 1, :], ACT.Relu,
                                   bias=col("b_pw", 1, C1)).then_inc(s["relu"], 1)

            def a_copy(u):
                for p in range(2):
                    after(act, "dft_c", u, per=2, k=p + 1)
                    after(act, "dft_t", u, back=1, per=2, k=p + 1)
                    act.copy(a["Z"][p][:, :], PS[:, 4 + p, 0:2 * C]).then_inc(s["z_copied"], 1)

            pipelined(act, B // 2, 2, 2, [(a_copy, 3), (a_tap_, 0), (a_relu, 2), (a_last_product, 0)])
            phase_end(act, "act", 1)

            m_ = Bm

            def b_zT(u):
                after(act, "b_turned", u)
                after(act, "b_v_made", u, back=2)
                act.copy(m_["zT"][u.slot][:, 0, :], PS[:, 0, 0:128])
                act.copy(m_["zT"][u.slot][0:C1, 1, :], PS[0:C1, 0, 128:256]).then_inc(s["b_zT"], 1)

            def b_qk(u):
                after(act, "b_qk_made", u)
                after(act, "b_scored", u, back=2)
                for j, (n, bias) in enumerate((("qT", "bq"), ("kT", "bk"))):
                    act.activation(m_[n][u.slot][:, 0, :], PS[:, 1, 2 * j * T:(2 * j + 1) * T], ACT.Identity,
                                   bias=col(bias, 0))
                    last = act.activation(m_[n][u.slot][0:C1, 1, :], PS[0:C1, 1, (2 * j + 1) * T:(2 * j + 2) * T],
                                          ACT.Identity, bias=col(bias, 1, C1))
                last.then_inc(s["b_qk"], 1)

            def b_exp(u):
                after(act, "b_max", u)
                after(act, "b_p_turned", u, back=2)
                act.activation(m_["p"][u.slot][:, :], PS[:, 3, 0:T], ACT.Exp, bias=m_["nm"][u.slot][:, 1:2],
                               scale=C ** -0.5, accum_out=m_["sum"][u.slot][:, 0:1]).then_inc(s["b_exp"], 1)

            pipelined(act, B, 2, 2, [(b_zT, 1), (b_exp, 2), (w_high, 1), (b_qk, 1)])
            phase_end(act, "act", 2)

            c = Cm

            def c_zT(u):
                after(act, "c_turned", u)
                after(act, "c_v_made", u, back=2)
                act.activation(c["zT"][u.slot][:, 0, :], PS[:, 6, 0:128], ACT.Identity, bias=col("ln1_b", 0),
                               scale=col("ln1_g", 0))
                act.activation(c["zT"][u.slot][0:C1, 1, :], PS[0:C1, 6, 128:256], ACT.Identity,
                               bias=col("ln1_b", 1, C1), scale=col("ln1_g", 1, C1)).then_inc(s["c_zT"], 1)

            def c_exp(u):
                after(act, "c_max", u)
                after(act, "c_p_turned", u, back=2, per=3)
                i = u.slot
                for j in range(4):
                    for g in range(3):
                        h = 3 * j + g
                        last = act.activation(c["E"][i][:, h, :], PS[:, j, g * T:(g + 1) * T], ACT.Exp,
                                              bias=c["nm"][i][:, h:h + 1], scale=HD ** -0.5,
                                              accum_out=c["sum"][i][:, h:h + 1])
                last.then_inc(s["c_exp"], 1)

            def c_pT01(u):
                after(act, "c_attended", u, back=1)
                for r in range(2):
                    after(act, "c_p_turned", u, per=3, k=r + 1)
                    act.copy(c["PT"][:, 4 * r:4 * r + 4, :],
                             PS[:, 4 + r, :].rearrange("p (h t) -> p h t", h=4)).then_inc(s["c_pT"], 1)

            def c_cT(u):
                after(act, "c_attended", u)
                after(act, "c_projected", u, back=2)
                act.copy(c["cT"][u.slot][:, :, :], PS[:, 7, 0:3 * T].rearrange("p (g t) -> p g t", g=3))\
                    .then_inc(s["c_cT"], 1)

            pipelined(act, B, 2, 3, [(c_cT, 4), (c_zT, 1), (c_pT01, 3), (c_exp, 2),
                                     (lambda u: w_high(shifted(u)), 1)])
            phase_end(act, "act", 3)

            q = D

            def gelus(f, w):
                for m in range(HCH):
                    after(act, "up", f, per=HCH, k=m + 1)
                    after(act, "gelu_split", f, back=1, per=HCH, k=HCH + m - 2) if m < 3 else \
                        after(act, "gelu_split", f, per=HCH, k=m - 2)
                    act.activation(q["G"][m % 3][:, :], PS[:, 2 + m % 2, :], ACT.Gelu,
                                   bias=cols[:, HB + w * HCH + m:HB + w * HCH + m + 1]).then_inc(s["gelu"], 1)

            def high_parts(g):
                act.wait_ge(s["x_turned"], g + 1)
                act.copy(q["XH"][:, g, :], PS[:, 0, :]).then_inc(s["x_hi"], 1)
                act.copy(q["XS"][:, g, :], PS[:, 1, :]).then_inc(s["x_hi"], 1)

            high_parts(0)
            for g in range(NG + 1):
                gelus(Unit(g, g, 0), 0 if g < NG else 1)
                if g > 0:
                    act.wait_ge(s["xm_turned"], g)
                    if g > 1:
                        act.wait_ge(s["gated"], g - 1)
                        act.wait_ge(s["xm_split"], g - 1)
                    for k in range(2):
                        act.activation(q["XM"][k][:, :], PS[:, k, :], ACT.Identity, bias=col("ln2_b", k),
                                       scale=col("ln2_g", k)).then_inc(s["xm_scaled"], 1)
                    act.wait_ge(s["up"], HCH * g)
                    for k, x in enumerate((q["XH"], q["XS"])):
                        act.wait_ge(s["xm_scaled"], 2 * g - 1 + k)
                        act.copy(x[:, g - 1, :], q["XM"][k][:, :]).then_inc(s["xm_hi"], 1)
                if g + 1 < NG:
                    high_parts(g + 1)
            act.wait_ge(s["logit_sub"], 1)
            act.activation(q["comb"][:, :, :], q["cmp"][:, :, :], ACT.Exp).then_inc(s["gate_exp"], 1)

            def d_experts(u, first):
                for e in range(first, NEXP):
                    gelus(Unit(u.v * NEXP + (NG + e), u.lo * NEXP + NG + e, 0), 1 + e)

            d_experts(Unit(0, 0, 0), 1)
            with act.Fori(0, NG - 1) as i:
                d_experts(Unit(i + 1, 1, 0), 0)
            phase_end(act, "act", 4)

            e_ = Em
            act.wait_ge(s["e_consts"], 9)

            def e_decay(u):
                if u.v == 0:
                    act.activation(e_["ndec"][:, :], cols[:, COL["decay"]:COL["decay"] + 2], ACT.Exp)\
                        .then_inc(s["e_decay"], 1)

            def e_zT(u):
                after(act, "e_turned", u)
                after(act, "e_mixed", u, back=1, per=3)
                act.copy(e_["zT"][:, 0:GB, 1:T + 1], PS[:, 0, :].rearrange("p (b t) -> p b t", b=GB))\
                    .then_inc(s["e_zT"], 1)
                for p in range(2):
                    act.copy(e_["zT"][64 * p:64 * p + 64, GB:NB6, 1:T + 1],
                             PS[64 * p:64 * p + 64, 1, 256 * p:256 * p + 256].rearrange("p (b t) -> p b t", b=2))\
                        .then_inc(s["e_zT"], 1)
                after(act, "e_zT", u, per=3)
                for n in "kvr":
                    for k, bl in enumerate((slice(0, GB), slice(GB, NB6))):
                        last = act.activation(e_["mt"][n][:, bl, :], e_["zT"][:, bl, 1:T + 1], ACT.Copy,
                                              scale=col("mix_" + n, k))
                    last.then_inc(s["e_mt"], 1)

            def e_read(u):
                def banks(j):
                    return (PS[:, 2 + 2 * j, :].rearrange("p (b t) -> p b t", b=GB),
                            PS[:, 3 + 2 * j, 0:256].rearrange("p (b t) -> p b t", b=2))
                i = u.slot
                after(act, "e_projected", u, per=3, k=1)
                after(act, "e_rw", u, back=2)
                for k, bl in enumerate((slice(0, GB), slice(GB, NB6))):
                    act.copy(e_["K"][i][:, bl, 1:T + 1], banks(0)[k])
                    last = act.activation(e_["ku"][i][:, bl, :], banks(0)[k], ACT.Identity, bias=col("first", k))
                last.then_inc(s["e_read_k"], 1)
                after(act, "e_projected", u, per=3, k=2)
                for k, bl in enumerate((slice(0, GB), slice(GB, NB6))):
                    last = act.copy(e_["v"][i][:, bl, :], banks(1)[k])
                last.then_inc(s["e_read_v"], 1)
                after(act, "e_projected", u, per=3, k=3)
                for k, bl in enumerate((slice(0, GB), slice(GB, NB6))):
                    last = act.activation(e_["er"][i][:, bl, :], banks(2)[k], ACT.Exp, scale=-1.0)
                last.then_inc(s["e_read_r"], 1)

            def e_exp(u):
                for n, dst, src in (("c", e_["D1"][:, :, 1:T + 1], "c"), ("dd", e_["E2s"][:, :, 1:T + 1], "dd"),
                                    ("a", e_["e1"][:, :, :], "a"), ("b", e_["e2"][:, :, :], "b")):
                    after(act, "e_arg_" + n, u)
                    after(act, "e_rw", u, back=1)
                    act.activation(dst, e_[src][:, :, :], ACT.Exp).then_inc(s["e_exp_" + n], 1)

            pipelined(act, NG, 2, 2, [(e_zT, 1), (e_decay, 1), (e_exp, 2), (e_read, 1)])

            f_ = Fm

            def f_unmagic(u):
                after(act, "f_clip", u)
                after(act, "f_turned", u, back=2)
                act.activation(f_["q"][u.slot][:, :], f_["xg"][u.slot][:, :], ACT.Identity, bias=magic[:, 0:1])\
                    .then_inc(s["f_q"], 1)

            def f_unmagic2(u):
                after(act, "f_clip2", u)
                after(act, "f_turned2", u, back=2)
                act.activation(f_["q2"][u.slot][:, :], f_["yg"][u.slot][:, :], ACT.Identity, bias=magic[:, 0:1])\
                    .then_inc(s["f_q2"], 1)

            def f_qT(u):
                tb = PS[:, 0, :].bitcast(BF16)
                after(act, "f_turned", u)
                after(act, "f_up", u, back=2)
                act.copy(f_["qT"][u.slot][:, 0, :], tb[:, 0:128])
                act.copy(f_["qT"][u.slot][0:C1, 1, :], tb[0:C1, 128:256]).then_inc(s["f_qT"], 1)

            def f_silu(u):
                after(act, "f_up", u)
                after(act, "f_y", u, back=2)
                act.activation(f_["sg"][u.slot][:, :], PS[:, 2 + 2 * u.slot, :], ACT.Silu,
                               scale=f_["rs"][u.slot][:, 6:7]).then_inc(s["f_silu"], 1)

            def f_square(u):
                after(act, "f_y", u)
                after(act, "f_scale2", u, back=2)
                act.activation(f_["sq"][u.slot][:, :], f_["y"][u.slot][:, :], ACT.Square,
                               accum_out=f_["rs"][u.slot][:, 7:8]).then_inc(s["f_sq"], 1)

            def f_q2T(u):
                after(act, "f_turned2", u)
                after(act, "f_down", u, back=2)
                tb = PS[:, 5, :].bitcast(BF16)
                act.copy(f_["q2T"][u.slot][:, :, :], tb[:, 0:BH].rearrange("p (k t) -> p k t", k=BH // 128))\
                    .then_inc(s["f_q2T"], 1)

            pipelined(act, B, 2, 2, [(f_square, 3), (f_silu, 2), (f_unmagic, 1), (f_unmagic2, 3), (f_qT, 1), (f_q2T, 3)])

        @block.vector
        def _(dve):
            def stt(o, i0, sc, i1, op0, op1, **kw):
                return dve.scalar_tensor_tensor(out=o, in0=i0, scalar=sc, in1=i1, op0=op0, op1=op1, **kw)

            def tt(o, i0, i1, op):
                return dve.tensor_tensor(o, i0, i1, op)

            a = A
            dve.wait_ge(s["in_x0"], 48)

            def a_taps(u):
                if u.lo == 2:
                    dve.wait_ge(s["in_x"], 32)
                after(dve, "tap0", u)
                for k in range(1, TAPS - 1):
                    if k > 1:
                        after(dve, "tap_a", u, per=TAPS - 2, k=k - 1)
                    stt(a["cv0"][u.slot][:, :, :], a["x0"][:, u.v, :, k:k + S], cols[:, TAP + k:TAP + k + 1],
                        a["cv0"][u.slot][:, :, :], ALU.mult, ALU.add).then_inc(s["tap_a"], 1)
                    if k > 1:
                        after(dve, "tap_b", u, per=TAPS - 2, k=k - 1)
                    stt(a["cv1"][u.slot][:, :], a["x1"][:, u.v, k:k + S], cols[:, TAP + TAPS + k:TAP + TAPS + k + 1],
                        a["cv1"][u.slot][:, :], ALU.mult, ALU.add).then_inc(s["tap_b"], 1)

            def a_pool(u):
                for p in range(2):
                    i = 2 * u.slot + p
                    bank = PS[:, i, :]
                    after(dve, "pointwise", u, per=2, k=p + 1)
                    after(dve, "relu", u, back=2, per=2, k=p + 1)
                    dve.tensor_reduce(a["hp"][i][:, 0, :], bank[:, 0:S].rearrange("p (t two) -> p t two", two=2),
                                      AX.X, ALU.max)
                    dve.tensor_reduce(a["hp"][i][0:C1, 1, :],
                                      bank[0:C1, S:2 * S].rearrange("p (t two) -> p t two", two=2),
                                      AX.X, ALU.max).then_inc(s["pooled"], 1)

            def a_stats(u):
                for p in range(2):
                    i = 2 * u.slot + p
                    after(dve, "dft_t", u, per=2, k=p + 1, nop=True)
                    dve.bn_stats(a["st"][i][:, :], PS[:, 6 + p, 0:C]).then_inc(s["a_st"], 1)
                for p in range(2):
                    i = 2 * u.slot + p
                    after(dve, "a_st", u, per=2, k=p + 1, nop=True)
                    dve.bn_aggr(a["mv"][i][:, :], a["st"][i][:, :]).then_inc(s["a_mv"], 1)

            def a_norm(u):
                for p in range(2):
                    i = 2 * u.slot + p
                    after(dve, "a_rstd", u, per=2, k=p + 1)
                    after(dve, "h_A", u, back=2, per=2, k=p + 1)
                    dve.tensor_scalar(a["yn"][i][:, :], PS[:, 6 + p, 0:C], a["mv"][i][:, 0:1], a["rs"][i][:, 1:2],
                                      ALU.subtract, ALU.mult).then_inc(s["y_normed"], 1)

            m_ = Bm

            def b_stats(u):
                i = u.slot
                if u.lo == 0:
                    dve.wait_ge(s["h_A"], 1)
                dve.bn_stats(m_["st"][i][:, :], H[:, u.v, :]).then_inc(s["b_st"], 1)
                after(dve, "b_st", u, nop=True)
                dve.bn_aggr(m_["mv"][i][:, :], m_["st"][i][:, :]).then_inc(s["b_mv"], 1)

            def b_norm(u):
                i = u.slot
                after(dve, "b_rstd", u)
                after(dve, "b_turned", u, back=2)
                dve.tensor_scalar(m_["zn"][i][:, :], H[:, u.v, :], m_["mv"][i][:, 0:1], m_["rs"][i][:, 1:2],
                                  ALU.subtract, ALU.mult).then_inc(s["b_normed"], 1)

            def b_first(u):
                if u.v == B // 2 - 2:
                    b_stats(Unit(0, 0, 0))
                if u.v == B // 2 - 1:
                    b_norm(Unit(0, 0, 0))

            pipelined(dve, B // 2, 2, 2, [(a_stats, 4), (b_first, 4), (a_taps, 1), (a_norm, 4), (a_pool, 2)])
            phase_end(dve, "dve", 1)

            m_ = Bm

            def b_v(u):
                after(dve, "b_v_made", u)
                after(dve, "b_attended", u, back=2)
                tt(m_["v"][u.slot][:, :], PS[:, 2, 0:C], row("bv"), ALU.add).then_inc(s["b_v"], 1)

            def b_max(u):
                i = u.slot
                after(dve, "b_scored", u)
                dve.tensor_reduce(m_["nm"][i][:, 0:1], PS[:, 3, 0:T], AX.X, ALU.max).then_inc(s["b_rowmax"], 1)
                after(dve, "b_rowmax", u)
                dve.tensor_scalar(m_["nm"][i][:, 1:2], m_["nm"][i][:, 0:1], -(C ** -0.5), None, ALU.mult)\
                    .then_inc(s["b_max"], 1)

            def b_pT(u):
                after(dve, "b_p_turned", u)
                after(dve, "b_attended", u, back=2)
                dve.tensor_copy(m_["pT"][u.slot][:, :], PS[:, 4, 0:T]).then_inc(s["b_pT"], 1)
                after(dve, "b_added", u, back=2)
                dve.reciprocal(m_["sum"][u.slot][:, 1:2], m_["sum"][u.slot][:, 0:1]).then_inc(s["b_recip"], 1)

            def b_add(u):
                i = u.slot
                after(dve, "b_attended", u)
                after(dve, "b_recip", u)
                stt(H[:, u.v, :], PS[:, 5, 0:C], m_["sum"][i][:, 1:2], H[:, u.v, :], ALU.mult, ALU.add)\
                    .then_inc(s["b_added"], 1)

            c = Cm

            def c_stats(u):
                i = u.slot
                if u.lo == 0:
                    dve.wait_ge(s["b_added"], 1)
                dve.bn_stats(c["st"][i][:, :], H[:, u.v, :]).then_inc(s["c_st"], 1)

            def c_aggr(u):
                i = u.slot
                after(dve, "c_st", u, nop=True)
                dve.bn_aggr(c["mv"][i][:, :], c["st"][i][:, :]).then_inc(s["c_mv"], 1)

            def c_norm_x(u):
                i = u.slot
                after(dve, "c_rstd", u)
                dve.tensor_scalar(X[:, u.v, :], H[:, u.v, :], c["mv"][i][:, 0:1], c["rs"][i][:, 1:2],
                                  ALU.subtract, ALU.mult).then_inc(s["c_x"], 1)

            def c_norm(u):
                i = u.slot
                after(dve, "c_x", u)
                after(dve, "c_turned", u, back=2)
                dve.tensor_scalar(c["zn"][i][:, :], X[:, u.v, :], c["rs"][i][:, 5:6], None, ALU.mult)\
                    .then_inc(s["c_normed"], 1)

            first = Unit(0, 0, 0)
            pipelined(dve, B, 2, 2, [(from_second(b_stats), 0), (early(0, lambda: (c_stats(first), c_aggr(first))), 4),
                                     (b_pT, 3), (b_max, 2), (from_second(b_norm), 0), (b_add, 4),
                                     (early(1, lambda: (c_norm_x(first), c_norm(first))), 4), (b_v, 2)])
            phase_end(dve, "dve", 2)

            c = Cm
            for i in range(2):
                dve.memset(c["v"][i][:, :, HD:32], 0.0).then_inc(s["c_zeros"], 1)
            dve.wait_ge(s["c_zeros"], 2)

            def c_q(u):
                after(dve, "c_q_made", u)
                after(dve, "c_scored", u, back=2)
                tt(c["qT"][u.slot][:, :, :], PS[:, 6, 0:3 * T].rearrange("p (g t) -> p g t", g=3),
                   cols[:, QB:QB + 3].rearrange("p (g one) -> p g one", one=1).to_broadcast([128, 3, T]), ALU.add)\
                    .then_inc(s["c_q"], 1)

            def c_pT2(u):
                after(dve, "c_p_turned", u, per=3)
                after(dve, "c_attended", u, back=1)
                dve.tensor_copy(c["PT"][:, 8:12, :], PS[:, 4, :].rearrange("p (h t) -> p h t", h=4))\
                    .then_inc(s["c_pT2"], 1)

            def c_k(u):
                after(dve, "c_k_made", u)
                after(dve, "c_scored", u, back=2)
                tt(c["kT"][u.slot][:, :, :], PS[:, 7, 0:3 * T].rearrange("p (g t) -> p g t", g=3),
                   cols[:, KB:KB + 3].rearrange("p (g one) -> p g one", one=1).to_broadcast([128, 3, T]), ALU.add)\
                    .then_inc(s["c_k"], 1)

            def c_v(u):
                after(dve, "c_v_made", u)
                after(dve, "c_attended", u, back=2)
                tt(c["v"][u.slot][:, :, 0:HD], PS[:, 5, 0:C].rearrange("p (h e) -> p h e", h=HEADS),
                   row("in_bv").rearrange("p (h e) -> p h e", h=HEADS), ALU.add).then_inc(s["c_v"], 1)

            def c_rowmax(u):
                after(dve, "c_scored", u)
                dve.tensor_reduce(c["mx"][u.slot][:, :].rearrange("p (j g) -> p j g", j=4),
                                  PS[:, 0:4, 0:3 * T].rearrange("p j (g t) -> p j g t", g=3), AX.X, ALU.max)\
                    .then_inc(s["c_rowmax"], 1)

            def c_max(u):
                after(dve, "c_rowmax", u)
                dve.tensor_scalar(c["nm"][u.slot][:, :], c["mx"][u.slot][:, :], -(HD ** -0.5), None, ALU.mult)\
                    .then_inc(s["c_max"], 1)

            def c_recip(u):
                after(dve, "c_exp", u)
                dve.reciprocal(c["rd"][u.slot][:, :], c["sum"][u.slot][:, :]).then_inc(s["c_recip"], 1)

            def c_scale(u):
                e = c["E"][u.slot][:, :, :]
                after(dve, "c_recip", u)
                tt(e, e, c["rd"][u.slot][:, :].rearrange("p (h one) -> p h one", one=1).to_broadcast([128, HEADS, T]),
                   ALU.mult).then_inc(s["c_scaled"], 1)

            def c_add(u):
                after(dve, "c_projected", u)
                after(dve, "c_xb", u)
                tt(X[:, u.v, :], PS[:, 6, 0:C], X[:, u.v, :], ALU.add).then_inc(s["c_added"], 1)

            pipelined(dve, B, 2, 3, [(from_second(c_norm_x), 1), (from_second(c_stats), 0), (from_second(c_norm), 1),
                                     (from_second(c_aggr), 0), (c_recip, 3), (c_scale, 3),
                                     (c_add, 5), (c_rowmax, 2), (c_max, 2), (c_q, 1), (c_pT2, 3), (c_k, 1), (c_v, 2)])
            phase_end(dve, "dve", 3)

            q = D

            def split_gelu(f):
                for m in range(HCH):
                    after(dve, "gelu", f, per=HCH, k=m + 1)
                    if m == 0:
                        after(dve, "down", f, back=1, per=GB)
                    dve.tensor_copy(q["Gh"][:, m, :], q["G"][m % 3][:, :]).then_inc(s["gelu_hi"], 1)
                    after(dve, "gelu_hi", f, per=HCH, k=m + 1)
                    tt(q["Gl"][:, m, :], q["G"][m % 3][:, :], q["Gh"][:, m, :].bitcast(F32), ALU.subtract)\
                        .then_inc(s["gelu_split"], 1)

            def low_parts(g, x0, x1, sem_hi, sem, u):
                after(dve, sem_hi, u, per=2, k=1)
                tt(q["XL"][:, g, :], x0, q["XH"][:, g, :].bitcast(F32), ALU.subtract).then_inc(s[sem + "_lo"], 1)
                after(dve, sem_hi, u, per=2, k=2)
                tt(q["XS"][64:128, g, :], x1[64:128, :], q["XS"][64:128, g, :].bitcast(F32), ALU.subtract)\
                    .then_inc(s[sem + "_split"], 1)

            def read_mlp(u):
                for part in range(2):
                    for t in range(GB):
                        x = X[:, u.v * GB + t, :]
                        if part == 0:
                            after(dve, "down", u, per=GB, k=t + 1)
                            after(dve, "xb_D", u, per=GB, k=t + 1)
                        else:
                            after(dve, "down_part", u, per=GB, k=t + 1)
                        tt(x, PS[:, 4 + t, part * C:(part + 1) * C], x, ALU.add)\
                            .then_inc(s["down_read" if part else "down_part"], 1)
                for t in range(GB):
                    after(dve, "down_read", u, per=GB, k=t + 1, nop=True)
                    dve.bn_stats(q["st"][:, t, :], X[:, u.v * GB + t, :]).then_inc(s["d_st"], 1)
                for t in range(GB):
                    after(dve, "d_st", u, per=GB, k=t + 1, nop=True)
                    dve.bn_aggr(q["mv"][:, t, :], q["st"][:, t, :]).then_inc(s["d_mv"], 1)

            def norm_xm(u):
                after(dve, "d_rstd", u)
                dve.wait_ge(s["x_turned"], min(u.v + 2, NG))
                for t in range(GB):
                    dve.tensor_scalar(q["xs"][t][:, 0:C], X[:, u.v * GB + t, :], q["mv"][:, t, 0:1],
                                      q["rs"][:, t, 1:2], ALU.subtract, ALU.mult).then_inc(s["xm"], 1)

            def read_logits(u):
                after(dve, "gated", u)
                tt(q["LG"][:, bass.ts(u.v, GB), :],
                   PS[:, 0, 0:GB * NEXP].rearrange("p (t e) -> p t e", t=GB),
                   row("gate_b").rearrange("p (one e) -> p one e", one=1).to_broadcast([128, GB, NEXP]), ALU.add)\
                    .then_inc(s["gate_read"], 1)

            low_parts(0, PS[:, 0, :], PS[:, 1, :], "x_hi", "x", Unit(0, 0, 0))
            for g in range(NG + 1):
                u, last = Unit(g, g, 0), Unit(g - 1, g - 1, 0)
                if g > 0:
                    norm_xm(last)
                split_gelu(u)
                if g > 0:
                    low_parts(g - 1, q["XM"][0][:, :], q["XM"][1][:, :], "xm_hi", "xm", last)
                if g > 0:
                    read_logits(last)
                if g + 1 < NG:
                    low_parts(g + 1, PS[:, 0, :], PS[:, 1, :], "x_hi", "x", Unit(g + 1, g + 1, 0))
                if g < NG:
                    read_mlp(u)

            n_link = [0]

            def link(ins):
                n_link[0] += 1
                ins.then_inc(s["gate_chain"], 1)
                dve.wait_ge(s["gate_chain"], n_link[0])

            LG, rank, cmp_, top, comb = q["LG"], q["rank"], q["cmp"], q["top"], q["comb"]
            dve.wait_ge(s["gate_read"], NG)
            for j in range(NEXP):
                lj = LG[:, :, j:j + 1].to_broadcast([128, B, NEXP])
                if j == 0:
                    link(tt(rank[:, :, :], lj, LG[:, :, :], ALU.is_gt))
                else:
                    link(tt(cmp_[:, :, :], lj, LG[:, :, :], ALU.is_gt))
                    link(tt(rank[:, :, :], rank[:, :, :], cmp_[:, :, :], ALU.add))
            for j in range(NEXP - 1):
                n = NEXP - 1 - j
                link(tt(cmp_[:, :, 0:n], LG[:, :, j:j + 1].to_broadcast([128, B, n]), LG[:, :, j + 1:NEXP], ALU.is_equal))
                link(tt(rank[:, :, j + 1:NEXP], rank[:, :, j + 1:NEXP], cmp_[:, :, 0:n], ALU.add))
            link(dve.tensor_reduce(top[:, :], LG[:, :, :], AX.X, ALU.max))
            tt(cmp_[:, :, :], LG[:, :, :], top[:, :].rearrange("p (b one) -> p b one", one=1).to_broadcast([128, B, NEXP]),
               ALU.subtract).then_inc(s["logit_sub"], 1)
            dve.wait_ge(s["gate_exp"], 1)
            link(stt(comb[:, :, :], rank[:, :, :], 2.0, comb[:, :, :], ALU.is_lt, ALU.mult))
            link(dve.tensor_reduce(top[:, :], comb[:, :, :], AX.X, ALU.add))
            link(dve.reciprocal(top[:, :], top[:, :]))
            tt(comb[:, :, :], comb[:, :, :], top[:, :].rearrange("p (b one) -> p b one", one=1).to_broadcast([128, B, NEXP]),
               ALU.mult).then_inc(s["comb"], 1)
            dve.wait_ge(s["comb"], 1)

            def read_expert(f, u, e):
                b2 = rows[:, ROW["exp_b2"][0] + e * C:ROW["exp_b2"][0] + (e + 1) * C]
                for part in range(3):
                    for t in range(GB):
                        g = u.v * GB + t
                        if part == 0:
                            if e == 0:
                                after(dve, "hx", u, per=GB, k=t + 1)
                            else:
                                after(dve, "down_read", f, back=1, per=GB, k=t + 1)
                            x, sem = b2, "h_bias"
                        elif part == 1:
                            after(dve, "down", f, per=GB, k=t + 1)
                            dve.wait_ge(s["h_bias"], f.v * GB + (t + 1 - NG * GB))
                            x, sem = PS[:, 4 + t, 0:C], "down_part"
                        else:
                            after(dve, "down_part", f, per=GB, k=t + 1)
                            x, sem = PS[:, 4 + t, C:2 * C], "down_read"
                        stt(H[:, g, :], x, comb[:, g, e:e + 1], H[:, g, :], ALU.mult, ALU.add).then_inc(s[sem], 1)

            read_expert(Unit(NG, NG, 0), Unit(0, 0, 0), 0)

            def d_experts(u, first):
                for e in range(first, NEXP):
                    f = Unit(u.v * NEXP + (NG + e), u.lo * NEXP + NG + e, 0)
                    split_gelu(f)
                    read_expert(f, u, e)

            e_ = Em

            def e_stats(u):
                if u.v == 0:
                    dve.wait_ge(s["down_read"], (NG + NEXP) * GB)
                for t in range(GB):
                    dve.bn_stats(e_["st"][:, t, :], H[:, u.v * GB + t, :]).then_inc(s["e_st"], 1)
                for t in range(GB):
                    after(dve, "e_st", u, per=GB, k=t + 1, nop=True)
                    dve.bn_aggr(e_["mv"][:, t, :], e_["st"][:, t, :]).then_inc(s["e_mv"], 1)

            def e_norm(u):
                after(dve, "e_rstd", u)
                if u.v == 0:
                    dve.wait_ge(s["xm_turned"], NG)
                after(dve, "e_turned", u, back=1)
                for t in range(GB):
                    dve.tensor_scalar(e_["zn"][t][:, 0:C], H[:, u.v * GB + t, :], e_["mv"][:, t, 0:1],
                                      e_["rs"][:, t, 1:2], ALU.subtract, ALU.mult).then_inc(s["e_zn"], 1)

            d_experts(Unit(0, 0, 0), 1)
            with dve.Fori(0, NG - 2) as i:
                d_experts(Unit(i + 1, 1, 0), 0)
            u = Unit(NG - 1, NG - 1, 0)
            for e in range(NEXP):
                f = Unit(u.v * NEXP + (NG + e), u.lo * NEXP + NG + e, 0)
                split_gelu(f)
                if e == 1:
                    e_stats(Unit(0, 0, 0))
                if e == 2:
                    e_norm(Unit(0, 0, 0))
                read_expert(f, u, e)
            phase_end(dve, "dve", 4)

            for n in "kvr":
                dve.tensor_scalar(e_["om"][n][:, :], cols[:, COL["mix_" + n]:COL["mix_" + n] + 2], -1.0, 1.0,
                                  ALU.mult, ALU.add).then_inc(s["e_consts"], 1)
            dve.memset(e_["zT"][:, :, 0:1], 0.0).then_inc(s["e_consts"], 1)
            for i in range(2):
                dve.memset(e_["K"][i][:, :, 0:1], FAR).then_inc(s["e_consts"], 1)
            for n in ("D1", "E2s", "EV"):
                dve.memset(e_[n][:, :, 0:1], 0.0).then_inc(s["e_consts"], 1)
            dve.wait_ge(s["e_consts"], 9)

            def e_mix(u):
                for j, n in enumerate("kvr"):
                    after(dve, "e_mt", u, per=3, k=j + 1)
                    after(dve, "e_projected", u, back=1, per=3, k=j + 1)
                    for k, bl in enumerate((slice(0, GB), slice(GB, NB6))):
                        last = stt(e_["mx"][n][:, bl, :], e_["zT"][:, bl, 0:T], e_["om"][n][:, k:k + 1],
                                   e_["mt"][n][:, bl, :], ALU.mult, ALU.add)
                    last.then_inc(s["e_mixed"], 1)

            def flat(t):
                return t[:, :, :].rearrange("p b t -> p (b t)")

            def e_wkv_args(u):
                i = u.slot
                K, ku, MX = e_["K"][i], e_["ku"][i], e_["MX"]
                prev, new = slice(0, T), slice(1, T + 1)
                after(dve, "e_read_k", u)
                after(dve, "e_arg_dd", u, back=1)
                dve.tensor_tensor_scan(flat(MX), flat(e_["WD"]), flat(K), FAR, ALU.add, ALU.max)\
                    .then_inc(s["e_mxscan"], 1)
                after(dve, "e_mxscan", u)
                after(dve, "e_arg_b", u, back=1)
                tt(e_["mo"][:, :, :], ku[:, :, :], MX[:, :, prev], ALU.max).then_inc(s["e_mo"], 1)
                for k, bl in enumerate((slice(0, GB), slice(GB, NB6))):
                    last = stt(e_["c"][:, bl, :], MX[:, bl, prev], e_["ndec"][:, k:k + 1], MX[:, bl, new],
                               ALU.add, ALU.subtract)
                last.then_inc(s["e_arg_c"], 1)
                after(dve, "e_mo", u)
                tt(e_["a"][:, :, :], MX[:, :, prev], e_["mo"][:, :, :], ALU.subtract).then_inc(s["e_arg_a"], 1)

            def e_wkv(u):
                i = u.slot
                v, er = e_["v"][i], e_["er"][i]
                D1, E2s, EV, NUM, DEN = (e_[n] for n in ("D1", "E2s", "EV", "NUM", "DEN"))
                prev, new = slice(0, T), slice(1, T + 1)
                after(dve, "e_exp_dd", u)
                after(dve, "e_read_v", u)
                tt(EV[:, :, new], E2s[:, :, new], v[:, :, :], ALU.mult).then_inc(s["e_ev"], 1)
                after(dve, "e_exp_c", u)
                dve.tensor_tensor_scan(flat(DEN), flat(D1), flat(E2s), 0.0, ALU.mult, ALU.add)\
                    .then_inc(s["e_den"], 1)
                after(dve, "e_ev", u)
                dve.tensor_tensor_scan(flat(NUM), flat(D1), flat(EV), 0.0, ALU.mult, ALU.add)\
                    .then_inc(s["e_num"], 1)
                after(dve, "e_exp_b", u)
                after(dve, "e_exp_a", u)
                after(dve, "e_den", u)
                tt(e_["t3"][:, :, :], e_["e1"][:, :, :], DEN[:, :, prev], ALU.mult).then_inc(s["e_t3"], 1)
                after(dve, "e_t3", u)
                tt(e_["t3"][:, :, :], e_["t3"][:, :, :], e_["e2"][:, :, :], ALU.add).then_inc(s["e_t3b"], 1)
                after(dve, "e_t3b", u)
                after(dve, "e_read_r", u)
                stt(e_["t3"][:, :, :], er[:, :, :], 1.0, e_["t3"][:, :, :], ALU.add, ALU.mult)\
                    .then_inc(s["e_t3c"], 1)
                after(dve, "e_t3c", u)
                dve.reciprocal(e_["t3"][:, :, :], e_["t3"][:, :, :]).then_inc(s["e_t3d"], 1)
                after(dve, "e_t3d", u)
                after(dve, "e_t1b", u)
                after(dve, "e_out", u, back=2)
                tt(e_["rw"][i][:, :, :], e_["t1"][:, :, :], e_["t3"][:, :, :], ALU.mult).then_inc(s["e_rw"], 1)

            def e_add(u):
                after(dve, "e_out", u)
                for t in range(GB):
                    h = H[:, u.v * GB + t, :]
                    tt(h, PS[:, 6 + t // 2, (t % 2) * C:(t % 2) * C + C], h, ALU.add).then_inc(s["e_added"], 1)

            def e_decays(u):
                if u.v != 0:
                    return
                dve.wait_ge(s["e_decay"], 1)
                dve.memset(e_["WD"][:, :, :], 0.0).then_inc(s["e_wd"], 1)
                dve.tensor_scalar(e_["ndec"][:, :], e_["ndec"][:, :], -1.0, None, ALU.mult).then_inc(s["e_wd"], 1)
                dve.wait_ge(s["e_wd"], 2)
                for k, bl in enumerate((slice(0, GB), slice(GB, NB6))):
                    dve.tensor_scalar(e_["WD"][:, bl, :], e_["WD"][:, bl, :], e_["ndec"][:, k:k + 1], None, ALU.add)\
                        .then_inc(s["e_wd"], 1)
                dve.wait_ge(s["e_wd"], 4)
                dve.memset(e_["WD"][:, :, 0:1], FAR).then_inc(s["e_wd"], 1)
                dve.wait_ge(s["e_wd"], 5)

            def w_sums(u):
                if u.v != 0:
                    return
                dve.wait_ge(s["in_F"], 32)
                dve.wait_ge(s["pool_ones"], 1)
                dve.tensor_reduce(qs[:, 2:4], rawI[:, :, :], AX.X, ALU.add, apply_absolute_value=True)\
                    .then_inc(s["f_prep"], 1)
                dve.tensor_reduce(qs[:, 1:2], rawO[:, :, :], AX.XY, ALU.add, apply_absolute_value=True)\
                    .then_inc(s["f_prep"], 1)
                dve.wait_ge(s["f_prep"], 2)
                stt(qs[:, 0:1], qs[:, 3:4], 0.5, qs[:, 2:3], ALU.mult, ALU.add).then_inc(s["f_wsum"], 1)

            def w_scales(u):
                if u.v != 0:
                    return
                dve.wait_ge(s["f_wmean"], 1)
                dve.tensor_scalar(qs[:, 4:5], PS[:, 7, 256:257], 1.0 / (2 * BH * C), EPS_Q, ALU.mult, ALU.max)\
                    .then_inc(s["f_prep"], 1)
                dve.tensor_scalar(qs[:, 5:6], PS[:, 7, 257:258], 1.0 / (BH * C), EPS_Q, ALU.mult, ALU.max)\
                    .then_inc(s["f_prep"], 1)
                dve.wait_ge(s["f_prep"], 4)
                dve.reciprocal(qs[:, 6:8], qs[:, 4:6]).then_inc(s["f_prep"], 1)
                dve.wait_ge(s["f_prep"], 5)

            def w_round(u):
                if u.v != 0:
                    return
                for j, raw in enumerate((rawI, rawO)):
                    dve.tensor_scalar(raw[:, :, :], raw[:, :, :], qs[:, 6 + j:7 + j], MAGIC, ALU.mult, ALU.add)\
                        .then_inc(s["f_prep"], 1)

            def w_clip(u):
                if u.v != 0:
                    return
                for j, raw in enumerate((rawI, rawO)):
                    dve.wait_ge(s["f_prep"], 6 + j)
                    dve.tensor_scalar(raw[:, :, :], raw[:, :, :], MAGIC, 1.0, ALU.subtract, ALU.min)\
                        .then_inc(s["f_prep2"], 1)
                for j, (raw, w) in enumerate(((rawI, wI), (rawO, wO))):
                    dve.wait_ge(s["f_prep2"], 1 + j)
                    dve.tensor_scalar(w[:, :, :], raw[:, :, :], -1.0, None, ALU.max).then_inc(s["f_weights"], 1)

            pipelined(dve, NG, 2, 2, [(lambda u: u.v and e_stats(u), 0), (e_wkv_args, 2), (lambda u: u.v < NG - 1 and e_add(u), 3), (e_mix, 1), (e_decays, 1),
                                      (w_scales, 2), (e_wkv, 2), (lambda u: u.v and e_norm(u), 0), (w_sums, 1), (w_round, 2),
                                      (w_clip, 2)])

            f_ = Fm

            def f_stats(u):
                i = u.slot
                after(dve, "e_added", u, nop=True)
                dve.bn_stats(f_["st"][i][:, :], H[:, u.v, :]).then_inc(s["f_st"], 1)

            def f_aggr(u):
                i = u.slot
                after(dve, "f_st", u)
                after(dve, "f_c", u, back=2, nop=True)
                dve.bn_aggr(f_["mv"][i][:, :], f_["st"][i][:, :]).then_inc(s["f_mv"], 1)

            def f_norm(u):
                i = u.slot
                after(dve, "f_rstd", u)
                dve.tensor_scalar(f_["xn"][i][:, :], H[:, u.v, :], f_["mv"][i][:, 0:1], f_["rs"][i][:, 2:3],
                                  ALU.subtract, ALU.mult).then_inc(s["f_xn"], 1)

            def f_gain(u):
                i = u.slot
                after(dve, "f_xn", u)
                after(dve, "f_q", u, back=2)
                tt(f_["xg"][i][:, :], f_["xn"][i][:, :], row("g_in"), ALU.mult).then_inc(s["f_xg"], 1)

            def f_amax(u):
                i = u.slot
                after(dve, "f_xg", u)
                dve.tensor_reduce(f_["rs"][i][:, 3:4], f_["xg"][i][:, :], AX.X, ALU.max, apply_absolute_value=True)\
                    .then_inc(s["f_amax"], 1)

            def f_step(u):
                rs = f_["rs"][u.slot]
                after(dve, "f_amax", u)
                dve.tensor_scalar(rs[:, 4:5], rs[:, 3:4], EPS_Q, 1.0 / 127.0, ALU.max, ALU.mult)\
                    .then_inc(s["f_step"], 1)

            def f_scale(u):
                rs = f_["rs"][u.slot]
                after(dve, "f_step", u)
                dve.reciprocal(rs[:, 5:6], rs[:, 4:5]).then_inc(s["f_scale"], 1)
                dve.tensor_scalar(rs[:, 6:7], rs[:, 4:5], qs[:, 4:5], None, ALU.mult).then_inc(s["f_c"], 1)

            def f_round(u):
                i = u.slot
                after(dve, "f_scale", u)
                dve.tensor_scalar(f_["xn"][i][:, :], f_["xg"][i][:, :], f_["rs"][i][:, 5:6], MAGIC,
                                  ALU.mult, ALU.add).then_inc(s["f_round"], 1)

            def f_clip(u):
                i = u.slot
                after(dve, "f_round", u)
                dve.tensor_scalar(f_["xg"][i][:, :], f_["xn"][i][:, :], MAGIC + 127.0, MAGIC - 128.0,
                                  ALU.min, ALU.max).then_inc(s["f_clip"], 1)

            def f_gate(u):
                i = u.slot
                rs = f_["rs"][i]
                after(dve, "f_silu", u)
                stt(f_["y"][i][:, :], PS[:, 1 + 2 * i, :], rs[:, 6:7], f_["sg"][i][:, :], ALU.mult, ALU.mult)\
                    .then_inc(s["f_y"], 1)

            def f_amax2(u):
                i = u.slot
                after(dve, "f_yg", u)
                dve.tensor_reduce(f_["rs"][i][:, 8:9], f_["yg"][i][:, :], AX.X, ALU.max, apply_absolute_value=True)\
                    .then_inc(s["f_amax2"], 1)

            def f_norm_max(u):
                rs = f_["rs"][u.slot]
                after(dve, "f_rms", u)
                after(dve, "f_amax2", u)
                dve.tensor_scalar(rs[:, 9:10], rs[:, 8:9], rs[:, 7:8], EPS_Q, ALU.mult, ALU.max)\
                    .then_inc(s["f_amax3"], 1)

            def f_inv(u):
                rs = f_["rs"][u.slot]
                after(dve, "f_amax3", u)
                dve.reciprocal(rs[:, 10:11], rs[:, 9:10]).then_inc(s["f_inv"], 1)
                dve.tensor_scalar(rs[:, 11:12], rs[:, 9:10], qs[:, 5:6], 1.0 / 127.0, ALU.mult, ALU.mult)\
                    .then_inc(s["f_c2"], 1)

            def f_scale2(u):
                rs = f_["rs"][u.slot]
                after(dve, "f_inv", u)
                dve.tensor_scalar(rs[:, 10:11], rs[:, 10:11], rs[:, 7:8], 127.0, ALU.mult, ALU.mult)\
                    .then_inc(s["f_scale2"], 1)

            def f_round2(u):
                i = u.slot
                after(dve, "f_scale2", u)
                dve.tensor_scalar(f_["yg"][i][:, :], f_["yg"][i][:, :], f_["rs"][i][:, 10:11], MAGIC,
                                  ALU.mult, ALU.add).then_inc(s["f_round2"], 1)

            def f_clip2(u):
                i = u.slot
                after(dve, "f_round2", u)
                dve.tensor_scalar(f_["yg"][i][:, :], f_["yg"][i][:, :], MAGIC + 127.0, MAGIC - 128.0,
                                  ALU.min, ALU.max).then_inc(s["f_clip2"], 1)

            def f_add(u):
                i = u.slot
                after(dve, "f_down", u)
                after(dve, "f_c2", u)
                stt(f_["o"][:, u.v, :], PS[:, 6, 0:C], f_["rs"][i][:, 11:12], H[:, u.v, :], ALU.mult, ALU.add)\
                    .then_inc(s["o_ready"], 1)

            pipelined(dve, B, 2, 2, [(f_norm, 1), (f_stats, 0), (f_gain, 1), (f_aggr, 0), (f_amax, 1), (f_step, 1),
                                     (f_amax2, 3), (f_scale, 1), (f_round, 1), (f_norm_max, 3),
                                     (lambda u: u.lo == 0 and e_add(Unit(NG - 1, NG - 1, 0)), 1),
                                     (f_clip, 1), (f_inv, 3), (f_add, 4), (f_scale2, 3), (f_round2, 3), (f_clip2, 3),
                                     (f_gate, 2)])

        @block.gpsimd
        def _(pool):
            def rsqrt(dst, tmp, src, eps, sem, u, per=1, k=None):
                pool.tensor_scalar(tmp, src, eps, None, ALU.add).then_inc(s[sem + "_a"], 1)
                after(pool, sem + "_a", u, per=per, k=k)
                exp = expo[:, 0:1] if len(dst.shape) == 2 else \
                    expo[:, 0:1].rearrange("p (a b) -> p a b", b=1).to_broadcast([128, dst.shape[1], 1])
                return pool.tensor_tensor(dst, tmp, exp, ALU.pow)

            pool.memset(expo[:, :], -0.5).then_inc(s["expo"], 1)
            pool.memset(magic[:, :], -MAGIC).then_inc(s["expo"], 1)
            pool.wait_ge(s["expo"], 2)
            pool.wait_ge(s["in_A"], 16 * 5)
            pool.tensor_copy(identb[:, :], ident[:, :])

            def w_low(u):
                after(pool, "w_hi", u)
                pool.tensor_tensor(WW[:, 1, bass.ts(u.v, PIECE)], raw[u.slot][:, :],
                                   WW[:, 0, bass.ts(u.v, PIECE)].bitcast(F32), ALU.subtract).then_inc(s["w_lo"], 1)

            a = A

            def a_rstd(u):
                for p in range(2):
                    i = 2 * u.slot + p
                    after(pool, "a_mv", u, per=2, k=p + 1, nop=True)
                    rsqrt(a["rs"][i][:, 1:2], a["rs"][i][:, 0:1], a["mv"][i][:, 1:2], EPS, "a_rs", u, 2, p + 1)\
                        .then_inc(s["a_rstd"], 1)

            def a_affine(u):
                for p in range(2):
                    i = 2 * u.slot + p
                    h = H[:, u.v + p * (B // 2), :]
                    after(pool, "y_normed", u, per=2, k=p + 1)
                    pool.tensor_tensor(a["yn"][i][:, :], a["yn"][i][:, :], row("gamma"), ALU.mult)\
                        .then_inc(s["a_gamma"], 1)
                    after(pool, "a_gamma", u, per=2, k=p + 1)
                    pool.tensor_tensor(h, a["yn"][i][:, :], row("beta"), ALU.add).then_inc(s["h_A"], 1)

            m_ = Bm

            def b_rstd(u):
                i = u.slot
                after(pool, "b_mv", u, nop=True)
                rsqrt(m_["rs"][i][:, 1:2], m_["rs"][i][:, 0:1], m_["mv"][i][:, 1:2], EPS, "b_rs", u)\
                    .then_inc(s["b_rstd"], 1)

            def a_last_tap(u):
                cv0, cv1 = a["cv0"][u.slot][:, :, :], a["cv1"][u.slot][:, :]
                after(pool, "last_product", u)
                after(pool, "tap_a", u, per=TAPS - 2)
                pool.tensor_tensor(cv0, cv0, a["lt0"][:, :, :], ALU.add).then_inc(s["last_tap"], 1)
                after(pool, "tap_b", u, per=TAPS - 2)
                pool.tensor_tensor(cv1, cv1, a["lt1"][:, :], ALU.add).then_inc(s["last_tap"], 1)

            def b_first(u):
                if u.v == B // 2 - 2:
                    b_rstd(Unit(0, 0, 0))

            pipelined(pool, B // 2, 2, 2, [(a_rstd, 4), (a_last_tap, 1), (a_affine, 4), (b_first, 4)])
            phase_end(pool, "pool", 1)
            m_ = Bm

            pipelined(pool, B, 2, 2, [(from_second(b_rstd), 0), (w_low, 1)])
            c = Cm

            def c_rstd(u):
                i = u.slot
                rs, var = c["rs"][i], c["mv"][i][:, 1:2]
                after(pool, "c_mv", u)
                after(pool, "c_normed", u, back=2, nop=True)
                rsqrt(rs[:, 1:2], rs[:, 0:1], var, EPS, "c_rs", u).then_inc(s["c_rstd1"], 1)
                after(pool, "c_rstd1", u)
                pool.nop(nofuse=True)
                pool.tensor_scalar(rs[:, 3:4], rs[:, 1:2], rs[:, 1:2], var, ALU.mult, ALU.mult)\
                    .then_inc(s["c_var2"], 1)
                after(pool, "c_var2", u, nop=True)
                rsqrt(rs[:, 5:6], rs[:, 4:5], rs[:, 3:4], EPS, "c_rs2", u).then_inc(s["c_rstd"], 1)

            c_rstd(Unit(0, 0, 0))
            phase_end(pool, "pool", 2)
            c = Cm

            def c_xb(u):
                after(pool, "c_normed", u)
                pool.tensor_tensor(X[:, u.v, :], X[:, u.v, :], row("out_b"), ALU.add).then_inc(s["c_xb"], 1)

            pipelined(pool, B, 2, 3, [(from_second(c_rstd), 0), (c_xb, 1), (lambda u: w_low(shifted(u)), 1)])
            def copy_x(g):
                if g == 0:
                    pool.wait_ge(s["c_added"], GB)
                    pool.nop(nofuse=True)
                if g > 0:
                    pool.wait_ge(s["x_turned"], g)
                if g > 1:
                    pool.wait_ge(s["xm_turned"], g - 1)
                    pool.nop(nofuse=True)
                for t in range(GB):
                    pool.tensor_copy(turning["xs"][t][:, 128:256].rearrange("p (two c) -> p two c", two=2),
                                     X[:, g * GB + t, 128:C].rearrange("p (one c) -> p one c", one=1)
                                     .to_broadcast([128, 2, C1])).then_inc(s["x_copied"], 1)

            def add_bias(g):
                for t in range(GB):
                    x = X[:, g * GB + t, :]
                    if t == 0:
                        pool.wait_ge(s["x_turned"], g + 1)
                    pool.tensor_tensor(x, x, row("mlp_b2"), ALU.add).then_inc(s["xb_D"], 1)

            copy_x(0)
            phase_end(pool, "pool", 3)
            q = D

            add_bias(0)
            copy_x(1)
            for g in range(NG):
                u = Unit(g, g, 0)
                after(pool, "d_mv", u, per=GB, nop=True)
                rsqrt(q["rs"][:, :, 1:2], q["rs"][:, :, 0:1], q["mv"][:, :, 1:2], EPS, "d_rs", u)\
                    .then_inc(s["d_rstd"], 1)
                for t in range(GB):
                    after(pool, "xm", u, per=GB, k=t + 1, nop=True)
                    pool.tensor_copy(q["xs"][t][:, C:256], q["xs"][t][:, 128:C]).then_inc(s["xm_copied"], 1)
                if g + 2 < NG:
                    copy_x(g + 2)
                if g + 1 < NG:
                    add_bias(g + 1)
                for t in range(GB):
                    n = g * GB + t
                    pool.tensor_tensor(H[:, n, :], H[:, n, :], X[:, n, :], ALU.add).then_inc(s["hx"], 1)
            e_ = Em

            def e_rstd(u):
                after(pool, "e_mv", u, per=GB, nop=True)
                rsqrt(e_["rs"][:, :, 1:2], e_["rs"][:, :, 0:1], e_["mv"][:, :, 1:2], EPS, "e_rs", u)\
                    .then_inc(s["e_rstd"], 1)
                for t in range(GB):
                    after(pool, "e_zn", u, per=GB, k=t + 1, nop=True)
                    pool.tensor_copy(e_["zn"][t][:, C:256], e_["zn"][t][:, 128:C]).then_inc(s["e_normed"], 1)

            e_rstd(Unit(0, 0, 0))
            phase_end(pool, "pool", 4)
            pool.memset(ones[:, :], 1.0).then_inc(s["pool_ones"], 1)

            def e_numerator(u):
                i = u.slot
                after(pool, "e_mxscan", u)
                after(pool, "e_exp_dd", u, back=1)
                pool.tensor_tensor(e_["dd"][:, :, :], e_["K"][i][:, :, 1:T + 1], e_["MX"][:, :, 1:T + 1],
                                   ALU.subtract).then_inc(s["e_arg_dd"], 1)
                after(pool, "e_mo", u)
                after(pool, "e_exp_b", u, back=1)
                pool.tensor_tensor(e_["b"][:, :, :], e_["ku"][i][:, :, :], e_["mo"][:, :, :],
                                   ALU.subtract).then_inc(s["e_arg_b"], 1)
                after(pool, "e_exp_b", u)
                pool.tensor_tensor(e_["t2"][:, :, :], e_["e2"][:, :, :], e_["v"][i][:, :, :], ALU.mult)\
                    .then_inc(s["e_t2"], 1)
                after(pool, "e_num", u)
                after(pool, "e_exp_a", u)
                after(pool, "e_rw", u, back=1)
                pool.tensor_tensor(e_["t1"][:, :, :], e_["e1"][:, :, :], e_["NUM"][:, :, 0:T], ALU.mult)\
                    .then_inc(s["e_t1"], 1)
                after(pool, "e_t1", u)
                after(pool, "e_t2", u)
                pool.tensor_tensor(e_["t1"][:, :, :], e_["t1"][:, :, :], e_["t2"][:, :, :], ALU.add)\
                    .then_inc(s["e_t1b"], 1)

            pipelined(pool, NG, 2, 2, [(e_numerator, 2), (lambda u: u.v and e_rstd(u), 0)])
            f_ = Fm

            def f_rstd(u):
                i = u.slot
                rs, var = f_["rs"][i], f_["mv"][i][:, 1:2]
                after(pool, "f_mv", u)
                after(pool, "f_round", u, back=2, nop=True)
                rsqrt(rs[:, 1:2], rs[:, 0:1], var, EPS, "f_rs", u).then_inc(s["f_rstd1"], 1)
                after(pool, "f_rstd1", u)
                pool.nop(nofuse=True)
                pool.tensor_scalar(rs[:, 3:4], rs[:, 1:2], rs[:, 1:2], var, ALU.mult, ALU.mult).then_inc(s["f_ms"], 1)
                after(pool, "f_ms", u, nop=True)
                rsqrt(rs[:, 5:6], rs[:, 4:5], rs[:, 3:4], EPS_RMS, "f_rs2", u).then_inc(s["f_rstd2"], 1)
                after(pool, "f_rstd2", u)
                pool.tensor_tensor(rs[:, 2:3], rs[:, 5:6], rs[:, 1:2], ALU.mult).then_inc(s["f_rstd"], 1)

            def f_rms(u):
                i = u.slot
                rs = f_["rs"][i]
                after(pool, "f_y", u)
                after(pool, "f_q2", u, back=2)
                pool.tensor_tensor(f_["yg"][i][:, :], f_["y"][i][:, :], row("g_out"), ALU.mult)\
                    .then_inc(s["f_yg"], 1)
                after(pool, "f_sq", u, nop=True)
                pool.tensor_scalar(rs[:, 7:8], rs[:, 7:8], 1.0 / BH, EPS_RMS, ALU.mult, ALU.add)\
                    .then_inc(s["f_ms2"], 1)
                after(pool, "f_ms2", u)
                pool.tensor_tensor(rs[:, 7:8], rs[:, 7:8], expo[:, 0:1], ALU.pow).then_inc(s["f_rms"], 1)

            pipelined(pool, B, 2, 2, [(f_rms, 3), (f_rstd, 0)])


def _chunk(wT):
    return np.ascontiguousarray(np.stack([wT[:128], np.concatenate([wT[128:], wT[128:]])], axis=1))


def _vec(v):
    return np.stack([v[:128], np.concatenate([v[128:], v[128:]])], axis=1)


def _headpad(w):
    out = np.zeros((3, 4, 32) + w.shape[1:], w.dtype)
    out[:, :, :HD] = w.reshape(3, 4, HD, *w.shape[1:])
    return out.reshape(384, *w.shape[1:])


def kernel(**inputs):
    import concourse.bacc as _bacc
    from concourse import mybir as _mybir
    from concourse.bass_utils import run_bass_kernel_spmd as _run

    i = {k: np.asarray(v) for k, v in inputs.items()}
    a = {}
    xT = np.pad(i["x"].transpose(2, 0, 1), ((0, 0), (0, 0), (TAPS // 2, TAPS // 2)))
    pair = xT.reshape(C, 2, B // 2, S + TAPS - 1).transpose(0, 2, 1, 3)
    x0 = pair[:128]
    x1 = pair[128:].transpose(2, 0, 1, 3).reshape(128, B // 2, S + TAPS - 1)
    a["x0a"], a["x0b"], a["x1a"], a["x1b"] = x0[:, :2], x0[:, 2:], x1[:, :2], x1[:, 2:]
    a["wpw"] = _chunk(i["L0_tok_w_pw"][:, :, 0].T)
    f32 = np.float32
    ang_c = 2 * np.pi * (np.outer(np.arange(C), np.arange(C)) % C) / C
    ang_t = 2 * np.pi * (np.outer(np.arange(T), np.arange(T)) % T) / T
    a["fd"] = _chunk(np.concatenate([np.cos(ang_c), -np.sin(ang_c)], axis=1).astype(f32))
    a["fs"] = np.stack([np.cos(ang_t), np.sin(ang_t)], axis=1).astype(f32)
    a["ident"] = np.eye(128, dtype=f32)
    a["wq"], a["wk"], a["wv"] = (_chunk(i[f"L0_attn_W{n}"].T) for n in "qkv")
    inw, inb = i["L0_ffn_in_w"], i["L0_ffn_in_b"]
    a["wqC"], a["wkC"] = _chunk(_headpad(inw[:C]).T), _chunk(_headpad(inw[C:2 * C]).T)
    a["wvC"] = _chunk(inw[2 * C:].T)
    a["woC"] = _headpad(i["L0_ffn_out_w"].T).reshape(3, 128, C).transpose(1, 0, 2)
    ups = [i["L0_ffn_mlp_w1"]] + list(i["L0_ffn_exp_w1"])
    dns = [i["L0_ffn_mlp_w2"]] + list(i["L0_ffn_exp_w2"])
    a["w_ffn"] = np.concatenate([p for f in range(NEXP + 1) for p in (
        _chunk(ups[f]).reshape(128, -1), dns[f].reshape(HCH, 128, C).transpose(1, 0, 2).reshape(128, -1))], axis=1)
    a["wg"] = _chunk(i["L0_ffn_gate_w"].T)
    for n in "kvro":
        a[f"w{n}E"] = _chunk(i[f"L1_attn_W{n}"].T)
    a["w_in"] = _chunk(i["L1_ffn_w_in"].T)
    a["w_out"] = i["L1_ffn_w_out"].T.reshape(BH // 128, 128, C).transpose(1, 0, 2)
    vec = {"b_dw": "L0_tok_b_dw", "b_pw": "L0_tok_b_pw", "bq": "L0_attn_bq", "bk": "L0_attn_bk",
           "ln1_g": "L0_ffn_ln1_g", "ln1_b": "L0_ffn_ln1_b", "ln2_g": "L0_ffn_ln2_g", "ln2_b": "L0_ffn_ln2_b",
           "decay": "L1_attn_time_decay", "first": "L1_attn_time_first", "mix_k": "L1_attn_mix_k",
           "mix_v": "L1_attn_mix_v", "mix_r": "L1_attn_mix_r"}
    parts = [_vec(i[vec[n]]) for n in COLS]
    parts += [_headpad(inb[:C]).reshape(3, 128).T, _headpad(inb[C:2 * C]).reshape(3, 128).T]
    taps = _chunk(i["L0_tok_w_dw"][:, 0, :])
    parts += [taps[:, 0], taps[:, 1]]
    parts += [i["L0_ffn_mlp_b1"].reshape(HCH, 128).T] + [b.reshape(HCH, 128).T for b in i["L0_ffn_exp_b1"]]
    a["cols"] = np.concatenate(parts, axis=1)
    assert a["cols"].shape == (128, NCOL)
    rowv = {"gamma": i["L0_tok_gamma"], "beta": i["L0_tok_beta"], "bv": i["L0_attn_bv"], "in_bv": inb[2 * C:],
            "out_b": i["L0_ffn_out_b"], "mlp_b2": i["L0_ffn_mlp_b2"], "exp_b2": i["L0_ffn_exp_b2"].reshape(-1),
            "g_in": i["L1_ffn_g_in"], "gate_b": i["L0_ffn_gate_b"], "g_out": i["L1_ffn_g_out"]}
    a["rows"] = np.broadcast_to(np.concatenate([rowv[n] for n, _ in ROWS]), (128, NROW))

    nc = _bacc.Bacc("TRN2", target_bir_lowering=False, num_devices=1)
    arrays, aps = {}, {}
    for name, v in a.items():
        v = np.ascontiguousarray(v)
        arrays["in_" + name] = v
        aps[name] = nc.dram_tensor("in_" + name, v.shape, _mybir.dt.from_np(v.dtype), kind="ExternalInput").ap()
    o = nc.dram_tensor("out_0", (B, T, C), _mybir.dt.float32, kind="ExternalOutput").ap()
    audio_tower(nc, aps, o)
    r = _run(nc, [arrays], core_ids=[0])
    return r.results[0]["out_0"]
```
